# Optimizing a Trainium2 kernel written in Bass

```python
import numpy as np
import jax
import jax.numpy as jnp

def _softmax(x, axis=-1):
    return jax.nn.softmax(x, axis=axis)

def _gelu(x):
    return jax.nn.gelu(x, approximate=True)

def _silu(x):
    return jax.nn.silu(x)

def _sigmoid(x):
    return jax.nn.sigmoid(x)

def _layernorm(x, axis=-1, eps=1e-05):
    m = jnp.mean(x, axis=axis, keepdims=True)
    v = jnp.var(x, axis=axis, keepdims=True)
    return (x - m) / jnp.sqrt(v + eps)

def _scatter_add(tgt, idx, src, axis=0):
    return tgt.at[idx].add(src)

def _segment_sum(src, seg, n):
    return jax.ops.segment_sum(src, seg, n)
kernel_name = 'mk_gnn_resnorm_d4_gnn_r64_15e35f'

def setup_inputs(seed: int=0):
    np.random.seed(seed)
    _w = jnp.asarray

    def _rec_inputs():
        import jax
        import jax.numpy as jnp
        _gk = jax.random.key(seed)
        x = -0.0003713 + 1 * jax.random.normal(jax.random.fold_in(_gk, 1), (100000, 128), jnp.float32)
        src = jax.random.randint(jax.random.fold_in(_gk, 2), (25000,), 0, 100000, jnp.int32)
        dst = jax.random.randint(jax.random.fold_in(_gk, 3), (25000,), 0, 100000, jnp.int32)
        _o = jnp.argsort(dst, stable=True)
        src = src[_o]
        dst = dst[_o]
        edge_weight = jax.random.uniform(jax.random.fold_in(_gk, 14), (25000,), jnp.float32, 0.0, 1)
        return (x, src, dst, edge_weight)
    x, src, dst, edge_weight = _rec_inputs()

    def _L0_gnn_setup():
        import jax, jax.numpy as jnp
        import numpy as np
        N_NODES = 100000
        N_EDGES = 9375
        DIM = 128
        key = jax.random.key(seed)
        ks = jax.random.split(key, 7)
        scale = 1.0 / np.sqrt(DIM)
        h = jax.random.normal(ks[0], (N_NODES, DIM), dtype=jnp.float32)
        edges = jax.random.randint(ks[1], (2, N_EDGES), 0, N_NODES, dtype=jnp.int32)
        Wq = jax.random.normal(ks[2], (DIM, DIM), dtype=jnp.float32) * scale
        Wk = jax.random.normal(ks[3], (DIM, DIM), dtype=jnp.float32) * scale
        Wv = jax.random.normal(ks[4], (DIM, DIM), dtype=jnp.float32) * scale
        Wp = jax.random.normal(ks[5], (DIM, DIM), dtype=jnp.float32) * scale
        bp = jnp.zeros((DIM,), dtype=jnp.float32)
        return {'h': h, 'edges': edges, 'Wq': Wq, 'Wk': Wk, 'Wv': Wv, 'Wp': Wp, 'bp': bp}
    _L0_gnn_all = _L0_gnn_setup()
    _L0_gnn_in = {k: v for k, v in _L0_gnn_all.items() if k in ('Wq', 'Wk', 'Wv', 'Wp', 'bp')}
    del _L0_gnn_all

    def _L1_gnn_setup():
        import jax, jax.numpy as jnp
        import numpy as np
        N, E, D = (100000, 500000, 128)
        key = jax.random.key(seed)
        ks = jax.random.split(key, 8)
        s = 1.0 / np.sqrt(D)
        return {'node_feat': jax.random.normal(ks[0], (N, D), dtype=jnp.float32), 'edge_index': jax.random.randint(ks[1], (2, E), 0, N, dtype=jnp.int64), 'W_edge': jax.random.normal(ks[2], (2 * D, D), dtype=jnp.float32) * s, 'b_edge': jnp.zeros((D,), dtype=jnp.float32), 'W1': jax.random.normal(ks[3], (D, D), dtype=jnp.float32) * s, 'b1': jnp.zeros((D,), dtype=jnp.float32), 'W2': jax.random.normal(ks[4], (D, D), dtype=jnp.float32) * s, 'b2': jnp.zeros((D,), dtype=jnp.float32), 'eps': jnp.zeros((1,), dtype=jnp.float32)}
    _L1_gnn_all = _L1_gnn_setup()
    _L1_gnn_in = {k: v for k, v in _L1_gnn_all.items() if k in ('W_edge', 'b_edge', 'W1', 'b1', 'W2', 'b2', 'eps')}
    del _L1_gnn_all

    def _L2_gnn_setup():
        import jax, jax.numpy as jnp
        import numpy as np
        N_NODES = 50000
        N_EDGES = 25000
        D = 128

        def _degree_norm(idx, n_nodes, dtype):
            deg = jax.ops.segment_sum(jnp.ones((idx.shape[0],), dtype=dtype), idx, num_segments=n_nodes)
            return jax.lax.rsqrt(jnp.maximum(deg, 1.0))

        def _graph_conv(h, e_weight, src, dst, W, b, out_norm, in_norm):
            feat_src = h * out_norm[:, None]
            msg = feat_src[src] * e_weight[:, None]
            agg = jax.ops.segment_sum(msg, dst, num_segments=h.shape[0])
            agg = agg * in_norm[:, None]
            return jax.nn.relu(agg @ W + b)
        key = jax.random.key(seed)
        ks = jax.random.split(key, 6)
        x = jax.random.normal(ks[0], (N_NODES, D), dtype=jnp.float32)
        e_weight = jax.random.uniform(ks[1], (N_EDGES,), dtype=jnp.float32)
        src = jax.random.randint(ks[2], (N_EDGES,), 0, N_NODES)
        dst = jax.random.randint(ks[3], (N_EDGES,), 0, N_NODES)
        scale = 1.0 / np.sqrt(D)
        W1 = jax.random.normal(ks[4], (D, D), dtype=jnp.float32) * scale
        W2 = jax.random.normal(ks[5], (D, D), dtype=jnp.float32) * scale
        b1 = jnp.zeros((D,), dtype=jnp.float32)
        b2 = jnp.zeros((D,), dtype=jnp.float32)
        return {'x': x, 'e_weight': e_weight, 'src': src, 'dst': dst, 'W1': W1, 'b1': b1, 'W2': W2, 'b2': b2}
    _L2_gnn_all = _L2_gnn_setup()
    _L2_gnn_in = {k: v for k, v in _L2_gnn_all.items() if k in ('W1', 'b1', 'W2', 'b2')}
    del _L2_gnn_all

    def _L3_gnn_setup():
        import jax, jax.numpy as jnp
        import numpy as np
        N_NODES = 100000
        N_EDGES = 25000
        D_IN = 128
        UNITS = 16
        HEADS = 8
        key = jax.random.key(seed)
        k1, k2, k3, k4, k5 = jax.random.split(key, 5)
        x = jax.random.normal(k1, (N_NODES, D_IN), dtype=jnp.float32)
        edges = jax.random.randint(k2, (N_EDGES, 2), 0, N_NODES, dtype=jnp.int64)
        kernel = jax.random.normal(k3, (D_IN, UNITS * HEADS), dtype=jnp.float32) * (2.0 / (D_IN + UNITS * HEADS)) ** 0.5
        ka1 = jax.random.normal(k4, (1, HEADS, UNITS), dtype=jnp.float32) * 0.1
        ka2 = jax.random.normal(k5, (1, HEADS, UNITS), dtype=jnp.float32) * 0.1
        bias = jnp.zeros((UNITS * HEADS,), dtype=jnp.float32)
        return {'x': x, 'edges': edges, 'kernel': kernel, 'ka1': ka1, 'ka2': ka2, 'bias': bias}
    _L3_gnn_all = _L3_gnn_setup()
    _L3_gnn_in = {k: v for k, v in _L3_gnn_all.items() if k in ('kernel', 'ka1', 'ka2', 'bias')}
    del _L3_gnn_all
    return {'x': x, 'src': src, 'dst': dst, 'edge_weight': edge_weight, 'L0_gnn_Wq': _L0_gnn_in['Wq'], 'L0_gnn_Wk': _L0_gnn_in['Wk'], 'L0_gnn_Wv': _L0_gnn_in['Wv'], 'L0_gnn_Wp': _L0_gnn_in['Wp'], 'L0_gnn_bp': _L0_gnn_in['bp'], 'L1_gnn_W_edge': _L1_gnn_in['W_edge'], 'L1_gnn_b_edge': _L1_gnn_in['b_edge'], 'L1_gnn_W1': _L1_gnn_in['W1'], 'L1_gnn_b1': _L1_gnn_in['b1'], 'L1_gnn_W2': _L1_gnn_in['W2'], 'L1_gnn_b2': _L1_gnn_in['b2'], 'L1_gnn_eps': _L1_gnn_in['eps'], 'L2_gnn_W1': _L2_gnn_in['W1'], 'L2_gnn_b1': _L2_gnn_in['b1'], 'L2_gnn_W2': _L2_gnn_in['W2'], 'L2_gnn_b2': _L2_gnn_in['b2'], 'L3_gnn_kernel': _L3_gnn_in['kernel'], 'L3_gnn_ka1': _L3_gnn_in['ka1'], 'L3_gnn_ka2': _L3_gnn_in['ka2'], 'L3_gnn_bias': _L3_gnn_in['bias']}

def reference(x, src, dst, edge_weight, L0_gnn_Wq, L0_gnn_Wk, L0_gnn_Wv, L0_gnn_Wp, L0_gnn_bp, L1_gnn_W_edge, L1_gnn_b_edge, L1_gnn_W1, L1_gnn_b1, L1_gnn_W2, L1_gnn_b2, L1_gnn_eps, L2_gnn_W1, L2_gnn_b1, L2_gnn_W2, L2_gnn_b2, L3_gnn_kernel, L3_gnn_ka1, L3_gnn_ka2, L3_gnn_bias):
    import jax
    import jax.numpy as jnp

    def _L0_gnn_ref(h, edges, Wq, Wk, Wv, Wp, bp):
        import jax, jax.numpy as jnp
        import numpy as np
        N_NODES = 100000
        N_EDGES = 9375
        DIM = 128
        src, dst = (edges[0], edges[1])
        N, d = h.shape
        q = h @ Wq.T
        k = h @ Wk.T
        v = h @ Wv.T
        scores = jnp.sum(q[dst] * k[src], axis=1) / jnp.sqrt(jnp.asarray(d, h.dtype))
        max_per_dst = jax.ops.segment_max(scores, dst, num_segments=N)
        exp = jnp.exp(jnp.clip(scores - max_per_dst[dst], -50.0, 50.0))
        sum_per_dst = jax.ops.segment_sum(exp, dst, num_segments=N)
        alpha = exp / (sum_per_dst[dst] + 1e-09)
        alpha = jnp.nan_to_num(alpha, nan=0.0, posinf=0.0, neginf=0.0)
        agg = jax.ops.segment_sum(v[src] * alpha[:, None], dst, num_segments=N)
        return jax.nn.relu(agg @ Wp.T + bp + h)

    def _L1_gnn_ref(node_feat, edge_index, W_edge, b_edge, W1, b1, W2, b2, eps):
        import jax, jax.numpy as jnp
        import numpy as np
        N, E, D = (100000, 500000, 128)
        n_nodes = node_feat.shape[0]
        src, dst = (edge_index[0], edge_index[1])
        h_src = node_feat[src]
        h_dst = node_feat[dst]
        edge_emb = jnp.concatenate([h_src, h_dst], axis=1)
        m = jax.nn.relu(edge_emb @ W_edge + b_edge)
        neigh = jax.ops.segment_sum(m, dst, num_segments=n_nodes)
        rst = (1.0 + eps[0]) * node_feat + neigh
        out = jax.nn.relu(rst @ W1 + b1) @ W2 + b2
        return out

    def _L2_gnn_ref(x, e_weight, src, dst, W1, b1, W2, b2):
        import jax, jax.numpy as jnp
        import numpy as np
        N_NODES = 50000
        N_EDGES = 25000
        D = 128

        def _degree_norm(idx, n_nodes, dtype):
            deg = jax.ops.segment_sum(jnp.ones((idx.shape[0],), dtype=dtype), idx, num_segments=n_nodes)
            return jax.lax.rsqrt(jnp.maximum(deg, 1.0))

        def _graph_conv(h, e_weight, src, dst, W, b, out_norm, in_norm):
            feat_src = h * out_norm[:, None]
            msg = feat_src[src] * e_weight[:, None]
            agg = jax.ops.segment_sum(msg, dst, num_segments=h.shape[0])
            agg = agg * in_norm[:, None]
            return jax.nn.relu(agg @ W + b)
        n = x.shape[0]
        out_norm = _degree_norm(src, n, x.dtype)
        in_norm = _degree_norm(dst, n, x.dtype)
        h = x
        for W, b in ((W1, b1), (W2, b2)):
            h_nxt = _graph_conv(h, e_weight, src, dst, W, b, out_norm, in_norm)
            h = h_nxt + h
        return h

    def _L3_gnn_ref(x, edges, kernel, ka1, ka2, bias):
        import jax, jax.numpy as jnp
        import numpy as np
        N_NODES = 100000
        N_EDGES = 25000
        D_IN = 128
        UNITS = 16
        HEADS = 8
        n = x.shape[0]
        src = edges[:, 0]
        tgt = edges[:, 1]
        xp = (x @ kernel).reshape(n, HEADS, UNITS)
        f_t = jnp.sum(xp * ka1, axis=-1)
        f_s = jnp.sum(xp * ka2, axis=-1)
        scores = jax.nn.leaky_relu(f_t[tgt] + f_s[src], negative_slope=0.2)
        seg_max = jax.ops.segment_max(scores, tgt, num_segments=n)
        scores = jnp.exp(scores - seg_max[tgt])
        denom = jax.ops.segment_sum(scores, tgt, num_segments=n) + 1e-07
        scores = scores / denom[tgt]
        out = jax.ops.segment_sum(scores[:, :, None] * xp[src], tgt, num_segments=n)
        out = out.reshape(n, HEADS * UNITS)
        return jax.nn.elu(out + bias)
    edge_index = jnp.stack([src, dst])
    edge_index_t = jnp.stack([src, dst], axis=1)
    x = _layernorm(x + _L0_gnn_ref(x, edge_index, L0_gnn_Wq, L0_gnn_Wk, L0_gnn_Wv, L0_gnn_Wp, L0_gnn_bp), axis=-1)
    x = _layernorm(x + _L1_gnn_ref(x, edge_index, L1_gnn_W_edge, L1_gnn_b_edge, L1_gnn_W1, L1_gnn_b1, L1_gnn_W2, L1_gnn_b2, L1_gnn_eps), axis=-1)
    x = _layernorm(x + _L2_gnn_ref(x, edge_weight, src, dst, L2_gnn_W1, L2_gnn_b1, L2_gnn_W2, L2_gnn_b2), axis=-1)
    x = _layernorm(x + _L3_gnn_ref(x, edge_index_t, L3_gnn_kernel, L3_gnn_ka1, L3_gnn_ka2, L3_gnn_bias), axis=-1)
    return x

_drawn_inputs = setup_inputs


def setup_inputs(seed=0):
    import zlib

    import numpy as np

    out = dict(_drawn_inputs(seed))
    spreads = {'L0_gnn_bp': (0.0, 0.1),
     'L1_gnn_b_edge': (0.0, 0.536),
     'L1_gnn_b1': (0.0, 0.1),
     'L1_gnn_b2': (0.0, 0.1),
     'L2_gnn_b1': (0.0, 0.282),
     'L2_gnn_b2': (0.0, 0.307),
     'L3_gnn_bias': (0.0, 0.1)}
    factors = {'L0_gnn_Wq': 2.853, 'L0_gnn_Wk': 2.912, 'L3_gnn_ka1': 8.0, 'L3_gnn_ka2': 4.138}
    for name, (base, spread) in spreads.items():
        noise = np.random.default_rng([zlib.crc32(name.encode()), seed]).standard_normal(out[name].shape)
        drawn = base * np.exp(spread * noise) if base else spread * noise
        out[name] = jnp.asarray(drawn.astype(out[name].dtype))
    for name, factor in factors.items():
        out[name] = (out[name] * factor).astype(out[name].dtype)
    return out
```

```python
from contextlib import ExitStack, contextmanager

import numpy as np

import concourse.bass as bass
from concourse import mybir

F32 = mybir.dt.float32
BF16 = mybir.dt.bfloat16
I32 = mybir.dt.int32
ALU = mybir.AluOpType
ACT = mybir.ActivationFunctionType

D = 128
T = 4
CH = T * D
DENSE_P = 125
HEADS = 8
UNITS = D // HEADS
TABLE_W = 1024
NO_NODE = 1 << 17
EPS = 1e-5
LOW = -1e30


def padded_slots(n_edges):
    return -(-n_edges // (2 * CH)) * 2 * CH


@contextmanager
def stage(nc, tag, single=(), paired=()):
    s = {n: nc.alloc_semaphore(f"{tag}_{n}") for n in single}
    s.update({n: [nc.alloc_semaphore(f"{tag}_{n}{b}") for b in (0, 1)] for n in paired})
    yield s
    every = [x for n in single for x in [s[n]]] + [x for n in paired for x in s[n]]
    nc.clear_and_free_semaphores(every)
    nc.all_engine_barrier()


class Program:
    pass


def gnn_kernel(nc, n_nodes, n_edges, args, out):
    k = Program()
    k.nc, k.args, k.out = nc, args, out
    k.n_nodes, k.n_edges = n_nodes, n_edges
    k.slots = padded_slots(n_edges)
    k.pairs = k.slots // (2 * CH)
    k.tiles = k.slots // D
    k.table_a = -(-n_nodes // TABLE_W)

    def scratch(name, shape, dt=F32):
        return nc.dram_tensor(name, shape, dt, kind="Internal").ap()

    k.table = scratch("node_table", (k.table_a * TABLE_W, 4), I32)
    k.d = [scratch(f"d{n}", (k.slots, D)) for n in range(4)]
    k.dh = scratch("dh", (k.slots, D))
    k.s = [scratch(f"s{n}", (k.slots, D)) for n in range(4)]
    k.sh = scratch("sh", (k.slots, D))
    k.val_t = scratch("val_t", (D, k.slots))
    k.score_t = scratch("score_t", (D, k.slots))
    k.max_t = scratch("max_t", (D, k.slots))

    with ExitStack() as ctx:
        def sb(name, shape, dt=F32):
            return ctx.enter_context(nc.sbuf_tensor(name, shape, dt))

        k.same = sb("same_dst", [D, k.slots + 2], BF16)
        k.src_ix = sb("src_ix", [D, k.tiles], I32)
        k.dst_ix = sb("dst_ix", [D, k.tiles], I32)
        k.first_ix = sb("first_ix", [D, k.tiles], I32)
        k.last_ix = sb("last_ix", [D, k.tiles], I32)
        k.out_ix = sb("out_ix", [D, k.tiles], I32)
        k.edge_scale = sb("edge_scale", [D, k.tiles])
        k.in_norm = sb("in_norm", [D, k.tiles])
        k.c = {n: sb(f"c_{n}", list(args[n].shape)) for n in CONSTANTS}
        k.att0 = sb("att0", [D, D])
        k.val0 = sb("val0", [D, D])
        k.att3_t = sb("att3_t", [D, D])
        k.att3_s = sb("att3_s", [D, D])
        k.one_eps = sb("one_eps", [D, 1])
        k.conv_c = sb("conv_c", [D, CH])
        k.conv_c1 = sb("conv_c1", [D, CH])
        k.elu_c = sb("elu_c", [D, CH])
        k.neg_half = sb("neg_half", [D, T])
        prepare_weights(k)
        prepare_graph(k)
        attention0_scores(k)
        attention0_sum(k)
        chain_pass(k, "chain_s", D, k.slots // CH, k.s[0], None)
        chain_pass(k, "dense", DENSE_P, k.n_nodes // (T * DENSE_P), args["x"], k.out)
        edge_mlp(k)
        convolution(k, "conv1", k.s[2], k.d[2], None, "L2_gnn_W1", "b_conv1", k.dh)
        convolution(k, "conv2", k.sh, k.dh, k.d[2], "L2_gnn_W2", "b_conv2", k.d[3])
        attention3_scores(k)
        attention3_sum(k)


CONSTANTS = [
    "L0_gnn_Wq", "L0_gnn_Wk", "L0_gnn_Wv", "Wp_t", "L1_Wa", "L1_Wb", "L1_gnn_W1", "L1_gnn_W2",
    "L2_gnn_W1", "L2_gnn_W2", "L3_gnn_kernel", "kernel_t", "b_p", "b_edge", "b_1", "b_2", "b_conv1",
    "b_conv2", "b_3", "ka1", "ka2", "eps", "identity", "head_block", "head_pick", "score_block",
    "first_row", "ones", "strict_upper",
]


def hold(eng, s, sem, value):
    eng.wait_ge(sem, value)
    eng.sem_inc(s["held"])


def chunk(ap, c):
    return ap.rearrange("(c t p) f -> c p t f", t=T, p=D)[bass.ds(c, 1)].rearrange("a p t f -> (a p) t f")


def columns(ap, c):
    return ap[:, bass.ds(c * CH, CH)]


def flat(t, b):
    return t[:, b].rearrange("p t f -> p (t f)")


def prepare_weights(k):
    nc, c = k.nc, k.c
    with stage(nc, "w", ["loaded", "zeroed", "block", "product", "copied", "relu", "conv", "low", "exp", "high"]) as s, ExitStack() as ctx:
        ps = [ctx.enter_context(nc.psum_tensor(f"w_ps{n}", [D, D], F32)) for n in range(4)]
        blocks = ctx.enter_context(nc.sbuf_tensor("w_blocks", [D, 2, D], F32))
        low = ctx.enter_context(nc.sbuf_tensor("w_low", [D, CH], F32))
        relu2 = ctx.enter_context(nc.sbuf_tensor("w_relu2", [D, CH], F32))
        n_loads = 16 * len(CONSTANTS)
        block = ctx.enter_context(nc.Block())

        @block.sync
        def _(sp):
            for n in CONSTANTS:
                sp.dma_start(c[n][:], k.args[n]).then_inc(s["loaded"], 16)

        @block.tensor
        def _(pe):
            pe.wait_ge(s["loaded"], n_loads)
            pe.matmul(ps[0][:], c["L0_gnn_Wq"][:], c["L0_gnn_Wk"][:], start=True, stop=True)
            pe.matmul(ps[1][:], c["L0_gnn_Wv"][:], c["Wp_t"][:], start=True, stop=True)
            pe.wait_ge(s["block"], 2)
            pe.matmul(ps[2][:], c["kernel_t"][:], blocks[:, 0], start=True, stop=True)
            pe.matmul(ps[3][:], c["kernel_t"][:], blocks[:, 1], start=True, stop=True).then_inc(s["product"], 1)

        @block.vector
        def _(dve):
            dve.wait_ge(s["loaded"], n_loads)
            dve.tensor_scalar(blocks[:, 0], c["head_block"][:], c["ka1"][:, 0:1], None, ALU.mult).then_inc(s["block"], 1)
            dve.tensor_scalar(blocks[:, 1], c["head_block"][:], c["ka2"][:, 0:1], None, ALU.mult).then_inc(s["block"], 1)
            dve.tensor_scalar(k.one_eps[:], c["eps"][:], 1.0, None, ALU.add)
            dve.memset(k.neg_half[:], -0.5)
            dve.tensor_scalar(k.conv_c1[:], c["b_conv1"][:], 0.0, None, ALU.max).then_inc(s["relu"], 1)
            dve.tensor_scalar(relu2[:], c["b_conv2"][:], 0.0, None, ALU.max).then_inc(s["relu"], 1)
            dve.tensor_scalar(low[:], c["b_3"][:], 0.0, None, ALU.min).then_inc(s["low"], 1)
            dve.wait_ge(s["relu"], 2)
            dve.tensor_tensor(k.conv_c[:], k.conv_c1[:], relu2[:], ALU.add).then_inc(s["conv"], 1)
            dve.wait_ge(s["exp"], 1)
            dve.wait_ge(s["conv"], 1)
            dve.tensor_scalar(relu2[:], k.elu_c[:], -1.0, None, ALU.add).then_inc(s["high"], 1)
            dve.wait_ge(s["high"], 1)
            dve.scalar_tensor_tensor(k.elu_c[:], c["b_3"][:], 0.0, relu2[:], ALU.max, ALU.add)
            dve.wait_ge(s["product"], 1)
            for to, frm in ((k.att0, ps[0]), (k.val0, ps[1]), (k.att3_t, ps[2]), (k.att3_s, ps[3])):
                dve.tensor_copy(to[:], frm[:])

        @block.scalar
        def _(act):
            act.wait_ge(s["low"], 1)
            act.activation(k.elu_c[:], low[:], ACT.Exp).then_inc(s["exp"], 1)


def prepare_graph(k):
    nc = k.nc
    A, W = k.table_a, TABLE_W
    half = W // 2
    with stage(nc, "h", ["held", "loaded", "split", "float", "iota", "cleared", "hot", "counted", "count_in", "ranks", "total", "offset", "offset_sb", "ended", "absent", "filled", "table"]) as s, ExitStack() as ctx:
        def sb(name, shape, dt=F32):
            return ctx.enter_context(nc.sbuf_tensor(f"h_{name}", shape, dt))
        cols = sb("cols", [D, 2, k.tiles], I32)
        parts = sb("parts", [D, 2, 2, k.tiles], I32)
        partsf = sb("partsf", [D, 2, 2, k.tiles])
        row_no = sb("row_no", [D, W], I32)
        row_nof = sb("row_nof", [D, W], mybir.dt.int16)
        hot_a = sb("hot_a", [D, 2, 2, A], BF16)
        hot_w = sb("hot_w", [D, 2, 2, W], BF16)
        zero = sb("zero", [D, half], BF16)
        count = sb("count", [A, W])
        upto = sb("upto", [A, W])
        ones_w = sb("ones_w", [A, W])
        offset = sb("offset", [A, 1])
        absent = sb("absent", [A, W])
        table = sb("table", [A, W, 4], I32)
        ps = [[ctx.enter_context(nc.psum_tensor(f"h_ps{g}{h}", [D, half], F32)) for h in (0, 1)] for g in (0, 1)]
        ps_off = ctx.enter_context(nc.psum_tensor("h_off", [D, 1], F32))
        block = ctx.enter_context(nc.Block())

        @block.sync
        def _(sp):
            sp.dma_start(cols[:, 0], k.args["src_hist"]).then_inc(s["loaded"], 16)
            sp.dma_start(cols[:, 1], k.args["dst_cols"]).then_inc(s["loaded"], 16)
            sp.dma_start(k.src_ix[:], k.args["src_cols"]).then_inc(s["loaded"], 16)
            sp.dma_start(k.dst_ix[:], k.args["dst_gather"]).then_inc(s["loaded"], 16)
            sp.wait_ge(s["filled"], 4)
            sp.dma_start(k.table.rearrange("(a w) f -> a (w f)", a=A), table[:].rearrange("a w f -> a (w f)")).then_inc(s["table"], 16)
            sp.wait_ge(s["table"], 16)
            sp.wait_ge(s["loaded"], 64)

        @block.gpsimd
        def _(pool):
            pool.iota(row_no[:], [[1, W]], base=0, channel_multiplier=0).then_inc(s["iota"], 1)

        @block.vector
        def _(dve):
            dve.memset(zero[:], 0.0).then_inc(s["cleared"], 1)
            dve.memset(ones_w[:], 1.0)
            dve.wait_ge(s["iota"], 1)
            dve.tensor_copy(row_nof[:], row_no[:]).then_inc(s["iota"], 1)
            dve.wait_ge(s["loaded"], 64)
            dve.tensor_scalar(parts[:, 0], cols[:], W.bit_length() - 1, None, ALU.logical_shift_right).then_inc(s["split"], 1)
            dve.tensor_scalar(parts[:, 1], cols[:], W - 1, None, ALU.bitwise_and).then_inc(s["split"], 1)
            dve.wait_ge(s["split"], 2)
            dve.tensor_copy(partsf[:], parts[:]).then_inc(s["float"], 1)
            dve.wait_ge(s["iota"], 2)
            dve.wait_ge(s["float"], 1)
            with dve.Fori(0, k.tiles // 2) as i:
                for b in (0, 1):
                    for g in (0, 1):
                        if g == 0:
                            dve.wait_ge(s["counted"], 2 * i + b + 1)
                        a_col = partsf[:, 0, g, bass.ds(2 * i + b, 1)]
                        w_col = partsf[:, 1, g, bass.ds(2 * i + b, 1)]
                        dve.tensor_scalar(hot_a[:, b, g], row_nof[:, 0:A], a_col, None, ALU.is_equal)
                        last = dve.tensor_scalar(hot_w[:, b, g], row_nof[:], w_col, None, ALU.is_equal)
                    last.then_inc(s["hot"], 1)
            dve.wait_ge(s["counted"], k.tiles + 2)
            for h in (0, 1):
                dve.tensor_copy(count[:, h * half:(h + 1) * half], ps[1][h][0:A, :]).then_inc(s["count_in"], 1)
                dve.tensor_copy(table[:, h * half:(h + 1) * half, 2], ps[0][h][0:A, :]).then_inc(s["filled"], 1)
            dve.wait_ge(s["count_in"], 2)
            dve.tensor_tensor_scan(upto[:], ones_w[:], count[:], 0.0, ALU.mult, ALU.add).then_inc(s["ranks"], 1)
            dve.wait_ge(s["offset"], 1)
            dve.tensor_copy(offset[:], ps_off[0:A, :]).then_inc(s["offset_sb"], 1)
            dve.tensor_scalar(absent[:], count[:], 0.0, float(NO_NODE), ALU.is_equal, ALU.mult).then_inc(s["absent"], 1)
            dve.wait_ge(s["offset_sb"], 1)
            dve.tensor_scalar(ones_w[:], upto[:], offset[:, 0:1], -1.0, ALU.add, ALU.add).then_inc(s["ended"], 1)
            dve.wait_ge(s["ended"], 1)
            dve.wait_ge(s["absent"], 1)
            dve.tensor_tensor(upto[:], ones_w[:], absent[:], ALU.add).then_inc(s["ended"], 1)
            dve.wait_ge(s["ended"], 2)
            dve.tensor_copy(table[:, :, 1], upto[:]).then_inc(s["filled"], 1)
            dve.tensor_copy(table[:, :, 3], upto[:])
            dve.tensor_tensor(absent[:], upto[:], count[:], ALU.subtract).then_inc(s["ended"], 1)
            dve.wait_ge(s["ended"], 3)
            dve.tensor_scalar(table[:, :, 0], absent[:], 1.0, None, ALU.add).then_inc(s["filled"], 1)

        @block.tensor
        def _(pe):
            pe.wait_ge(s["cleared"], 1)
            for g in (0, 1):
                for h in (0, 1):
                    last = pe.matmul(ps[g][h][:], zero[:, 0:D], zero[:], start=True, stop=False, skip_group_check=True)
            last.then_inc(s["counted"], 2)
            with pe.Fori(0, k.tiles // 2) as i:
                for b in (0, 1):
                    pe.wait_ge(s["hot"], 2 * i + b + 1)
                    for g in (0, 1):
                        for h in (0, 1):
                            last = pe.matmul(ps[g][h][0:A, :], hot_a[:, b, g], hot_w[:, b, g, h * half:(h + 1) * half],
                                             start=False, stop=False, skip_group_check=True)
                    last.then_inc(s["counted"], 1)
            pe.wait_ge(s["ranks"], 1)
            pe.matmul(ps_off[0:A, :], k.c["strict_upper"][0:A, 0:A], upto[:, W - 1:W], start=True, stop=True).then_inc(s["offset"], 1)

    with stage(nc, "m", ["held", "same", "counted", "degree", "loaded_ix", "skip", "start"], ["loaded"]) as s, ExitStack() as ctx:
        def sb(name, shape, dt=F32):
            return ctx.enter_context(nc.sbuf_tensor(f"m_{name}", shape, dt))
        dst = sb("dst", [D, 2, CH + 1], I32)
        count = sb("count", [D, 2, CH])
        one = sb("one", [D, CH])
        nxt = sb("nxt", [D, 2, k.tiles], I32)
        skip = sb("skip", [D, k.tiles], I32)
        ps = ctx.enter_context(nc.psum_tensor("m_ps", [D, k.tiles], F32))
        dst_ext = k.args["dst_ext"]
        block = ctx.enter_context(nc.Block())

        @block.sync
        def _(sp):
            def load(i, b):
                src = dst_ext[bass.ds((2 * i + b) * CH, CH + 1)] if not isinstance(i, int) else dst_ext[(2 * i + b) * CH:(2 * i + b + 1) * CH + 1]
                sp.dma_start(dst[:, b], src.partition_broadcast(D)).then_inc(s["loaded"][b], 16)
            sp.dma_start(nxt[:, 0], k.args["dst_cols"]).then_inc(s["loaded_ix"], 16)
            sp.dma_start(nxt[:, 1], k.args["dst_next"]).then_inc(s["loaded_ix"], 16)
            for b in (0, 1):
                load(0, b)
            with sp.Fori(0, k.pairs - 1) as i:
                for b in (0, 1):
                    hold(sp, s, s["same"], 2 * i + b + 1)
                    load(i + 1, b)

        @block.vector
        def _(dve):
            dve.memset(one[:], 1.0).then_inc(s["start"], 1)
            dve.memset(count[:, 1, CH - 1:CH], 0.0).then_inc(s["start"], 1)
            dve.memset(k.same[:, k.slots:], 0.0)
            dve.wait_ge(s["start"], 2)
            with dve.Fori(0, k.pairs) as i:
                for b in (0, 1):
                    c = 2 * i + b
                    dve.wait_ge(s["loaded"][b], 16 * (i + 1))
                    dve.tensor_tensor(k.same[:, bass.ds(c * CH, CH)], dst[:, b, 1:], dst[:, b, 0:CH], ALU.is_equal).then_inc(s["same"], 1)
                    dve.wait_ge(s["same"], c + 1)
                    if b == 0:
                        dve.wait_ge(s["degree"], 2 * i + 1)
                    else:
                        dve.wait_ge(s["degree"], 2 * i + 2)
                    dve.tensor_tensor_scan(count[:, b], k.same[:, bass.ds(c * CH, CH)], one[:], count[:, 1 - b, CH - 1:CH],
                                           ALU.mult, ALU.add).then_inc(s["counted"], 1)
                    dve.wait_ge(s["counted"], c + 1)
            dve.wait_ge(s["loaded_ix"], 32)
            dve.tensor_tensor(skip[:], nxt[:, 0], nxt[:, 1], ALU.is_equal).then_inc(s["skip"], 1)
            dve.wait_ge(s["skip"], 1)
            dve.scalar_tensor_tensor(k.out_ix[:], skip[:], float(NO_NODE), nxt[:, 0], ALU.mult, ALU.add)
            dve.wait_ge(s["degree"], 2 * k.pairs + 2)
            dve.tensor_copy(k.in_norm[:], ps[:])

        @block.tensor
        def _(pe):
            pe.sem_inc(s["degree"], 2)
            with pe.Fori(0, k.pairs) as i:
                for b in (0, 1):
                    c = 2 * i + b
                    pe.wait_ge(s["counted"], c + 1)
                    for t in range(T):
                        last = pe.matmul(ps[:, bass.ds(c * T + t, 1)], count[:, b, t * D:(t + 1) * D], k.c["first_row"][:],
                                         start=True, stop=True, skip_group_check=True)
                    last.then_inc(s["degree"], 1)

    with stage(nc, "g", ["held", "index", "split", "loaded", "atleast", "power", "half"], ["gathered"]) as s, ExitStack() as ctx:
        def sb(name, shape, dt=F32):
            return ctx.enter_context(nc.sbuf_tensor(f"g_{name}", shape, dt))
        index = sb("index", [D, 2, T], I32)
        found = sb("found", [D, 2, T, 4], I32)
        degree = sb("degree", [D, k.tiles])
        bounded = sb("bounded", [D, 2, k.tiles])
        power = sb("power", [D, k.tiles])
        neg_half = sb("neg_half", [D, k.tiles])
        weight = sb("weight", [D, k.tiles])
        block = ctx.enter_context(nc.Block())

        @block.sync
        def _(sp):
            sp.dma_start(weight[:], k.args["weight_cols"]).then_inc(s["loaded"], 16)

        @block.gpsimd
        def _(pool):
            def gather(i, b):
                c = 2 * i + b
                pool.tensor_copy(index[:, b], k.src_ix[:, bass.ds(c * T, T)]).then_inc(s["index"], 1)
                hold(pool, s, s["index"], c + 1)
                for t in range(T):
                    pool.indirect_dma_start(out=found[:, b, t], out_offset=None, in_=k.table,
                                            in_offset=bass.IndirectOffsetOnAxis(ap=index[:, b, t:t + 1], axis=0),
                                            bounds_check=k.table_a * TABLE_W - 1, oob_is_err=False).then_inc(s["gathered"][b], 16)
            for b in (0, 1):
                gather(0, b)
            with pool.Fori(0, k.pairs - 1) as i:
                for b in (0, 1):
                    hold(pool, s, s["split"], 2 * i + b + 1)
                    gather(i + 1, b)
            pool.wait_ge(s["atleast"], 2)
            pool.tensor_tensor(power[:], bounded[:, 0], neg_half[:], ALU.pow).then_inc(s["power"], 1)
            pool.tensor_tensor(k.in_norm[:], bounded[:, 1], neg_half[:], ALU.pow).then_inc(s["power"], 1)

        @block.vector
        def _(dve):
            dve.memset(neg_half[:], -0.5).then_inc(s["atleast"], 1)
            dve.tensor_scalar(bounded[:, 1], k.in_norm[:], 1.0, None, ALU.max)
            with dve.Fori(0, k.pairs) as i:
                for b in (0, 1):
                    at = bass.ds((2 * i + b) * T, T)
                    dve.wait_ge(s["gathered"][b], 16 * T * (i + 1))
                    dve.tensor_copy(k.first_ix[:, at], found[:, b, :, 0])
                    dve.tensor_copy(k.last_ix[:, at], found[:, b, :, 1])
                    dve.tensor_copy(degree[:, at], found[:, b, :, 2]).then_inc(s["split"], 1)
            dve.wait_ge(s["split"], 2 * k.pairs)
            dve.tensor_scalar(bounded[:, 0], degree[:], 1.0, None, ALU.max).then_inc(s["atleast"], 1)
            dve.wait_ge(s["loaded"], 16)
            dve.wait_ge(s["power"], 2)
            dve.tensor_tensor(k.edge_scale[:], weight[:], power[:], ALU.mult)


def moments(dve, s, z, stats, mv, n):
    for t in range(T):
        last = dve.bn_stats(stats[:, t], z[:, t])
    last.then_inc(s["stats_ready"], 1)
    hold(dve, s, s["stats_ready"], n + 1)
    for t in range(T):
        last = dve.bn_aggr(mv[:, t], stats[:, t])
    last.then_inc(s["moments_ready"], 1)


def rstd(pool, s, k, P, mv, var_eps, r, n, quarter=False):
    hold(pool, s, s["moments_ready"], n + 1)
    if quarter:
        pool.tensor_scalar(var_eps, mv[:, :, 1], EPS, 0.25, ALU.add, ALU.mult).then_inc(s["var_eps_ready"], 1)
    else:
        pool.tensor_scalar(var_eps, mv[:, :, 1], EPS, None, ALU.add).then_inc(s["var_eps_ready"], 1)
    hold(pool, s, s["var_eps_ready"], n + 1)
    pool.tensor_tensor(r, var_eps, k.neg_half[0:r.shape[0]], ALU.pow).then_inc(s["rstd_ready"], 1)


def normalise(dve, out, z, mv, r):
    for t in range(T):
        last = dve.tensor_scalar(out[:, t], z[:, t], mv[:, t, 0:1], r[:, t:t + 1], ALU.subtract, ALU.mult)
    return last


LN = ["stats_ready", "moments_ready", "var_eps_ready", "rstd_ready"]


def chain_pass(k, tag, P, groups, source, final):
    nc, c = k.nc, k.c
    keep = final is None
    norms = 3 if keep else 4
    pairs = groups // 2
    stored = ["stored_x1", "stored_x2", "stored_h1", "stored_x3"] if keep else ["stored_out"]
    single = ["held", "u_ready", "t_ready", "x1_ready", "x1T_ready", "rstT_ready", "hidden_ready", "hT_ready", "mlp_ready",
              "z_ready", "x2_ready", "h1_ready", "t2_ready", "x3_ready", "out_ready"] + LN
    with stage(nc, tag, single, ["loaded"] + stored) as s, ExitStack() as ctx:
        def sb(name, shape, dt=F32):
            return ctx.enter_context(nc.sbuf_tensor(f"{tag}_{name}", shape, dt))

        def bank(name):
            return [ctx.enter_context(nc.psum_tensor(f"{tag}_{name}{b}", [D, CH], F32)) for b in (0, 1)]
        rows = {n: sb(n, [D, 2, T, D]) for n in ["x", "u", "t", "x1", "z", "x2", "t2", "x3", "out"] + (["h1"] if keep else [])}
        stats, mv = sb("stats", [D, 2, T, 6]), sb("mv", [D, 2, T, 2])
        var_eps, r = sb("var_eps", [D, 2, T]), sb("r", [D, 2, T])
        rstT, hT = sb("rstT", [D, 2, T * P]), sb("hT", [D, 2, T * P])
        psT, psH, psO = bank("psT"), bank("psH"), bank("psO")

        def view(ap, g):
            if keep:
                return chunk(ap, g)
            return ap.rearrange("(g p t) f -> g p t f", p=P, t=T)[bass.ds(g, 1)].rearrange("a p t f -> (a p) t f")

        def R(name, b):
            return rows[name][0:P, b]

        def F(name, b):
            return R(name, b).rearrange("p t f -> p (t f)")
        block = ctx.enter_context(nc.Block())

        @block.sync
        def _(sp):
            def load(i, b):
                sp.dma_start(R("x", b), view(source, 2 * i + b)).then_inc(s["loaded"][b], 16)

            def store(i, b, ready, name, sem, to):
                hold(sp, s, s[ready], 2 * i + b + 1)
                sp.dma_start(view(to, 2 * i + b), R(name, b)).then_inc(s[sem][b], 16)

            def body(i, more):
                if more:
                    for b in (0, 1):
                        hold(sp, s, s["t_ready"], 2 * i + b + 1)
                        load(i + 1, b)
                if keep:
                    for ready, name, sem, to in (("x1_ready", "x1", "stored_x1", k.s[1]), ("x2_ready", "x2", "stored_x2", k.s[2]),
                                                 ("h1_ready", "h1", "stored_h1", k.sh), ("x3_ready", "x3", "stored_x3", k.s[3])):
                        for b in (0, 1):
                            store(i, b, ready, name, sem, to)
                else:
                    for b in (0, 1):
                        store(i, b, "out_ready", "out", "stored_out", final)
            for b in (0, 1):
                load(0, b)
            with sp.Fori(0, pairs - 1) as i:
                body(i, True)
            body(pairs - 1, False)
            for n in stored:
                for b in (0, 1):
                    sp.wait_ge(s[n][b], 16 * (pairs + 1))

        @block.vector
        def _(dve):
            for n in stored:
                for b in (0, 1):
                    dve.sem_inc(s[n][b], 16)
            with dve.Fori(0, pairs) as i:
                def at(b):
                    return 2 * i + b + 1

                def norm_no(n, b):
                    return 2 * norms * i + 2 * n + b

                def mom(name, n, b):
                    moments(dve, s, R(name, b), stats[0:P, b], mv[0:P, b], norm_no(n, b))

                def freed(sem, b):
                    if sem in stored:
                        dve.wait_ge(s[sem][b], 16 * (i + 1))
                for b in (0, 1):
                    dve.wait_ge(s["loaded"][b], 16 * (i + 1))
                    dve.tensor_tensor(F("u", b), F("x", b), c["b_p"][0:P], ALU.add).then_inc(s["u_ready"], 1)
                for b in (0, 1):
                    dve.wait_ge(s["u_ready"], at(b))
                    dve.scalar_tensor_tensor(F("t", b), F("u", b), 0.0, F("x", b), ALU.max, ALU.add).then_inc(s["t_ready"], 1)
                for b in (0, 1):
                    dve.wait_ge(s["t_ready"], at(b))
                    mom("t", 0, b)
                for b in (0, 1):
                    dve.wait_ge(s["rstd_ready"], norm_no(0, b) + 1)
                    freed("stored_x1", b)
                    normalise(dve, R("x1", b), R("t", b), mv[0:P, b], r[0:P, b]).then_inc(s["x1_ready"], 1)
                for b in (0, 1):
                    dve.wait_ge(s["mlp_ready"], at(b))
                    dve.tensor_tensor(F("z", b), psO[b][0:P], F("x1", b), ALU.add).then_inc(s["z_ready"], 1)
                for b in (0, 1):
                    dve.wait_ge(s["z_ready"], at(b))
                    mom("z", 1, b)
                if keep:
                    for b in (0, 1):
                        dve.wait_ge(s["rstd_ready"], norm_no(1, b) + 1)
                        freed("stored_x2", b)
                        normalise(dve, R("x2", b), R("z", b), mv[0:P, b], r[0:P, b]).then_inc(s["x2_ready"], 1)
                    for b in (0, 1):
                        dve.wait_ge(s["x2_ready"], at(b))
                        freed("stored_h1", b)
                        dve.tensor_tensor(F("h1", b), F("x2", b), k.conv_c1[0:P], ALU.add).then_inc(s["h1_ready"], 1)
                        dve.scalar_tensor_tensor(F("t2", b), F("x2", b), 2.0, k.conv_c[0:P], ALU.mult, ALU.add).then_inc(s["t2_ready"], 1)
                else:
                    for b in (0, 1):
                        dve.wait_ge(s["rstd_ready"], norm_no(1, b) + 1)
                        for t in range(T):
                            last = dve.scalar_tensor_tensor(rows["t2"][0:P, b, t], rows["z"][0:P, b, t], r[0:P, b, t:t + 1],
                                                            k.conv_c[0:P, 0:D], ALU.mult, ALU.add)
                        last.then_inc(s["t2_ready"], 1)
                for b in (0, 1):
                    dve.wait_ge(s["t2_ready"], at(b))
                    mom("t2", 2, b)
                if keep:
                    for b in (0, 1):
                        dve.wait_ge(s["rstd_ready"], norm_no(2, b) + 1)
                        freed("stored_x3", b)
                        normalise(dve, R("x3", b), R("t2", b), mv[0:P, b], r[0:P, b]).then_inc(s["x3_ready"], 1)
                else:
                    for b in (0, 1):
                        dve.wait_ge(s["rstd_ready"], norm_no(2, b) + 1)
                        for t in range(T):
                            last = dve.scalar_tensor_tensor(rows["x3"][0:P, b, t], rows["t2"][0:P, b, t], r[0:P, b, t:t + 1],
                                                            k.elu_c[0:P, 0:D], ALU.mult, ALU.add)
                        last.then_inc(s["x3_ready"], 1)
                    for b in (0, 1):
                        dve.wait_ge(s["x3_ready"], at(b))
                        mom("x3", 3, b)
                    for b in (0, 1):
                        dve.wait_ge(s["rstd_ready"], norm_no(3, b) + 1)
                        freed("stored_out", b)
                        normalise(dve, R("out", b), R("x3", b), mv[0:P, b], r[0:P, b]).then_inc(s["out_ready"], 1)

        @block.gpsimd
        def _(pool):
            with pool.Fori(0, pairs) as i:
                for n in range(norms):
                    for b in (0, 1):
                        rstd(pool, s, k, P, mv[0:P, b], var_eps[0:P, b], r[0:P, b], 2 * norms * i + 2 * n + b,
                             quarter=(n == 1 and not keep))

        @block.scalar
        def _(act):
            with act.Fori(0, pairs) as i:
                for b in (0, 1):
                    act.wait_ge(s["x1T_ready"], 2 * i + b + 1)
                    act.activation(rstT[:, b], psT[b][:, 0:T * P], ACT.Copy, scale=k.one_eps[:, 0:1]).then_inc(s["rstT_ready"], 1)
                for b in (0, 1):
                    act.wait_ge(s["hidden_ready"], 2 * i + b + 1)
                    act.activation(hT[:, b], psH[b][:, 0:T * P], ACT.Relu, bias=c["b_1"][:, 0:1]).then_inc(s["hT_ready"], 1)

        @block.tensor
        def _(pe):
            with pe.Fori(0, pairs) as i:
                for b in (0, 1):
                    pe.wait_ge(s["x1_ready"], 2 * i + b + 1)
                    for t in range(T):
                        last = pe.transpose(psT[b][:, t * P:(t + 1) * P], rows["x1"][0:P, b, t], c["identity"][0:P, 0:P])
                    last.then_inc(s["x1T_ready"], 1)
                for b in (0, 1):
                    pe.wait_ge(s["rstT_ready"], 2 * i + b + 1)
                    pe.matmul(psH[b][:, 0:T * P], c["L1_gnn_W1"][:], rstT[:, b], start=True, stop=True).then_inc(s["hidden_ready"], 1)
                for b in (0, 1):
                    pe.matmul(psO[b][0:P], c["ones"][0:1, 0:P], c["b_2"][0:1, :], start=True, stop=False, skip_group_check=True)
                    pe.wait_ge(s["hT_ready"], 2 * i + b + 1)
                    for t in range(T):
                        last = pe.matmul(psO[b][0:P, t * D:(t + 1) * D], hT[:, b, t * P:(t + 1) * P], c["L1_gnn_W2"][:],
                                         start=False, stop=(t == T - 1), skip_group_check=True)
                    last.then_inc(s["mlp_ready"], 1)


def gather_rows(pool, s, index, ix, rows, table, last_row, c, b, done):
    pool.tensor_copy(index[:, b], ix[:, bass.ds(c * T, T)]).then_inc(s["index_ready"], 1)
    hold(pool, s, s["index_ready"], c + 1)
    for t in range(T):
        pool.indirect_dma_start(out=rows[:, b, t], out_offset=None, in_=table,
                                in_offset=bass.IndirectOffsetOnAxis(ap=index[:, b, t:t + 1], axis=0),
                                bounds_check=last_row, oob_is_err=False).then_inc(done, 16)


def attention0_scores(k):
    nc, c = k.nc, k.c
    pairs = k.pairs
    single = ["held", "index_ready", "index_d_ready", "rowsT_ready", "srcT_ready", "dstT_ready", "query_ready", "product_ready",
              "score_ready", "score_sb_ready", "low_ready", "max_ready", "start"]
    with stage(nc, "a0", single, ["gathered", "stored_rows", "stored_T"]) as s, ExitStack() as ctx:
        def sb(name, shape, dt=F32):
            return ctx.enter_context(nc.sbuf_tensor(f"a0_{name}", shape, dt))

        def bank(name):
            return [ctx.enter_context(nc.psum_tensor(f"a0_{name}{b}", [D, CH], F32)) for b in (0, 1)]
        index = sb("index", [D, 2, T], I32)
        index_d = sb("index_d", [D, 2, T], I32)
        src, dst = sb("src", [D, 2, T, D]), sb("dst", [D, 2, T, D])
        srcT, dstT = sb("srcT", [D, 2, CH]), sb("dstT", [D, 2, CH])
        product, score = sb("product", [D, 2, CH]), sb("score", [D, 2, CH])
        low, top = sb("low", [D, 2, CH]), sb("top", [D, 2, CH])
        psS, psD, psQ, psC = bank("psS"), bank("psD"), bank("psQ"), bank("psC")
        block = ctx.enter_context(nc.Block())

        @block.gpsimd
        def _(pool):
            def gather(i, b):
                n = 2 * i + b
                gather_rows(pool, s, index, k.src_ix, src, k.args["x"], k.n_nodes - 1, n, b, s["gathered"][b])
                pool.tensor_copy(index_d[:, b], k.dst_ix[:, bass.ds(n * T, T)]).then_inc(s["index_d_ready"], 1)
                hold(pool, s, s["index_d_ready"], n + 1)
                for t in range(T):
                    pool.indirect_dma_start(out=dst[:, b, t], out_offset=None, in_=k.args["x"],
                                            in_offset=bass.IndirectOffsetOnAxis(ap=index_d[:, b, t:t + 1], axis=0),
                                            bounds_check=k.n_nodes - 1, oob_is_err=False).then_inc(s["gathered"][b], 16)
            for b in (0, 1):
                gather(0, b)
            with pool.Fori(0, pairs - 1) as i:
                for b in (0, 1):
                    hold(pool, s, s["rowsT_ready"], 2 * i + b + 1)
                    hold(pool, s, s["stored_rows"][b], 32 * (i + 1))
                    gather(i + 1, b)

        @block.sync
        def _(sp):
            with sp.Fori(0, pairs) as i:
                for b in (0, 1):
                    n = 2 * i + b
                    hold(sp, s, s["gathered"][b], 32 * T * (i + 1))
                    sp.dma_start(chunk(k.s[0], n), src[:, b]).then_inc(s["stored_rows"][b], 16)
                    sp.dma_start(chunk(k.d[0], n), dst[:, b]).then_inc(s["stored_rows"][b], 16)
                for b in (0, 1):
                    n = 2 * i + b
                    hold(sp, s, s["srcT_ready"], n + 1)
                    sp.dma_start(columns(k.val_t, n), srcT[:, b]).then_inc(s["stored_T"][b], 16)
                    hold(sp, s, s["score_sb_ready"], n + 1)
                    sp.dma_start(columns(k.score_t, n), score[:, b]).then_inc(s["stored_T"][b], 16)
                    hold(sp, s, s["max_ready"], n + 1)
                    sp.dma_start(columns(k.max_t, n), top[:, b]).then_inc(s["stored_T"][b], 16)
            for b in (0, 1):
                sp.wait_ge(s["stored_rows"][b], 32 * pairs)
                sp.wait_ge(s["stored_T"][b], 48 * (pairs + 1))

        @block.tensor
        def _(pe):
            with pe.Fori(0, pairs) as i:
                for b in (0, 1):
                    pe.wait_ge(s["gathered"][b], 32 * T * (i + 1))
                    for t in range(T):
                        pe.transpose(psS[b][:, t * D:(t + 1) * D], src[:, b, t], c["identity"][:])
                        last = pe.transpose(psD[b][:, t * D:(t + 1) * D], dst[:, b, t], c["identity"][:])
                    last.then_inc(s["rowsT_ready"], 1)
                for b in (0, 1):
                    pe.wait_ge(s["dstT_ready"], 2 * i + b + 1)
                    pe.matmul(psQ[b][:], k.att0[:], dstT[:, b], start=True, stop=True).then_inc(s["query_ready"], 1)
                for b in (0, 1):
                    pe.wait_ge(s["product_ready"], 2 * i + b + 1)
                    pe.matmul(psC[b][:], c["score_block"][:], product[:, b], start=True, stop=True).then_inc(s["score_ready"], 1)

        @block.scalar
        def _(act):
            for b in (0, 1):
                act.sem_inc(s["stored_T"][b], 48)
            with act.Fori(0, pairs) as i:
                for b in (0, 1):
                    act.wait_ge(s["rowsT_ready"], 2 * i + b + 1)
                    act.activation(dstT[:, b], psD[b][:], ACT.Copy).then_inc(s["dstT_ready"], 1)
                    act.wait_ge(s["stored_T"][b], 48 * (i + 1))
                    act.activation(srcT[:, b], psS[b][:], ACT.Copy).then_inc(s["srcT_ready"], 1)
                for b in (0, 1):
                    act.wait_ge(s["score_ready"], 2 * i + b + 1)
                    act.activation(score[:, b], psC[b][:], ACT.Copy).then_inc(s["score_sb_ready"], 1)

        @block.vector
        def _(dve):
            dve.memset(top[:, 1, CH - 1:CH], 0.0).then_inc(s["start"], 1)
            dve.wait_ge(s["start"], 1)
            with dve.Fori(0, pairs) as i:
                for b in (0, 1):
                    dve.tensor_scalar(low[:, b], k.same[:, bass.ds((2 * i + b) * CH, CH)], -1.0, -LOW, ALU.add, ALU.mult).then_inc(s["low_ready"], 1)
                    dve.wait_ge(s["query_ready"], 2 * i + b + 1)
                    dve.wait_ge(s["srcT_ready"], 2 * i + b + 1)
                    dve.tensor_tensor(product[:, b], psQ[b][:], srcT[:, b], ALU.mult).then_inc(s["product_ready"], 1)
                for b in (0, 1):
                    dve.wait_ge(s["low_ready"], 2 * i + b + 1)
                    dve.wait_ge(s["stored_T"][b], 48 * (i + 1))
                    dve.wait_ge(s["score_sb_ready"], 2 * i + b + 1)
                    if b == 1:
                        dve.wait_ge(s["max_ready"], 2 * i + 1)
                    dve.tensor_tensor_scan(top[:, b], low[:, b], score[:, b], top[:, 1 - b, CH - 1:CH], ALU.add, ALU.max).then_inc(s["max_ready"], 1)
                dve.wait_ge(s["max_ready"], 2 * i + 2)


def attention0_sum(k):
    nc, c = k.nc, k.c
    pairs = k.pairs
    single = ["held", "start", "mask_ready", "lastmax_ready", "maxheld_ready", "shifted_ready", "clipped_ready", "exp_ready", "weighted_ready",
              "den_ready", "num_ready", "agg_ready", "denb_ready", "rden_ready", "biased_ready", "scaled_ready", "u_ready",
              "t_ready", "x1_ready"] + LN
    with stage(nc, "b0", single, ["loaded", "stored"]) as s, ExitStack() as ctx:
        def sb(name, shape, dt=F32):
            return ctx.enter_context(nc.sbuf_tensor(f"b0_{name}", shape, dt))

        def bank(name, n=CH):
            return [ctx.enter_context(nc.psum_tensor(f"b0_{name}{b}", [D, n], F32)) for b in (0, 1)]
        valT, score, top, x = sb("valT", [D, 2, CH]), sb("score", [D, 2, CH]), sb("top", [D, 2, CH]), sb("x", [D, 2, T, D])
        lastmax, maxheld, shifted, clipped = (sb(n, [D, 2, CH]) for n in ("lastmax", "maxheld", "shifted", "clipped"))
        expo, weighted, num, den = (sb(n, [D, 2, CH]) for n in ("expo", "weighted", "num", "den"))
        mask = sb("mask", [D, 2, CH], BF16)
        denb, rden = sb("denb", [D, 2, T]), sb("rden", [D, 2, T])
        biased, scaled, u, t_, x1 = (sb(n, [D, 2, T, D]) for n in ("biased", "scaled", "u", "t", "x1"))
        stats, mv = sb("stats", [D, 2, T, 6]), sb("mv", [D, 2, T, 2])
        var_eps, r = sb("var_eps", [D, 2, T]), sb("r", [D, 2, T])
        psA, psN = bank("psA"), bank("psN", T)
        block = ctx.enter_context(nc.Block())

        def q(i, b):
            return (2 * pairs - 1) - (2 * i + b)

        @block.sync
        def _(sp):
            def load(i, b):
                sp.dma_start(valT[:, b], columns(k.val_t, q(i, b))).then_inc(s["loaded"][b], 16)
                sp.dma_start(score[:, b], columns(k.score_t, q(i, b))).then_inc(s["loaded"][b], 16)
                sp.dma_start(top[:, b], columns(k.max_t, q(i, b))).then_inc(s["loaded"][b], 16)
                sp.dma_start(x[:, b], chunk(k.d[0], q(i, b))).then_inc(s["loaded"][b], 16)

            def body(i, more):
                for b in (0, 1):
                    if more:
                        hold(sp, s, s["t_ready"], 2 * i + b + 1)
                        load(i + 1, b)
                for b in (0, 1):
                    hold(sp, s, s["x1_ready"], 2 * i + b + 1)
                    sp.dma_start(chunk(k.d[1], q(i, b)), x1[:, b]).then_inc(s["stored"][b], 16)
            for b in (0, 1):
                load(0, b)
            with sp.Fori(0, pairs - 1) as i:
                body(i, True)
            body(pairs - 1, False)
            for b in (0, 1):
                sp.wait_ge(s["stored"][b], 16 * (pairs + 1))

        @block.scalar
        def _(act):
            def load_mask(i, b):
                act.activation(mask[:, b], k.same[:, bass.ds(q(i, b) * CH + 1, CH)], ACT.Copy).then_inc(s["mask_ready"], 1)

            def body(i, more):
                for b in (0, 1):
                    act.wait_ge(s["clipped_ready"], 2 * i + b + 1)
                    act.activation(expo[:, b], clipped[:, b], ACT.Exp).then_inc(s["exp_ready"], 1)
                for b in (0, 1):
                    if more:
                        act.wait_ge(s["num_ready"], 2 * i + b + 1)
                        load_mask(i + 1, b)
            for b in (0, 1):
                load_mask(0, b)
            with act.Fori(0, pairs - 1) as i:
                body(i, True)
            body(pairs - 1, False)

        @block.gpsimd
        def _(pool):
            with pool.Fori(0, pairs) as i:
                for b in (0, 1):
                    hold(pool, s, s["loaded"][b], 64 * (i + 1))
                    pool.tensor_tensor(flat(biased, b), flat(x, b), c["b_p"][:], ALU.add).then_inc(s["biased_ready"], 1)
                for b in (0, 1):
                    rstd(pool, s, k, D, mv[:, b], var_eps[:, b], r[:, b], 2 * i + b)

        @block.tensor
        def _(pe):
            with pe.Fori(0, pairs) as i:
                for b in (0, 1):
                    pe.wait_ge(s["den_ready"], 2 * i + b + 1)
                    for t in range(T):
                        pe.matmul(psN[b][:, t:t + 1], den[:, b, t * D:(t + 1) * D], c["first_row"][:], start=True, stop=True, skip_group_check=True)
                    pe.wait_ge(s["num_ready"], 2 * i + b + 1)
                    for t in range(T):
                        last = pe.matmul(psA[b][:, t * D:(t + 1) * D], num[:, b, t * D:(t + 1) * D], k.val0[:], start=True, stop=True, skip_group_check=True)
                    last.then_inc(s["agg_ready"], 1)

        @block.vector
        def _(dve):
            for b in (0, 1):
                dve.sem_inc(s["stored"][b], 16)
            for buf in (maxheld, num, den):
                dve.memset(buf[:, 1, 0:1], 0.0).then_inc(s["start"], 1)
            dve.wait_ge(s["start"], 3)
            with dve.Fori(0, pairs) as i:
                both = (0, 1)

                def at(b):
                    return 2 * i + b + 1

                for b in both:
                    dve.wait_ge(s["mask_ready"], at(b))
                    dve.wait_ge(s["loaded"][b], 64 * (i + 1))
                    dve.scalar_tensor_tensor(lastmax[:, b], mask[:, b], -1.0, top[:, b], ALU.add, ALU.mult).then_inc(s["lastmax_ready"], 1)
                for b in both:
                    dve.wait_ge(s["lastmax_ready"], at(b))
                    if b == 1:
                        dve.wait_ge(s["maxheld_ready"], 2 * i + 1)
                    dve.tensor_tensor_scan(maxheld[:, b, ::-1], mask[:, b, ::-1], lastmax[:, b, ::-1], maxheld[:, 1 - b, 0:1],
                                           ALU.mult, ALU.subtract).then_inc(s["maxheld_ready"], 1)
                for b in both:
                    dve.wait_ge(s["maxheld_ready"], at(b))
                    dve.tensor_tensor(shifted[:, b], score[:, b], maxheld[:, b], ALU.subtract).then_inc(s["shifted_ready"], 1)
                for b in both:
                    dve.wait_ge(s["shifted_ready"], at(b))
                    dve.tensor_scalar(clipped[:, b], shifted[:, b], -50.0, 50.0, ALU.max, ALU.min).then_inc(s["clipped_ready"], 1)
                for b in both:
                    dve.wait_ge(s["exp_ready"], at(b))
                    dve.tensor_tensor(weighted[:, b], expo[:, b], valT[:, b], ALU.mult).then_inc(s["weighted_ready"], 1)
                    if b == 1:
                        dve.wait_ge(s["den_ready"], 2 * i + 1)
                    dve.tensor_tensor_scan(den[:, b, ::-1], mask[:, b, ::-1], expo[:, b, ::-1], den[:, 1 - b, 0:1],
                                           ALU.mult, ALU.add).then_inc(s["den_ready"], 1)
                for b in both:
                    dve.wait_ge(s["weighted_ready"], at(b))
                    if b == 1:
                        dve.wait_ge(s["num_ready"], 2 * i + 1)
                    dve.tensor_tensor_scan(num[:, b, ::-1], mask[:, b, ::-1], weighted[:, b, ::-1], num[:, 1 - b, 0:1],
                                           ALU.mult, ALU.add).then_inc(s["num_ready"], 1)
                for b in both:
                    dve.wait_ge(s["agg_ready"], at(b))
                    dve.tensor_scalar(denb[:, b], psN[b][:], 1e-9, None, ALU.add).then_inc(s["denb_ready"], 1)
                    dve.wait_ge(s["denb_ready"], at(b))
                    dve.reciprocal(rden[:, b], denb[:, b]).then_inc(s["rden_ready"], 1)
                for b in both:
                    dve.wait_ge(s["rden_ready"], at(b))
                    dve.tensor_tensor(scaled[:, b], psA[b][:].rearrange("p (t f) -> p t f", t=T),
                                      rden[:, b].unsqueeze(2).to_broadcast([D, T, D]), ALU.mult).then_inc(s["scaled_ready"], 1)
                for b in both:
                    dve.wait_ge(s["scaled_ready"], at(b))
                    dve.wait_ge(s["biased_ready"], at(b))
                    dve.tensor_tensor(flat(u, b), flat(scaled, b), flat(biased, b), ALU.add).then_inc(s["u_ready"], 1)
                for b in both:
                    dve.wait_ge(s["u_ready"], at(b))
                    dve.scalar_tensor_tensor(flat(t_, b), flat(u, b), 0.0, flat(x, b), ALU.max, ALU.add).then_inc(s["t_ready"], 1)
                for b in both:
                    dve.wait_ge(s["t_ready"], at(b))
                    moments(dve, s, t_[:, b], stats[:, b], mv[:, b], 2 * i + b)
                for b in both:
                    dve.wait_ge(s["rstd_ready"], at(b))
                    dve.wait_ge(s["stored"][b], 16 * (i + 1))
                    normalise(dve, x1[:, b], t_[:, b], mv[:, b], r[:, b]).then_inc(s["x1_ready"], 1)


def edge_mlp(k):
    nc, c = k.nc, k.c
    pairs = k.pairs
    single = ["held", "start", "index_ready", "rowsT_ready", "srcT_ready", "firstrow_ready", "dstheld_ready", "message_ready",
              "relu_ready", "sum_ready", "rst_ready", "hidden_ready", "hT_ready", "z_ready", "x2_ready"] + LN
    with stage(nc, "l1", single, ["loaded_s", "loaded_d", "gathered", "stored"]) as s, ExitStack() as ctx:
        def sb(name, shape, dt=F32):
            return ctx.enter_context(nc.sbuf_tensor(f"l1_{name}", shape, dt))

        def bank(name):
            return [ctx.enter_context(nc.psum_tensor(f"l1_{name}{b}", [D, CH], F32)) for b in (0, 1)]
        index = sb("index", [D, 2, T], I32)
        src, dst, x2 = (sb(n, [D, 2, T, D]) for n in ("src", "dst", "x2"))
        srcT, firstrow, dstheld, message, neigh, rst, hT = (sb(n, [D, 2, CH]) for n in ("srcT", "firstrow", "dstheld", "message", "neigh", "rst", "hT"))
        stats, mv = sb("stats", [D, 2, T, 6]), sb("mv", [D, 2, T, 2])
        var_eps, r = sb("var_eps", [D, 2, T]), sb("r", [D, 2, T])
        psS, psD, psM, psO = bank("psS"), bank("psD"), bank("psM"), bank("psO")
        block = ctx.enter_context(nc.Block())

        @block.sync
        def _(sp):
            def load(i, b):
                sp.dma_start(src[:, b], chunk(k.s[1], 2 * i + b)).then_inc(s["loaded_s"][b], 16)
                sp.dma_start(dst[:, b], chunk(k.d[1], 2 * i + b)).then_inc(s["loaded_d"][b], 16)

            def body(i, more):
                for b in (0, 1):
                    if more:
                        hold(sp, s, s["rowsT_ready"], 2 * i + b + 1)
                        load(i + 1, b)
                for b in (0, 1):
                    hold(sp, s, s["x2_ready"], 2 * i + b + 1)
                    sp.dma_start(chunk(k.d[2], 2 * i + b), x2[:, b]).then_inc(s["stored"][b], 16)
            for b in (0, 1):
                load(0, b)
            with sp.Fori(0, pairs - 1) as i:
                body(i, True)
            body(pairs - 1, False)
            for b in (0, 1):
                sp.wait_ge(s["stored"][b], 16 * (pairs + 1))

        @block.gpsimd
        def _(pool):
            def gather(i, b):
                hold(pool, s, s["loaded_s"][b], 16 * (i + 1))
                gather_rows(pool, s, index, k.first_ix, src, k.d[1], k.slots - 1, 2 * i + b, b, s["gathered"][b])
            for b in (0, 1):
                gather(0, b)
            with pool.Fori(0, pairs - 1) as i:
                for b in (0, 1):
                    gather(i + 1, b)
                    rstd(pool, s, k, D, mv[:, b], var_eps[:, b], r[:, b], 2 * i + b)
            for b in (0, 1):
                rstd(pool, s, k, D, mv[:, b], var_eps[:, b], r[:, b], 2 * (pairs - 1) + b)

        @block.tensor
        def _(pe):
            with pe.Fori(0, pairs) as i:
                for b in (0, 1):
                    pe.wait_ge(s["gathered"][b], 16 * T * (i + 1))
                    pe.wait_ge(s["loaded_d"][b], 16 * (i + 1))
                    for t in range(T):
                        pe.transpose(psS[b][:, t * D:(t + 1) * D], src[:, b, t], c["identity"][:])
                        last = pe.transpose(psD[b][:, t * D:(t + 1) * D], dst[:, b, t], c["identity"][:])
                    last.then_inc(s["rowsT_ready"], 1)
                for b in (0, 1):
                    pe.wait_ge(s["srcT_ready"], 2 * i + b + 1)
                    pe.matmul(psM[b][:], c["L1_Wa"][:], srcT[:, b], start=True, stop=False)
                    pe.wait_ge(s["dstheld_ready"], 2 * i + b + 1)
                    pe.matmul(psM[b][:], c["L1_Wb"][:], dstheld[:, b], start=False, stop=True).then_inc(s["message_ready"], 1)
                for b in (0, 1):
                    pe.wait_ge(s["rst_ready"], 2 * i + b + 1)
                    pe.matmul(psM[b][:], c["L1_gnn_W1"][:], rst[:, b], start=True, stop=True).then_inc(s["hidden_ready"], 1)
                for b in (0, 1):
                    pe.matmul(psO[b][:], c["ones"][0:1, :], c["b_2"][0:1, :], start=True, stop=False, skip_group_check=True)
                    pe.wait_ge(s["hT_ready"], 2 * i + b + 1)
                    for t in range(T):
                        at = slice(t * D, (t + 1) * D)
                        pe.matmul(psO[b][:, at], dstheld[:, b, at], c["identity"][:], start=False, stop=False, skip_group_check=True)
                        last = pe.matmul(psO[b][:, at], hT[:, b, at], c["L1_gnn_W2"][:], start=False, stop=(t == T - 1), skip_group_check=True)
                    last.then_inc(s["z_ready"], 1)

        @block.scalar
        def _(act):
            with act.Fori(0, pairs) as i:
                for b in (0, 1):
                    act.wait_ge(s["rowsT_ready"], 2 * i + b + 1)
                    act.activation(srcT[:, b], psS[b][:], ACT.Copy).then_inc(s["srcT_ready"], 1)
                for b in (0, 1):
                    act.wait_ge(s["message_ready"], 2 * i + b + 1)
                    act.activation(message[:, b], psM[b][:], ACT.Relu, bias=c["b_edge"][:, 0:1]).then_inc(s["relu_ready"], 1)
                for b in (0, 1):
                    act.wait_ge(s["hidden_ready"], 2 * i + b + 1)
                    act.activation(hT[:, b], psM[b][:], ACT.Relu, bias=c["b_1"][:, 0:1]).then_inc(s["hT_ready"], 1)

        @block.vector
        def _(dve):
            for b in (0, 1):
                dve.sem_inc(s["stored"][b], 16)
            for buf in (dstheld, neigh):
                dve.memset(buf[:, 1, CH - 1:CH], 0.0).then_inc(s["start"], 1)
            dve.wait_ge(s["start"], 2)
            with dve.Fori(0, pairs) as i:
                both = (0, 1)

                def at(b):
                    return 2 * i + b + 1

                def same(b):
                    return k.same[:, bass.ds((2 * i + b) * CH, CH)]
                for b in both:
                    dve.wait_ge(s["rowsT_ready"], at(b))
                    dve.scalar_tensor_tensor(firstrow[:, b], same(b), -1.0, psD[b][:], ALU.add, ALU.mult).then_inc(s["firstrow_ready"], 1)
                for b in both:
                    dve.wait_ge(s["firstrow_ready"], at(b))
                    if b == 1:
                        dve.wait_ge(s["dstheld_ready"], 2 * i + 1)
                    dve.tensor_tensor_scan(dstheld[:, b], same(b), firstrow[:, b], dstheld[:, 1 - b, CH - 1:CH], ALU.mult, ALU.subtract).then_inc(s["dstheld_ready"], 1)
                for b in both:
                    dve.wait_ge(s["relu_ready"], at(b))
                    if b == 1:
                        dve.wait_ge(s["sum_ready"], 2 * i + 1)
                    dve.tensor_tensor_scan(neigh[:, b], same(b), message[:, b], neigh[:, 1 - b, CH - 1:CH], ALU.mult, ALU.add).then_inc(s["sum_ready"], 1)
                for b in both:
                    dve.wait_ge(s["sum_ready"], at(b))
                    dve.scalar_tensor_tensor(rst[:, b], dstheld[:, b], k.one_eps[:, 0:1], neigh[:, b], ALU.mult, ALU.add).then_inc(s["rst_ready"], 1)
                for b in both:
                    z = psO[b][:].rearrange("p (t f) -> p t f", t=T)
                    dve.wait_ge(s["z_ready"], at(b))
                    moments(dve, s, z, stats[:, b], mv[:, b], 2 * i + b)
                for b in both:
                    z = psO[b][:].rearrange("p (t f) -> p t f", t=T)
                    dve.wait_ge(s["rstd_ready"], at(b))
                    dve.wait_ge(s["stored"][b], 16 * (i + 1))
                    normalise(dve, x2[:, b], z, mv[:, b], r[:, b]).then_inc(s["x2_ready"], 1)
                dve.wait_ge(s["x2_ready"], at(1))


def convolution(k, tag, own, table, residual, weight, bias, out):
    nc, c = k.nc, k.c
    pairs = k.pairs
    ends = residual is not None
    single = ["held", "start", "index_ready", "weighted_ready", "rowsT_ready", "sum_ready", "product_ready", "scaled_ready", "u_ready",
              "h_ready", "t_ready", "out_ready"] + LN
    with stage(nc, tag, single, ["loaded_s", "loaded_d", "gathered", "stored"]) as s, ExitStack() as ctx:
        def sb(name, shape, dt=F32):
            return ctx.enter_context(nc.sbuf_tensor(f"{tag}_{name}", shape, dt))

        def bank(name):
            return [ctx.enter_context(nc.psum_tensor(f"{tag}_{name}{b}", [D, CH], F32)) for b in (0, 1)]
        index = sb("index", [D, 2, T], I32)
        src, dst, res, weighted, scaled, u, h, t_, x3 = (sb(n, [D, 2, T, D]) for n in ("src", "dst", "res", "weighted", "scaled", "u", "h", "t", "x3"))
        agg = sb("agg", [D, 2, CH])
        stats, mv = sb("stats", [D, 2, T, 6]), sb("mv", [D, 2, T, 2])
        var_eps, r = sb("var_eps", [D, 2, T]), sb("r", [D, 2, T])
        psS, psA = bank("psS"), bank("psA")
        final, final_ready, used = (x3, "out_ready", "t_ready") if ends else (h, "h_ready", "h_ready")
        n_d = 2 if ends else 1
        block = ctx.enter_context(nc.Block())

        @block.sync
        def _(sp):
            def load(i, b):
                sp.dma_start(src[:, b], chunk(own, 2 * i + b)).then_inc(s["loaded_s"][b], 16)
                sp.dma_start(dst[:, b], chunk(table, 2 * i + b)).then_inc(s["loaded_d"][b], 16)
                if ends:
                    sp.dma_start(res[:, b], chunk(residual, 2 * i + b)).then_inc(s["loaded_d"][b], 16)

            def body(i, more):
                for b in (0, 1):
                    if more:
                        hold(sp, s, s[used], 2 * i + b + 1)
                        load(i + 1, b)
                for b in (0, 1):
                    hold(sp, s, s[final_ready], 2 * i + b + 1)
                    sp.dma_start(chunk(out, 2 * i + b), final[:, b]).then_inc(s["stored"][b], 16)
            for b in (0, 1):
                load(0, b)
            with sp.Fori(0, pairs - 1) as i:
                body(i, True)
            body(pairs - 1, False)
            for b in (0, 1):
                sp.wait_ge(s["stored"][b], 16 * (pairs + 1))

        @block.gpsimd
        def _(pool):
            def gather(i, b):
                hold(pool, s, s["loaded_s"][b], 16 * (i + 1))
                gather_rows(pool, s, index, k.last_ix, src, table, k.slots - 1, 2 * i + b, b, s["gathered"][b])
            for b in (0, 1):
                gather(0, b)
            with pool.Fori(0, pairs - 1) as i:
                for b in (0, 1):
                    if ends:
                        rstd(pool, s, k, D, mv[:, b], var_eps[:, b], r[:, b], 2 * i + b)
                    gather(i + 1, b)
            if ends:
                for b in (0, 1):
                    rstd(pool, s, k, D, mv[:, b], var_eps[:, b], r[:, b], 2 * (pairs - 1) + b)

        @block.tensor
        def _(pe):
            with pe.Fori(0, pairs) as i:
                for b in (0, 1):
                    pe.wait_ge(s["weighted_ready"], 2 * i + b + 1)
                    for t in range(T):
                        last = pe.transpose(psS[b][:, t * D:(t + 1) * D], weighted[:, b, t], c["identity"][:])
                    last.then_inc(s["rowsT_ready"], 1)
                for b in (0, 1):
                    pe.wait_ge(s["sum_ready"], 2 * i + b + 1)
                    for t in range(T):
                        at = slice(t * D, (t + 1) * D)
                        last = pe.matmul(psA[b][:, at], agg[:, b, at], c[weight][:], start=True, stop=True, skip_group_check=True)
                    last.then_inc(s["product_ready"], 1)

        @block.vector
        def _(dve):
            for b in (0, 1):
                dve.sem_inc(s["stored"][b], 16)
            dve.memset(agg[:, 1, CH - 1:CH], 0.0).then_inc(s["start"], 1)
            dve.wait_ge(s["start"], 1)
            with dve.Fori(0, pairs) as i:
                both = (0, 1)

                def at(b):
                    return 2 * i + b + 1

                def per_slot(ap, b):
                    return ap[:, bass.ds((2 * i + b) * T, T)].unsqueeze(2).to_broadcast([D, T, D])
                for b in both:
                    dve.wait_ge(s["gathered"][b], 16 * T * (i + 1))
                    dve.tensor_tensor(weighted[:, b], src[:, b], per_slot(k.edge_scale, b), ALU.mult).then_inc(s["weighted_ready"], 1)
                for b in both:
                    dve.wait_ge(s["rowsT_ready"], at(b))
                    if b == 1:
                        dve.wait_ge(s["sum_ready"], 2 * i + 1)
                    dve.tensor_tensor_scan(agg[:, b], k.same[:, bass.ds((2 * i + b) * CH, CH)], psS[b][:], agg[:, 1 - b, CH - 1:CH],
                                           ALU.mult, ALU.add).then_inc(s["sum_ready"], 1)
                for b in both:
                    dve.wait_ge(s["product_ready"], at(b))
                    dve.tensor_tensor(scaled[:, b], psA[b][:].rearrange("p (t f) -> p t f", t=T), per_slot(k.in_norm, b), ALU.mult).then_inc(s["scaled_ready"], 1)
                for b in both:
                    dve.wait_ge(s["scaled_ready"], at(b))
                    dve.tensor_tensor(flat(u, b), flat(scaled, b), c[bias][:], ALU.add).then_inc(s["u_ready"], 1)
                for b in both:
                    dve.wait_ge(s["u_ready"], at(b))
                    dve.wait_ge(s["loaded_d"][b], 16 * n_d * (i + 1))
                    if not ends:
                        dve.wait_ge(s["stored"][b], 16 * (i + 1))
                    dve.scalar_tensor_tensor(flat(h, b), flat(u, b), 0.0, flat(dst, b), ALU.max, ALU.add).then_inc(s["h_ready"], 1)
                if ends:
                    for b in both:
                        dve.wait_ge(s["h_ready"], at(b))
                        dve.tensor_tensor(flat(t_, b), flat(h, b), flat(res, b), ALU.add).then_inc(s["t_ready"], 1)
                    for b in both:
                        dve.wait_ge(s["t_ready"], at(b))
                        moments(dve, s, t_[:, b], stats[:, b], mv[:, b], 2 * i + b)
                    for b in both:
                        dve.wait_ge(s["rstd_ready"], at(b))
                        dve.wait_ge(s["stored"][b], 16 * (i + 1))
                        normalise(dve, x3[:, b], t_[:, b], mv[:, b], r[:, b]).then_inc(s["out_ready"], 1)


def attention3_scores(k):
    nc, c = k.nc, k.c
    pairs = k.pairs
    single = ["held", "start", "mask_ready", "index_ready", "rowsT_ready", "srcT_ready", "dstT_ready", "product_ready", "value_ready",
              "lastrow_ready", "target_ready", "z_ready", "score_ready", "low_ready", "max_ready"]
    with stage(nc, "a3", single, ["loaded_s", "loaded_d", "gathered", "stored"]) as s, ExitStack() as ctx:
        def sb(name, shape, dt=F32):
            return ctx.enter_context(nc.sbuf_tensor(f"a3_{name}", shape, dt))

        def bank(name):
            return [ctx.enter_context(nc.psum_tensor(f"a3_{name}{b}", [D, CH], F32)) for b in (0, 1)]
        index = sb("index", [D, 2, T], I32)
        src, dst = sb("src", [D, 2, T, D]), sb("dst", [D, 2, T, D])
        srcT, dstT, value, lastrow, target, z, score, low, top = (
            sb(n, [D, 2, CH]) for n in ("srcT", "dstT", "value", "lastrow", "target", "z", "score", "low", "top"))
        mask = sb("mask", [D, 2, CH], BF16)
        psS, psD, psX, psF = bank("psS"), bank("psD"), bank("psX"), bank("psF")
        block = ctx.enter_context(nc.Block())

        def q(i, b):
            return (2 * pairs - 1) - (2 * i + b)

        @block.sync
        def _(sp):
            def load(i, b):
                sp.dma_start(src[:, b], chunk(k.s[3], q(i, b))).then_inc(s["loaded_s"][b], 16)
                sp.dma_start(dst[:, b], chunk(k.d[3], q(i, b))).then_inc(s["loaded_d"][b], 16)

            def body(i, more):
                for b in (0, 1):
                    if more:
                        hold(sp, s, s["rowsT_ready"], 2 * i + b + 1)
                        load(i + 1, b)
                for b in (0, 1):
                    hold(sp, s, s["value_ready"], 2 * i + b + 1)
                    sp.dma_start(columns(k.val_t, q(i, b)), value[:, b]).then_inc(s["stored"][b], 16)
                    hold(sp, s, s["max_ready"], 2 * i + b + 1)
                    sp.dma_start(columns(k.score_t, q(i, b)), score[:, b]).then_inc(s["stored"][b], 16)
                    sp.dma_start(columns(k.max_t, q(i, b)), top[:, b]).then_inc(s["stored"][b], 16)
            for b in (0, 1):
                load(0, b)
            with sp.Fori(0, pairs - 1) as i:
                body(i, True)
            body(pairs - 1, False)
            for b in (0, 1):
                sp.wait_ge(s["stored"][b], 48 * (pairs + 1))

        @block.gpsimd
        def _(pool):
            def gather(i, b):
                hold(pool, s, s["loaded_s"][b], 16 * (i + 1))
                pool.tensor_copy(index[:, b], k.last_ix[:, bass.ds(q(i, b) * T, T)]).then_inc(s["index_ready"], 1)
                hold(pool, s, s["index_ready"], 2 * i + b + 1)
                for t in range(T):
                    pool.indirect_dma_start(out=src[:, b, t], out_offset=None, in_=k.d[3],
                                            in_offset=bass.IndirectOffsetOnAxis(ap=index[:, b, t:t + 1], axis=0),
                                            bounds_check=k.slots - 1, oob_is_err=False).then_inc(s["gathered"][b], 16)
            with pool.Fori(0, pairs) as i:
                for b in (0, 1):
                    gather(i, b)

        @block.tensor
        def _(pe):
            with pe.Fori(0, pairs) as i:
                for b in (0, 1):
                    pe.wait_ge(s["gathered"][b], 16 * T * (i + 1))
                    pe.wait_ge(s["loaded_d"][b], 16 * (i + 1))
                    for t in range(T):
                        pe.transpose(psS[b][:, t * D:(t + 1) * D], src[:, b, t], c["identity"][:])
                        last = pe.transpose(psD[b][:, t * D:(t + 1) * D], dst[:, b, t], c["identity"][:])
                    last.then_inc(s["rowsT_ready"], 1)
                for b in (0, 1):
                    pe.wait_ge(s["dstT_ready"], 2 * i + b + 1)
                    pe.matmul(psD[b][:], k.att3_t[:], dstT[:, b], start=True, stop=True)
                    pe.wait_ge(s["srcT_ready"], 2 * i + b + 1)
                    pe.matmul(psF[b][:], k.att3_s[:], srcT[:, b], start=True, stop=True)
                    pe.matmul(psX[b][:], c["L3_gnn_kernel"][:], srcT[:, b], start=True, stop=True).then_inc(s["product_ready"], 1)
                pe.wait_ge(s["z_ready"], 2 * i + 2)
                pe.wait_ge(s["value_ready"], 2 * i + 2)

        @block.scalar
        def _(act):
            for b in (0, 1):
                act.sem_inc(s["stored"][b], 48)
            def load_mask(i, b):
                act.activation(mask[:, b], k.same[:, bass.ds(q(i, b) * CH + 1, CH)], ACT.Copy).then_inc(s["mask_ready"], 1)

            def body(i, more):
                for b in (0, 1):
                    act.wait_ge(s["rowsT_ready"], 2 * i + b + 1)
                    act.activation(dstT[:, b], psD[b][:], ACT.Copy).then_inc(s["dstT_ready"], 1)
                    act.activation(srcT[:, b], psS[b][:], ACT.Copy).then_inc(s["srcT_ready"], 1)
                for b in (0, 1):
                    act.wait_ge(s["product_ready"], 2 * i + b + 1)
                    act.wait_ge(s["stored"][b], 48 * (i + 1))
                    act.activation(value[:, b], psX[b][:], ACT.Copy).then_inc(s["value_ready"], 1)
                for b in (0, 1):
                    if more:
                        act.wait_ge(s["target_ready"], 2 * i + b + 1)
                        load_mask(i + 1, b)
            for b in (0, 1):
                load_mask(0, b)
            with act.Fori(0, pairs - 1) as i:
                body(i, True)
            body(pairs - 1, False)

        @block.vector
        def _(dve):
            for buf in (target, top):
                dve.memset(buf[:, 1, 0:1], 0.0).then_inc(s["start"], 1)
            dve.wait_ge(s["start"], 2)
            with dve.Fori(0, pairs) as i:
                both = (0, 1)

                def at(b):
                    return 2 * i + b + 1

                for b in both:
                    dve.wait_ge(s["mask_ready"], at(b))
                    dve.tensor_scalar(low[:, b], mask[:, b], -1.0, -LOW, ALU.add, ALU.mult).then_inc(s["low_ready"], 1)
                for b in both:
                    dve.wait_ge(s["product_ready"], at(b))
                    dve.scalar_tensor_tensor(lastrow[:, b], mask[:, b], -1.0, psD[b][:], ALU.add, ALU.mult).then_inc(s["lastrow_ready"], 1)
                for b in both:
                    dve.wait_ge(s["lastrow_ready"], at(b))
                    if b == 1:
                        dve.wait_ge(s["target_ready"], 2 * i + 1)
                    dve.tensor_tensor_scan(target[:, b, ::-1], mask[:, b, ::-1], lastrow[:, b, ::-1], target[:, 1 - b, 0:1],
                                           ALU.mult, ALU.subtract).then_inc(s["target_ready"], 1)
                for b in both:
                    dve.wait_ge(s["target_ready"], at(b))
                    dve.tensor_tensor(z[:, b], psF[b][:], target[:, b], ALU.add).then_inc(s["z_ready"], 1)
                for b in both:
                    dve.wait_ge(s["z_ready"], at(b))
                    dve.wait_ge(s["stored"][b], 48 * (i + 1))
                    dve.scalar_tensor_tensor(score[:, b], z[:, b], 0.2, z[:, b], ALU.mult, ALU.max).then_inc(s["score_ready"], 1)
                for b in both:
                    dve.wait_ge(s["score_ready"], at(b))
                    if b == 1:
                        dve.wait_ge(s["max_ready"], 2 * i + 1)
                    dve.tensor_tensor_scan(top[:, b, ::-1], low[:, b, ::-1], score[:, b, ::-1], top[:, 1 - b, 0:1],
                                           ALU.add, ALU.max).then_inc(s["max_ready"], 1)
                dve.wait_ge(s["max_ready"], at(1))


def attention3_sum(k):
    nc, c = k.nc, k.c
    pairs = k.pairs
    single = ["held", "start", "index_ready", "firstmax_ready", "maxheld_ready", "shifted_ready", "exp_ready", "weighted_ready",
              "den_ready", "num_ready", "rows_ready", "denb_ready", "rden_ready", "scaled_ready", "y_ready", "neg_ready",
              "expm_ready", "pos_ready", "t_ready", "out_ready", "out_free"] + LN
    with stage(nc, "b3", single, ["loaded", "scattered"]) as s, ExitStack() as ctx:
        def sb(name, shape, dt=F32):
            return ctx.enter_context(nc.sbuf_tensor(f"b3_{name}", shape, dt))

        def bank(name, n=CH):
            return [ctx.enter_context(nc.psum_tensor(f"b3_{name}{b}", [D, n], F32)) for b in (0, 1)]
        index = sb("index", [D, 2, T], I32)
        valT, score, top, firstmax, maxheld, shifted, expo, weighted, num, den = (
            sb(n, [D, 2, CH]) for n in ("valT", "score", "top", "firstmax", "maxheld", "shifted", "expo", "weighted", "num", "den"))
        x, scaled, y, neg, expm, pos, t_, out = (sb(n, [D, 2, T, D]) for n in ("x", "scaled", "y", "neg", "expm", "pos", "t", "out"))
        denb, rden = sb("denb", [D, 2, T * HEADS]), sb("rden", [D, 2, T * HEADS])
        stats, mv = sb("stats", [D, 2, T, 6]), sb("mv", [D, 2, T, 2])
        var_eps, r = sb("var_eps", [D, 2, T]), sb("r", [D, 2, T])
        psA, psN = bank("psA"), bank("psN", T * HEADS)
        block = ctx.enter_context(nc.Block())

        @block.sync
        def _(sp):
            def load(i, b):
                n = 2 * i + b
                sp.dma_start(valT[:, b], columns(k.val_t, n)).then_inc(s["loaded"][b], 16)
                sp.dma_start(score[:, b], columns(k.score_t, n)).then_inc(s["loaded"][b], 16)
                sp.dma_start(top[:, b], columns(k.max_t, n)).then_inc(s["loaded"][b], 16)
                sp.dma_start(x[:, b], chunk(k.d[3], n)).then_inc(s["loaded"][b], 16)
            for b in (0, 1):
                load(0, b)
            with sp.Fori(0, pairs - 1) as i:
                for b in (0, 1):
                    hold(sp, s, s["pos_ready"], 2 * i + b + 1)
                    load(i + 1, b)

        @block.scalar
        def _(act):
            with act.Fori(0, pairs) as i:
                for b in (0, 1):
                    act.wait_ge(s["shifted_ready"], 2 * i + b + 1)
                    act.activation(expo[:, b], shifted[:, b], ACT.Exp).then_inc(s["exp_ready"], 1)
                for b in (0, 1):
                    act.wait_ge(s["neg_ready"], 2 * i + b + 1)
                    act.activation(flat(expm, b), flat(neg, b), ACT.Exp).then_inc(s["expm_ready"], 1)

        @block.gpsimd
        def _(pool):
            pool.sem_inc(s["out_free"], 2)
            with pool.Fori(0, pairs) as i:
                for b in (0, 1):
                    rstd(pool, s, k, D, mv[:, b], var_eps[:, b], r[:, b], 2 * i + b)
                for b in (0, 1):
                    n = 2 * i + b
                    hold(pool, s, s["out_ready"], n + 1)
                    pool.tensor_copy(index[:, b], k.out_ix[:, bass.ds(n * T, T)]).then_inc(s["index_ready"], 1)
                    hold(pool, s, s["index_ready"], n + 1)
                    for t in range(T):
                        pool.indirect_dma_start(out=k.out, out_offset=bass.IndirectOffsetOnAxis(ap=index[:, b, t:t + 1], axis=0),
                                                in_=out[:, b, t], in_offset=None,
                                                bounds_check=k.n_nodes - 1, oob_is_err=False).then_inc(s["scattered"][b], 16)
                for b in (0, 1):
                    hold(pool, s, s["scattered"][b], 16 * T * (i + 1))
                    pool.sem_inc(s["out_free"])

        @block.tensor
        def _(pe):
            with pe.Fori(0, pairs) as i:
                for b in (0, 1):
                    pe.wait_ge(s["den_ready"], 2 * i + b + 1)
                    for t in range(T):
                        pe.matmul(psN[b][:, t * HEADS:(t + 1) * HEADS], den[:, b, t * D:(t + 1) * D], c["head_pick"][:],
                                  start=True, stop=True, skip_group_check=True)
                    pe.wait_ge(s["num_ready"], 2 * i + b + 1)
                    for t in range(T):
                        last = pe.transpose(psA[b][:, t * D:(t + 1) * D], num[:, b, t * D:(t + 1) * D], c["identity"][:])
                    last.then_inc(s["rows_ready"], 1)

        @block.vector
        def _(dve):
            for buf in (maxheld, num, den):
                dve.memset(buf[:, 1, CH - 1:CH], 0.0).then_inc(s["start"], 1)
            dve.wait_ge(s["start"], 3)
            with dve.Fori(0, pairs) as i:
                both = (0, 1)

                def at(b):
                    return 2 * i + b + 1

                def same(b):
                    return k.same[:, bass.ds((2 * i + b) * CH, CH)]
                for b in both:
                    dve.wait_ge(s["loaded"][b], 64 * (i + 1))
                    dve.scalar_tensor_tensor(firstmax[:, b], same(b), -1.0, top[:, b], ALU.add, ALU.mult).then_inc(s["firstmax_ready"], 1)
                for b in both:
                    dve.wait_ge(s["firstmax_ready"], at(b))
                    if b == 1:
                        dve.wait_ge(s["maxheld_ready"], 2 * i + 1)
                    dve.tensor_tensor_scan(maxheld[:, b], same(b), firstmax[:, b], maxheld[:, 1 - b, CH - 1:CH], ALU.mult, ALU.subtract).then_inc(s["maxheld_ready"], 1)
                for b in both:
                    dve.wait_ge(s["maxheld_ready"], at(b))
                    dve.tensor_tensor(shifted[:, b], score[:, b], maxheld[:, b], ALU.subtract).then_inc(s["shifted_ready"], 1)
                for b in both:
                    dve.wait_ge(s["exp_ready"], at(b))
                    dve.tensor_tensor(weighted[:, b], expo[:, b], valT[:, b], ALU.mult).then_inc(s["weighted_ready"], 1)
                    if b == 1:
                        dve.wait_ge(s["den_ready"], 2 * i + 1)
                    dve.tensor_tensor_scan(den[:, b], same(b), expo[:, b], den[:, 1 - b, CH - 1:CH], ALU.mult, ALU.add).then_inc(s["den_ready"], 1)
                for b in both:
                    dve.wait_ge(s["weighted_ready"], at(b))
                    if b == 1:
                        dve.wait_ge(s["num_ready"], 2 * i + 1)
                    dve.tensor_tensor_scan(num[:, b], same(b), weighted[:, b], num[:, 1 - b, CH - 1:CH], ALU.mult, ALU.add).then_inc(s["num_ready"], 1)
                for b in both:
                    dve.wait_ge(s["rows_ready"], at(b))
                    dve.tensor_scalar(denb[:, b], psN[b][:], 1e-7, None, ALU.add).then_inc(s["denb_ready"], 1)
                    dve.wait_ge(s["denb_ready"], at(b))
                    dve.reciprocal(rden[:, b], denb[:, b]).then_inc(s["rden_ready"], 1)
                for b in both:
                    dve.wait_ge(s["rden_ready"], at(b))
                    dve.tensor_tensor(flat(scaled, b).rearrange("p (g u) -> p g u", u=UNITS), psA[b][:].rearrange("p (g u) -> p g u", u=UNITS),
                                      rden[:, b].unsqueeze(2).to_broadcast([D, T * HEADS, UNITS]), ALU.mult).then_inc(s["scaled_ready"], 1)
                for b in both:
                    dve.wait_ge(s["scaled_ready"], at(b))
                    dve.tensor_tensor(flat(y, b), flat(scaled, b), c["b_3"][:], ALU.add).then_inc(s["y_ready"], 1)
                for b in both:
                    dve.wait_ge(s["y_ready"], at(b))
                    dve.tensor_scalar(flat(neg, b), flat(y, b), 0.0, None, ALU.min).then_inc(s["neg_ready"], 1)
                    dve.scalar_tensor_tensor(flat(pos, b), flat(y, b), 0.0, flat(x, b), ALU.max, ALU.add).then_inc(s["pos_ready"], 1)
                for b in both:
                    dve.wait_ge(s["pos_ready"], at(b))
                    dve.wait_ge(s["expm_ready"], at(b))
                    dve.scalar_tensor_tensor(flat(t_, b), flat(expm, b), -1.0, flat(pos, b), ALU.add, ALU.add).then_inc(s["t_ready"], 1)
                for b in both:
                    dve.wait_ge(s["t_ready"], at(b))
                    moments(dve, s, t_[:, b], stats[:, b], mv[:, b], 2 * i + b)
                for b in both:
                    dve.wait_ge(s["rstd_ready"], at(b))
                    dve.wait_ge(s["out_free"], at(b))
                    normalise(dve, out[:, b], t_[:, b], mv[:, b], r[:, b]).then_inc(s["out_ready"], 1)


def launch_arrays(inputs, n_nodes, n_edges):
    g = {n: np.ascontiguousarray(v) for n, v in inputs.items()}
    slots = padded_slots(n_edges)

    def pad(a, value):
        return np.concatenate([a, np.full(slots - n_edges, value, a.dtype)])

    def cols(a):
        return np.ascontiguousarray(a.reshape(-1, D).T)

    def rows(a):
        return np.ascontiguousarray(np.tile(a[None, :], (D, T)))

    def col(a):
        return np.ascontiguousarray(a.reshape(D, 1))
    dst_ext = np.concatenate([np.full(1, -1, np.int32), pad(g["dst"], NO_NODE), np.full(1, NO_NODE + 1, np.int32)])
    a = {
        "x": g["x"],
        "src_cols": cols(pad(g["src"], 0)), "src_hist": cols(pad(g["src"], NO_NODE)),
        "dst_gather": cols(pad(g["dst"], 0)), "dst_cols": cols(pad(g["dst"], NO_NODE)),
        "dst_next": cols(dst_ext[2:]), "dst_ext": dst_ext, "weight_cols": cols(pad(g["edge_weight"], 0)),
        "Wp_t": np.ascontiguousarray(g["L0_gnn_Wp"].T), "kernel_t": np.ascontiguousarray(g["L3_gnn_kernel"].T),
        "L1_Wa": np.ascontiguousarray(g["L1_gnn_W_edge"][:D]), "L1_Wb": np.ascontiguousarray(g["L1_gnn_W_edge"][D:]),
        "b_p": rows(g["L0_gnn_bp"]), "b_2": rows(g["L1_gnn_b2"]), "b_conv1": rows(g["L2_gnn_b1"]),
        "b_conv2": rows(g["L2_gnn_b2"]), "b_3": rows(g["L3_gnn_bias"]),
        "b_edge": col(g["L1_gnn_b_edge"]), "b_1": col(g["L1_gnn_b1"]),
        "ka1": col(g["L3_gnn_ka1"]), "ka2": col(g["L3_gnn_ka2"]),
        "eps": np.ascontiguousarray(np.broadcast_to(g["L1_gnn_eps"].reshape(1, 1), (D, 1))),
    }
    for n in ("L0_gnn_Wq", "L0_gnn_Wk", "L0_gnn_Wv", "L1_gnn_W1", "L1_gnn_W2", "L2_gnn_W1", "L2_gnn_W2", "L3_gnn_kernel"):
        a[n] = g[n]
    head = np.arange(D) // UNITS
    a["identity"] = np.eye(D, dtype=np.float32)
    a["head_block"] = (head[:, None] == head[None, :]).astype(np.float32)
    a["head_pick"] = (np.arange(D)[:, None] == UNITS * np.arange(HEADS)[None, :]).astype(np.float32)
    a["score_block"] = np.full((D, D), D ** -0.5, np.float32)
    a["first_row"] = (np.arange(D) == 0).astype(np.float32)[:, None]
    a["ones"] = np.ones((D, D), np.float32)
    a["strict_upper"] = np.triu(np.ones((D, D), np.float32), 1)
    return a


def build(nc, arrays, n_nodes, n_edges):
    args = {n: nc.dram_tensor(f"in_{n}", v.shape, mybir.dt.from_np(v.dtype), kind="ExternalInput").ap() for n, v in arrays.items()}
    out = nc.dram_tensor("out", (n_nodes, D), F32, kind="ExternalOutput").ap()
    gnn_kernel(nc, n_nodes, n_edges, args, out)


def kernel(**inputs):
    import concourse.bacc as bacc
    from concourse.bass_utils import run_bass_kernel_spmd

    n_nodes, n_edges = inputs["x"].shape[0], inputs["src"].shape[0]
    nc = bacc.Bacc("TRN2", target_bir_lowering=False, num_devices=1)
    arrays = launch_arrays({n: np.asarray(v) for n, v in inputs.items()}, n_nodes, n_edges)
    build(nc, arrays, n_nodes, n_edges)
    r = run_bass_kernel_spmd(nc, [{f"in_{n}": v for n, v in arrays.items()}], core_ids=[0])
    return r.results[0]["out"]
```

```python
from contextlib import ExitStack, contextmanager

import numpy as np

import concourse.bass as bass
from concourse import mybir

F32 = mybir.dt.float32
BF16 = mybir.dt.bfloat16
I32 = mybir.dt.int32
ALU = mybir.AluOpType
ACT = mybir.ActivationFunctionType

D = 128
T = 4
CH = T * D
UT = 8
DENSE_P = 125
HEADS = 8
UNITS = D // HEADS
TABLE_W = 1024
NO_NODE = 1 << 17
EPS = 1e-5
LOW = -1e30


def padded_slots(n_edges):
    return -(-n_edges // (2 * CH)) * 2 * CH


@contextmanager
def stage(nc, tag, single=(), paired=()):
    s = {n: nc.alloc_semaphore(f"{tag}_{n}") for n in single}
    s.update({n: [nc.alloc_semaphore(f"{tag}_{n}{b}") for b in (0, 1)] for n in paired})
    yield s
    every = [x for n in single for x in [s[n]]] + [x for n in paired for x in s[n]]
    nc.clear_and_free_semaphores(every)
    nc.all_engine_barrier()


class Program:
    pass


def gnn_kernel(nc, n_nodes, n_edges, args, out):
    k = Program()
    k.nc, k.args, k.out = nc, args, out
    k.n_nodes, k.n_edges = n_nodes, n_edges
    k.slots = padded_slots(n_edges)
    k.pairs = k.slots // (2 * CH)
    k.tiles = k.slots // D
    k.table_a = -(-n_nodes // TABLE_W)

    def scratch(name, shape, dt=F32):
        return nc.dram_tensor(name, shape, dt, kind="Internal").ap()

    k.table = scratch("node_table", (k.table_a * TABLE_W, 4), I32)
    k.d = [scratch(f"d{n}", (k.slots, D)) for n in range(4)]
    k.dh = scratch("dh", (k.slots, D))
    k.s = [scratch(f"s{n}", (k.slots, D)) for n in range(4)]
    k.sh = scratch("sh", (k.slots, D))
    k.val_t = scratch("val_t", (D, k.slots))
    k.score_t = scratch("score_t", (D, k.slots))
    k.max_t = scratch("max_t", (D, k.slots))

    with ExitStack() as ctx:
        def sb(name, shape, dt=F32):
            return ctx.enter_context(nc.sbuf_tensor(name, shape, dt))

        k.same = sb("same_dst", [D, k.slots + 2], BF16)
        k.src_ix = sb("src_ix", [D, k.tiles], I32)
        k.dst_ix = sb("dst_ix", [D, k.tiles], I32)
        k.first_ix = sb("first_ix", [D, k.tiles], I32)
        k.last_ix = sb("last_ix", [D, k.tiles], I32)
        k.out_ix = sb("out_ix", [D, k.tiles], I32)
        k.edge_scale = sb("edge_scale", [D, k.tiles])
        k.in_norm = sb("in_norm", [D, k.tiles])
        k.c = {n: sb(f"c_{n}", list(args[n].shape)) for n in CONSTANTS}
        k.att0 = sb("att0", [D, D])
        k.val0 = sb("val0", [D, D])
        k.att3_t = sb("att3_t", [D, D])
        k.att3_s = sb("att3_s", [D, D])
        k.one_eps = sb("one_eps", [D, 1])
        k.conv_c = sb("conv_c", [D, CH])
        k.conv_c1 = sb("conv_c1", [D, CH])
        k.elu_c = sb("elu_c", [D, CH])
        k.neg_half = sb("neg_half", [D, T])
        k.eps_ln, k.eps_quarter = sb("eps_ln", [D, 1]), sb("eps_quarter", [D, 1])
        prepare_weights(k)
        prepare_graph(k)
        attention0_scores(k)
        attention0_sum(k)
        chain_pass(k, "chain_s", D, k.tiles, k.s[0], None)
        chain_pass(k, "dense", DENSE_P, k.n_nodes // DENSE_P, args["x"], k.out)
        edge_mlp(k)
        convolution(k, "conv1", k.s[2], k.d[2], None, "L2_gnn_W1", "b_conv1", k.dh)
        convolution(k, "conv2", k.sh, k.dh, k.d[2], "L2_gnn_W2", "b_conv2", k.d[3])
        attention3_scores(k)
        attention3_sum(k)


CONSTANTS = [
    "L0_gnn_Wq", "L0_gnn_Wk", "L0_gnn_Wv", "Wp_t", "L1_Wa", "L1_Wb", "L1_gnn_W1", "L1_gnn_W2",
    "L2_gnn_W1", "L2_gnn_W2", "L3_gnn_kernel", "kernel_t", "b_p", "b_edge", "b_1", "b_2", "b_conv1",
    "b_conv2", "b_3", "ka1", "ka2", "eps", "identity", "head_block", "head_pick", "score_block",
    "first_row", "ones", "strict_upper",
]


def hold(eng, s, sem, value):
    eng.wait_ge(sem, value)
    eng.sem_inc(s["held"])


def chunk(ap, c):
    return ap.rearrange("(c t p) f -> c p t f", t=T, p=D)[bass.ds(c, 1)].rearrange("a p t f -> (a p) t f")


def columns(ap, c):
    return ap[:, bass.ds(c * CH, CH)]


def flat(t, b):
    return t[:, b].rearrange("p t f -> p (t f)")


def prepare_weights(k):
    nc, c = k.nc, k.c
    with stage(nc, "w", ["loaded", "zeroed", "block", "product", "copied", "relu", "conv", "low", "exp", "high"]) as s, ExitStack() as ctx:
        ps = [ctx.enter_context(nc.psum_tensor(f"w_ps{n}", [D, D], F32)) for n in range(4)]
        blocks = ctx.enter_context(nc.sbuf_tensor("w_blocks", [D, 2, D], F32))
        low = ctx.enter_context(nc.sbuf_tensor("w_low", [D, CH], F32))
        relu2 = ctx.enter_context(nc.sbuf_tensor("w_relu2", [D, CH], F32))
        n_loads = 16 * len(CONSTANTS)
        block = ctx.enter_context(nc.Block())

        @block.sync
        def _(sp):
            for n in CONSTANTS:
                sp.dma_start(c[n][:], k.args[n]).then_inc(s["loaded"], 16)

        @block.tensor
        def _(pe):
            pe.wait_ge(s["loaded"], n_loads)
            pe.matmul(ps[0][:], c["L0_gnn_Wq"][:], c["L0_gnn_Wk"][:], start=True, stop=True)
            pe.matmul(ps[1][:], c["L0_gnn_Wv"][:], c["Wp_t"][:], start=True, stop=True)
            pe.wait_ge(s["block"], 2)
            pe.matmul(ps[2][:], c["kernel_t"][:], blocks[:, 0], start=True, stop=True)
            pe.matmul(ps[3][:], c["kernel_t"][:], blocks[:, 1], start=True, stop=True).then_inc(s["product"], 1)

        @block.vector
        def _(dve):
            dve.wait_ge(s["loaded"], n_loads)
            dve.tensor_scalar(blocks[:, 0], c["head_block"][:], c["ka1"][:, 0:1], None, ALU.mult).then_inc(s["block"], 1)
            dve.tensor_scalar(blocks[:, 1], c["head_block"][:], c["ka2"][:, 0:1], None, ALU.mult).then_inc(s["block"], 1)
            dve.tensor_scalar(k.one_eps[:], c["eps"][:], 1.0, None, ALU.add)
            dve.memset(k.neg_half[:], -0.5)
            dve.memset(k.eps_ln[:], EPS)
            dve.memset(k.eps_quarter[:], EPS / 4)
            dve.tensor_scalar(k.conv_c1[:], c["b_conv1"][:], 0.0, None, ALU.max).then_inc(s["relu"], 1)
            dve.tensor_scalar(relu2[:], c["b_conv2"][:], 0.0, None, ALU.max).then_inc(s["relu"], 1)
            dve.tensor_scalar(low[:], c["b_3"][:], 0.0, None, ALU.min).then_inc(s["low"], 1)
            dve.wait_ge(s["relu"], 2)
            dve.tensor_tensor(k.conv_c[:], k.conv_c1[:], relu2[:], ALU.add).then_inc(s["conv"], 1)
            dve.wait_ge(s["exp"], 1)
            dve.wait_ge(s["conv"], 1)
            dve.tensor_scalar(relu2[:], k.elu_c[:], -1.0, None, ALU.add).then_inc(s["high"], 1)
            dve.wait_ge(s["high"], 1)
            dve.scalar_tensor_tensor(k.elu_c[:], c["b_3"][:], 0.0, relu2[:], ALU.max, ALU.add)
            dve.wait_ge(s["product"], 1)
            for to, frm in ((k.att0, ps[0]), (k.val0, ps[1]), (k.att3_t, ps[2]), (k.att3_s, ps[3])):
                dve.tensor_copy(to[:], frm[:])

        @block.scalar
        def _(act):
            act.wait_ge(s["low"], 1)
            act.activation(k.elu_c[:], low[:], ACT.Exp).then_inc(s["exp"], 1)


def prepare_graph(k):
    nc = k.nc
    A, W = k.table_a, TABLE_W
    half = W // 2
    with stage(nc, "h", ["held", "loaded", "split", "float", "iota", "cleared", "hot", "counted", "count_in", "ranks", "total", "offset", "offset_sb", "ended", "absent", "filled", "table"]) as s, ExitStack() as ctx:
        def sb(name, shape, dt=F32):
            return ctx.enter_context(nc.sbuf_tensor(f"h_{name}", shape, dt))
        cols = sb("cols", [D, 2, k.tiles], I32)
        parts = sb("parts", [D, 2, 2, k.tiles], I32)
        partsf = sb("partsf", [D, 2, 2, k.tiles])
        row_no = sb("row_no", [D, W], I32)
        row_nof = sb("row_nof", [D, W], mybir.dt.int16)
        hot_a = sb("hot_a", [D, 2, 2, A], BF16)
        hot_w = sb("hot_w", [D, 2, 2, W], BF16)
        zero = sb("zero", [D, half], BF16)
        count = sb("count", [A, W])
        upto = sb("upto", [A, W])
        ones_w = sb("ones_w", [A, W])
        offset = sb("offset", [A, 1])
        absent = sb("absent", [A, W])
        table = sb("table", [A, W, 4], I32)
        ps = [[ctx.enter_context(nc.psum_tensor(f"h_ps{g}{h}", [D, half], F32)) for h in (0, 1)] for g in (0, 1)]
        ps_off = ctx.enter_context(nc.psum_tensor("h_off", [D, 1], F32))
        block = ctx.enter_context(nc.Block())

        @block.sync
        def _(sp):
            sp.dma_start(cols[:, 0], k.args["src_hist"]).then_inc(s["loaded"], 16)
            sp.dma_start(cols[:, 1], k.args["dst_cols"]).then_inc(s["loaded"], 16)
            sp.dma_start(k.src_ix[:], k.args["src_cols"]).then_inc(s["loaded"], 16)
            sp.dma_start(k.dst_ix[:], k.args["dst_gather"]).then_inc(s["loaded"], 16)
            sp.wait_ge(s["filled"], 4)
            sp.dma_start(k.table.rearrange("(a w) f -> a (w f)", a=A), table[:].rearrange("a w f -> a (w f)")).then_inc(s["table"], 16)
            sp.wait_ge(s["table"], 16)
            sp.wait_ge(s["loaded"], 64)

        @block.gpsimd
        def _(pool):
            pool.iota(row_no[:], [[1, W]], base=0, channel_multiplier=0).then_inc(s["iota"], 1)

        @block.vector
        def _(dve):
            dve.memset(zero[:], 0.0).then_inc(s["cleared"], 1)
            dve.memset(ones_w[:], 1.0)
            dve.wait_ge(s["iota"], 1)
            dve.tensor_copy(row_nof[:], row_no[:]).then_inc(s["iota"], 1)
            dve.wait_ge(s["loaded"], 64)
            dve.tensor_scalar(parts[:, 0], cols[:], W.bit_length() - 1, None, ALU.logical_shift_right).then_inc(s["split"], 1)
            dve.tensor_scalar(parts[:, 1], cols[:], W - 1, None, ALU.bitwise_and).then_inc(s["split"], 1)
            dve.wait_ge(s["split"], 2)
            dve.tensor_copy(partsf[:], parts[:]).then_inc(s["float"], 1)
            dve.wait_ge(s["iota"], 2)
            dve.wait_ge(s["float"], 1)
            with dve.Fori(0, k.tiles // 2) as i:
                for b in (0, 1):
                    for g in (0, 1):
                        if g == 0:
                            dve.wait_ge(s["counted"], 2 * i + b + 1)
                        a_col = partsf[:, 0, g, bass.ds(2 * i + b, 1)]
                        w_col = partsf[:, 1, g, bass.ds(2 * i + b, 1)]
                        dve.tensor_scalar(hot_a[:, b, g], row_nof[:, 0:A], a_col, None, ALU.is_equal)
                        last = dve.tensor_scalar(hot_w[:, b, g], row_nof[:], w_col, None, ALU.is_equal)
                    last.then_inc(s["hot"], 1)
            dve.wait_ge(s["counted"], k.tiles + 2)
            for h in (0, 1):
                dve.tensor_copy(count[:, h * half:(h + 1) * half], ps[1][h][0:A, :]).then_inc(s["count_in"], 1)
                dve.tensor_copy(table[:, h * half:(h + 1) * half, 2], ps[0][h][0:A, :]).then_inc(s["filled"], 1)
            dve.wait_ge(s["count_in"], 2)
            dve.tensor_tensor_scan(upto[:], ones_w[:], count[:], 0.0, ALU.mult, ALU.add).then_inc(s["ranks"], 1)
            dve.wait_ge(s["offset"], 1)
            dve.tensor_copy(offset[:], ps_off[0:A, :]).then_inc(s["offset_sb"], 1)
            dve.tensor_scalar(absent[:], count[:], 0.0, float(NO_NODE), ALU.is_equal, ALU.mult).then_inc(s["absent"], 1)
            dve.wait_ge(s["offset_sb"], 1)
            dve.tensor_scalar(ones_w[:], upto[:], offset[:, 0:1], -1.0, ALU.add, ALU.add).then_inc(s["ended"], 1)
            dve.wait_ge(s["ended"], 1)
            dve.wait_ge(s["absent"], 1)
            dve.tensor_tensor(upto[:], ones_w[:], absent[:], ALU.add).then_inc(s["ended"], 1)
            dve.wait_ge(s["ended"], 2)
            dve.tensor_copy(table[:, :, 1], upto[:]).then_inc(s["filled"], 1)
            dve.tensor_copy(table[:, :, 3], upto[:])
            dve.tensor_tensor(absent[:], upto[:], count[:], ALU.subtract).then_inc(s["ended"], 1)
            dve.wait_ge(s["ended"], 3)
            dve.tensor_scalar(table[:, :, 0], absent[:], 1.0, None, ALU.add).then_inc(s["filled"], 1)

        @block.tensor
        def _(pe):
            pe.wait_ge(s["cleared"], 1)
            for g in (0, 1):
                for h in (0, 1):
                    last = pe.matmul(ps[g][h][:], zero[:, 0:D], zero[:], start=True, stop=False, skip_group_check=True)
            last.then_inc(s["counted"], 2)
            with pe.Fori(0, k.tiles // 2) as i:
                for b in (0, 1):
                    pe.wait_ge(s["hot"], 2 * i + b + 1)
                    for g in (0, 1):
                        for h in (0, 1):
                            last = pe.matmul(ps[g][h][0:A, :], hot_a[:, b, g], hot_w[:, b, g, h * half:(h + 1) * half],
                                             start=False, stop=False, skip_group_check=True)
                    last.then_inc(s["counted"], 1)
            pe.wait_ge(s["ranks"], 1)
            pe.matmul(ps_off[0:A, :], k.c["strict_upper"][0:A, 0:A], upto[:, W - 1:W], start=True, stop=True).then_inc(s["offset"], 1)

    with stage(nc, "m", ["held", "same", "counted", "degree", "loaded_ix", "skip", "start"], ["loaded"]) as s, ExitStack() as ctx:
        def sb(name, shape, dt=F32):
            return ctx.enter_context(nc.sbuf_tensor(f"m_{name}", shape, dt))
        dst = sb("dst", [D, 2, CH + 1], I32)
        count = sb("count", [D, 2, CH])
        one = sb("one", [D, CH])
        nxt = sb("nxt", [D, 2, k.tiles], I32)
        skip = sb("skip", [D, k.tiles], I32)
        ps = ctx.enter_context(nc.psum_tensor("m_ps", [D, k.tiles], F32))
        dst_ext = k.args["dst_ext"]
        block = ctx.enter_context(nc.Block())

        @block.sync
        def _(sp):
            def load(i, b):
                src = dst_ext[bass.ds((2 * i + b) * CH, CH + 1)] if not isinstance(i, int) else dst_ext[(2 * i + b) * CH:(2 * i + b + 1) * CH + 1]
                sp.dma_start(dst[:, b], src.partition_broadcast(D)).then_inc(s["loaded"][b], 16)
            sp.dma_start(nxt[:, 0], k.args["dst_cols"]).then_inc(s["loaded_ix"], 16)
            sp.dma_start(nxt[:, 1], k.args["dst_next"]).then_inc(s["loaded_ix"], 16)
            for b in (0, 1):
                load(0, b)
            with sp.Fori(0, k.pairs - 1) as i:
                for b in (0, 1):
                    hold(sp, s, s["same"], 2 * i + b + 1)
                    load(i + 1, b)

        @block.vector
        def _(dve):
            dve.memset(one[:], 1.0).then_inc(s["start"], 1)
            dve.memset(count[:, 1, CH - 1:CH], 0.0).then_inc(s["start"], 1)
            dve.memset(k.same[:, k.slots:], 0.0)
            dve.wait_ge(s["start"], 2)
            with dve.Fori(0, k.pairs) as i:
                for b in (0, 1):
                    c = 2 * i + b
                    dve.wait_ge(s["loaded"][b], 16 * (i + 1))
                    dve.tensor_tensor(k.same[:, bass.ds(c * CH, CH)], dst[:, b, 1:], dst[:, b, 0:CH], ALU.is_equal).then_inc(s["same"], 1)
                    dve.wait_ge(s["same"], c + 1)
                    if b == 0:
                        dve.wait_ge(s["degree"], 2 * i + 1)
                    else:
                        dve.wait_ge(s["degree"], 2 * i + 2)
                    dve.tensor_tensor_scan(count[:, b], k.same[:, bass.ds(c * CH, CH)], one[:], count[:, 1 - b, CH - 1:CH],
                                           ALU.mult, ALU.add).then_inc(s["counted"], 1)
                    dve.wait_ge(s["counted"], c + 1)
            dve.wait_ge(s["loaded_ix"], 32)
            dve.tensor_tensor(skip[:], nxt[:, 0], nxt[:, 1], ALU.is_equal).then_inc(s["skip"], 1)
            dve.wait_ge(s["skip"], 1)
            dve.scalar_tensor_tensor(k.out_ix[:], skip[:], float(NO_NODE), nxt[:, 0], ALU.mult, ALU.add)
            dve.wait_ge(s["degree"], 2 * k.pairs + 2)
            dve.tensor_copy(k.in_norm[:], ps[:])

        @block.tensor
        def _(pe):
            pe.sem_inc(s["degree"], 2)
            with pe.Fori(0, k.pairs) as i:
                for b in (0, 1):
                    c = 2 * i + b
                    pe.wait_ge(s["counted"], c + 1)
                    for t in range(T):
                        last = pe.matmul(ps[:, bass.ds(c * T + t, 1)], count[:, b, t * D:(t + 1) * D], k.c["first_row"][:],
                                         start=True, stop=True, skip_group_check=True)
                    last.then_inc(s["degree"], 1)

    with stage(nc, "g", ["held", "index", "split", "loaded", "atleast", "power", "half"], ["gathered"]) as s, ExitStack() as ctx:
        def sb(name, shape, dt=F32):
            return ctx.enter_context(nc.sbuf_tensor(f"g_{name}", shape, dt))
        index = sb("index", [D, 2, T], I32)
        found = sb("found", [D, 2, T, 4], I32)
        degree = sb("degree", [D, k.tiles])
        bounded = sb("bounded", [D, 2, k.tiles])
        power = sb("power", [D, k.tiles])
        neg_half = sb("neg_half", [D, k.tiles])
        weight = sb("weight", [D, k.tiles])
        block = ctx.enter_context(nc.Block())

        @block.sync
        def _(sp):
            sp.dma_start(weight[:], k.args["weight_cols"]).then_inc(s["loaded"], 16)

        @block.gpsimd
        def _(pool):
            def gather(i, b):
                c = 2 * i + b
                pool.tensor_copy(index[:, b], k.src_ix[:, bass.ds(c * T, T)]).then_inc(s["index"], 1)
                hold(pool, s, s["index"], c + 1)
                for t in range(T):
                    pool.indirect_dma_start(out=found[:, b, t], out_offset=None, in_=k.table,
                                            in_offset=bass.IndirectOffsetOnAxis(ap=index[:, b, t:t + 1], axis=0),
                                            bounds_check=k.table_a * TABLE_W - 1, oob_is_err=False).then_inc(s["gathered"][b], 16)
            for b in (0, 1):
                gather(0, b)
            with pool.Fori(0, k.pairs - 1) as i:
                for b in (0, 1):
                    hold(pool, s, s["split"], 2 * i + b + 1)
                    gather(i + 1, b)
            pool.wait_ge(s["atleast"], 2)
            pool.tensor_tensor(power[:], bounded[:, 0], neg_half[:], ALU.pow).then_inc(s["power"], 1)
            pool.tensor_tensor(k.in_norm[:], bounded[:, 1], neg_half[:], ALU.pow).then_inc(s["power"], 1)

        @block.vector
        def _(dve):
            dve.memset(neg_half[:], -0.5).then_inc(s["atleast"], 1)
            dve.tensor_scalar(bounded[:, 1], k.in_norm[:], 1.0, None, ALU.max)
            with dve.Fori(0, k.pairs) as i:
                for b in (0, 1):
                    at = bass.ds((2 * i + b) * T, T)
                    dve.wait_ge(s["gathered"][b], 16 * T * (i + 1))
                    dve.tensor_copy(k.first_ix[:, at], found[:, b, :, 0])
                    dve.tensor_copy(k.last_ix[:, at], found[:, b, :, 1])
                    dve.tensor_copy(degree[:, at], found[:, b, :, 2]).then_inc(s["split"], 1)
            dve.wait_ge(s["split"], 2 * k.pairs)
            dve.tensor_scalar(bounded[:, 0], degree[:], 1.0, None, ALU.max).then_inc(s["atleast"], 1)
            dve.wait_ge(s["loaded"], 16)
            dve.wait_ge(s["power"], 2)
            dve.tensor_tensor(k.edge_scale[:], weight[:], power[:], ALU.mult)


def moments(dve, s, z, stats, mv, n):
    for t in range(T):
        last = dve.bn_stats(stats[:, t], z[:, t])
    last.then_inc(s["stats_ready"], 1)
    hold(dve, s, s["stats_ready"], n + 1)
    for t in range(T):
        last = dve.bn_aggr(mv[:, t], stats[:, t])
    last.then_inc(s["moments_ready"], 1)


def rstd(pool, s, k, P, mv, var_eps, r, n, quarter=False):
    hold(pool, s, s["moments_ready"], n + 1)
    if quarter:
        pool.tensor_scalar(var_eps, mv[:, :, 1], EPS, 0.25, ALU.add, ALU.mult).then_inc(s["var_eps_ready"], 1)
    else:
        pool.tensor_scalar(var_eps, mv[:, :, 1], EPS, None, ALU.add).then_inc(s["var_eps_ready"], 1)
    hold(pool, s, s["var_eps_ready"], n + 1)
    pool.tensor_tensor(r, var_eps, k.neg_half[0:r.shape[0]], ALU.pow).then_inc(s["rstd_ready"], 1)


def normalise(dve, out, z, mv, r):
    for t in range(T):
        last = dve.tensor_scalar(out[:, t], z[:, t], mv[:, t, 0:1], r[:, t:t + 1], ALU.subtract, ALU.mult)
    return last


LN = ["stats_ready", "moments_ready", "var_eps_ready", "rstd_ready"]


def wait_count(eng, sem, value):
    if not isinstance(value, int) or value > 0:
        eng.wait_ge(sem, value)


def chain_pass(k, tag, P, tiles, source, final):
    nc, c = k.nc, k.c
    keep = final is None
    norms = 3 if keep else 4
    units = tiles // UT
    half = UT // 2
    W = half * P
    stored = ["stored_x1", "stored_x2", "stored_h1", "stored_x3"] if keep else ["stored_out"]
    single = ["held", "u_ready", "t_ready", "x1_ready", "x1T_ready", "rstT_ready", "hidden_ready", "hT_ready", "z_ready",
              "x2_ready", "h1_ready", "t2_ready", "x3_ready", "out_ready"]
    per_norm = [f"{n}{m}" for m in range(norms) for n in ("stats", "joined", "squared", "variance", "root", "inverse", "scale")]
    with stage(nc, tag, single + per_norm, ["loaded"] + stored) as s, ExitStack() as ctx:
        def sb(name, shape, dt=F32):
            return ctx.enter_context(nc.sbuf_tensor(f"{tag}_{name}", shape, dt))
        names = ["x", "u", "t", "x1", "t2", "x3"] + (["x2", "h1"] if keep else ["out"])
        rows = {n: sb(n, [D, 2, UT, D]) for n in names}
        stats = sb("stats", [D, 2, norms, UT, 6])
        small = {n: sb(n, [D, 2, norms, UT]) for n in ("diff", "sum", "both", "square", "both32", "var", "sd", "r", "shift")}
        rstT, hT = sb("rstT", [D, 2, 2, W]), sb("hT", [D, 2, 2, W])
        psT = [[ctx.enter_context(nc.psum_tensor(f"{tag}_psT{b}{h}", [D, CH], F32)) for h in (0, 1)] for b in (0, 1)]
        psO = [[ctx.enter_context(nc.psum_tensor(f"{tag}_psO{b}{h}", [D, CH], F32)) for h in (0, 1)] for b in (0, 1)]

        def view(ap, g):
            if keep:
                v = ap.rearrange("(g t p) f -> g p t f", p=P, t=UT)
            else:
                v = ap.rearrange("(g p t) f -> g p t f", p=P, t=UT)
            return v[bass.ds(g, 1)].rearrange("a p t f -> (a p) t f")

        def R(name, b):
            return rows[name][0:P, b]

        def V(name, n, b):
            return small[name][0:P, b, n]

        def per_row(ap):
            return ap[0:P, 0:D].unsqueeze(1).to_broadcast([P, UT, D])

        def z_tile(b, t):
            return psO[b][t // half][0:P, (t % half) * D:(t % half + 1) * D]

        def turns(engine, turn):
            pairs, odd = units // 2, units % 2
            turn(0, (0, 1), ())
            turn(1, (0, 1), (0, 1))
            with engine.Fori(2, pairs) as i:
                turn(i, (0, 1), (0, 1))
            if odd:
                turn(pairs, (0,), (0, 1))
                turn(pairs + 1, (), (0,))
            else:
                turn(pairs, (), (0, 1))
        block = ctx.enter_context(nc.Block())

        @block.sync
        def _(sp):
            def load(i, b):
                sp.dma_start(R("x", b), view(source, 2 * i + b)).then_inc(s["loaded"][b], 16)

            def store(i, b, ready, name, sem, to):
                hold(sp, s, s[ready], 2 * i + b + 1)
                sp.dma_start(view(to, 2 * i + b), R(name, b)).then_inc(s[sem][b], 16)
            pairs, odd = units // 2, units % 2

            def turn(i, front, back, more=(0, 1)):
                for b in more:
                    hold(sp, s, s["t_ready"], 2 * i + b + 1)
                    load(i + 1, b)
                if keep:
                    for b in back:
                        store(i - 1, b, "x2_ready", "x2", "stored_x2", k.s[2])
                        store(i - 1, b, "h1_ready", "h1", "stored_h1", k.sh)
                    for b in front:
                        store(i, b, "x1_ready", "x1", "stored_x1", k.s[1])
                for b in back:
                    if keep:
                        store(i - 1, b, "x3_ready", "x3", "stored_x3", k.s[3])
                    else:
                        store(i - 1, b, "out_ready", "out", "stored_out", final)
            for b in (0, 1):
                load(0, b)
            turn(0, (0, 1), ())
            with sp.Fori(1, pairs - 1) as i:
                turn(i, (0, 1), (0, 1))
            turn(pairs - 1, (0, 1), (0, 1), more=(0,) if odd else ())
            if odd:
                turn(pairs, (0,), (0, 1), more=())
                turn(pairs + 1, (), (0,), more=())
            else:
                turn(pairs, (), (0, 1), more=())
            for n in stored:
                sp.wait_ge(s[n][0], 16 * (pairs + odd))
                sp.wait_ge(s[n][1], 16 * pairs)

        @block.vector
        def _(dve):
            def statistics(j, b, n, tile):
                for t in range(UT):
                    last = dve.bn_stats(stats[0:P, b, n, t], tile(t))
                last.then_inc(s[f"stats{n}"], 1)

            def inverse(j, b, n, shift):
                dve.wait_ge(s[f"root{n}"], 2 * j + b + 1)
                dve.reciprocal(V("r", n, b), V("sd", n, b)).then_inc(s[f"inverse{n}"], 1)
                dve.wait_ge(s[f"inverse{n}"], 2 * j + b + 1)
                if shift:
                    dve.scalar_tensor_tensor(V("shift", n, b), V("sum", n, b), -0.5, V("r", n, b), ALU.mult, ALU.mult).then_inc(s[f"scale{n}"], 1)

            def turn(i, front, back):
                j = i - 1
                for b in front:
                    dve.wait_ge(s["u_ready"], 2 * i + b + 1)
                    wait_count(dve, s["x1_ready"], 2 * j + b + 1)
                    dve.scalar_tensor_tensor(R("t", b), R("u", b), 0.0, R("x", b), ALU.max, ALU.add).then_inc(s["t_ready"], 1)
                    dve.wait_ge(s["t_ready"], 2 * i + b + 1)
                    statistics(i, b, 0, lambda t: rows["t"][0:P, b, t])
                for b in back:
                    dve.wait_ge(s["z_ready"], 2 * j + b + 1)
                    statistics(j, b, 1, lambda t: z_tile(b, t))
                for b in (0, 1):
                    if b in front:
                        inverse(i, b, 0, True)
                    if keep and b in back:
                        inverse(j, b, 1, True)
                for b in back:
                    if keep:
                        dve.wait_ge(s["x2_ready"], 2 * j + b + 1)
                        last = dve.scalar_tensor_tensor(R("t2", b), R("x2", b), 2.0, per_row(k.conv_c), ALU.mult, ALU.add)
                    else:
                        inverse(j, b, 1, False)
                        for t in range(UT):
                            last = dve.scalar_tensor_tensor(rows["t2"][0:P, b, t], z_tile(b, t), V("r", 1, b)[:, t:t + 1],
                                                            k.conv_c[0:P, 0:D], ALU.mult, ALU.add)
                    last.then_inc(s["t2_ready"], 1)
                    dve.wait_ge(s["t2_ready"], 2 * j + b + 1)
                    statistics(j, b, 2, lambda t: rows["t2"][0:P, b, t])
                for b in back:
                    inverse(j, b, 2, keep)
                    if keep:
                        continue
                    wait_count(dve, s["out_ready"], 2 * (j - 1) + b + 1)
                    for t in range(UT):
                        last = dve.scalar_tensor_tensor(rows["x3"][0:P, b, t], rows["t2"][0:P, b, t], V("r", 2, b)[:, t:t + 1],
                                                        k.elu_c[0:P, 0:D], ALU.mult, ALU.add)
                    last.then_inc(s["x3_ready"], 1)
                    dve.wait_ge(s["x3_ready"], 2 * j + b + 1)
                    statistics(j, b, 3, lambda t: rows["x3"][0:P, b, t])
                if not keep:
                    for b in back:
                        inverse(j, b, 3, True)
            turns(dve, turn)

        @block.gpsimd
        def _(pool):
            def add_bias(i, b):
                hold(pool, s, s["loaded"][b], 16 * (i + 1))
                if not isinstance(i, int) or i > 0:
                    hold(pool, s, s["t_ready"], 2 * (i - 1) + b + 1)
                pool.tensor_tensor(R("u", b), R("x", b), per_row(c["b_p"]), ALU.add).then_inc(s["u_ready"], 1)

            def variance(j, b, n, need_sum):
                st = stats[0:P, b, n]
                at = 2 * j + b + 1
                hold(pool, s, s[f"stats{n}"], at)
                if need_sum:
                    pool.tensor_tensor(V("sum", n, b), st[:, :, 1], st[:, :, 4], ALU.add)
                pool.tensor_tensor(V("diff", n, b), st[:, :, 1], st[:, :, 4], ALU.subtract)
                pool.tensor_tensor(V("both", n, b), st[:, :, 2], st[:, :, 5], ALU.add).then_inc(s[f"joined{n}"], 1)
                hold(pool, s, s[f"joined{n}"], at)
                pool.tensor_tensor(V("square", n, b), V("diff", n, b), V("diff", n, b), ALU.mult)
                pool.tensor_scalar(V("both32", n, b), V("both", n, b), 1.0 / 32, None, ALU.mult).then_inc(s[f"squared{n}"], 1)
                hold(pool, s, s[f"squared{n}"], at)
                pool.tensor_tensor(V("var", n, b), V("square", n, b), V("both32", n, b), ALU.add).then_inc(s[f"variance{n}"], 1)

            def turn(i, front, back, more=(0, 1)):
                j = i - 1
                for b in front:
                    variance(i, b, 0, True)
                for b in back:
                    variance(j, b, 1, keep)
                for b in (0, 1):
                    if b in more:
                        add_bias(i + 1, b)
                    if b in back:
                        if keep:
                            hold(pool, s, s["x2_ready"], 2 * j + b + 1)
                            if not isinstance(j, int) or j > 0:
                                hold(pool, s, s["stored_h1"][b], 16 * j)
                            pool.tensor_tensor(R("h1", b), R("x2", b), per_row(k.conv_c1), ALU.add).then_inc(s["h1_ready"], 1)
                        variance(j, b, 2, keep)
                if not keep:
                    for b in back:
                        variance(j, b, 3, True)
            pairs, odd = units // 2, units % 2
            for b in (0, 1):
                add_bias(0, b)
            turn(0, (0, 1), ())
            turn(1, (0, 1), (0, 1))
            with pool.Fori(2, pairs - 1) as i:
                turn(i, (0, 1), (0, 1))
            turn(pairs - 1, (0, 1), (0, 1), more=(0,) if odd else ())
            if odd:
                turn(pairs, (0,), (0, 1), more=())
                turn(pairs + 1, (), (0,), more=())
            else:
                turn(pairs, (), (0, 1), more=())

        @block.scalar
        def _(act):
            def root(j, b, n):
                act.wait_ge(s[f"variance{n}"], 2 * j + b + 1)
                halved = n == 1 and not keep
                act.activation(V("sd", n, b), V("var", n, b), ACT.Sqrt, bias=(k.eps_quarter if halved else k.eps_ln)[0:P, 0:1],
                               scale=1.0 / 16 if halved else 0.25).then_inc(s[f"root{n}"], 1)

            def apply(j, b, n, name, tile, ready):
                act.wait_ge(s[f"scale{n}"], 2 * j + b + 1)
                for t in range(UT):
                    last = act.activation(rows[name][0:P, b, t], tile(t), ACT.Identity, bias=V("shift", n, b)[:, t:t + 1],
                                          scale=V("r", n, b)[:, t:t + 1])
                last.then_inc(s[ready], 1)

            def turn(i, front, back):
                j = i - 1
                for b in front:
                    root(i, b, 0)
                for b in back:
                    root(j, b, 1)
                for b in (0, 1):
                    if b in front:
                        wait_count(act, s["z_ready"], 2 * j + b + 1)
                        if keep:
                            wait_count(act, s["stored_x1"][b], 16 * i)
                        apply(i, b, 0, "x1", lambda t: rows["t"][0:P, b, t], "x1_ready")
                    if keep and b in back:
                        wait_count(act, s["stored_x2"][b], 16 * j)
                        wait_count(act, s["t2_ready"], 2 * (j - 1) + b + 1)
                        wait_count(act, s["h1_ready"], 2 * (j - 1) + b + 1)
                        apply(j, b, 1, "x2", lambda t: z_tile(b, t), "x2_ready")
                for b in (0, 1):
                    if b in front:
                        act.wait_ge(s["x1T_ready"], 2 * i + b + 1)
                        for h in (0, 1):
                            last = act.activation(rstT[:, b, h], psT[b][h][:, 0:W], ACT.Copy, scale=k.one_eps[:, 0:1])
                        last.then_inc(s["rstT_ready"], 1)
                    if b in back:
                        root(j, b, 2)
                for b in (0, 1):
                    if b in front:
                        act.wait_ge(s["hidden_ready"], 2 * i + b + 1)
                        for h in (0, 1):
                            last = act.activation(hT[:, b, h], psT[b][h][:, 0:W], ACT.Relu, bias=c["b_1"][:, 0:1])
                        last.then_inc(s["hT_ready"], 1)
                    if b in back and not keep:
                        root(j, b, 3)
                for b in back:
                    if keep:
                        wait_count(act, s["stored_x3"][b], 16 * j)
                        apply(j, b, 2, "x3", lambda t: rows["t2"][0:P, b, t], "x3_ready")
                    else:
                        wait_count(act, s["stored_out"][b], 16 * j)
                        apply(j, b, 3, "out", lambda t: rows["x3"][0:P, b, t], "out_ready")
            turns(act, turn)

        @block.tensor
        def _(pe):
            def turn(i, front, back):
                j = i - 1
                for b in front:
                    pe.wait_ge(s["x1_ready"], 2 * i + b + 1)
                    for t in range(UT):
                        last = pe.transpose(psT[b][t // half][:, (t % half) * P:(t % half + 1) * P], rows["x1"][0:P, b, t], c["identity"][0:P, 0:P])
                    last.then_inc(s["x1T_ready"], 1)
                for b in front:
                    pe.wait_ge(s["rstT_ready"], 2 * i + b + 1)
                    for h in (0, 1):
                        last = pe.matmul(psT[b][h][:, 0:W], c["L1_gnn_W1"][:], rstT[:, b, h], start=True, stop=True)
                    last.then_inc(s["hidden_ready"], 1)
                for b in front:
                    wait_count(pe, s["x2_ready" if keep else "t2_ready"], 2 * j + b + 1)
                    for h in (0, 1):
                        pe.matmul(psO[b][h][0:P], c["ones"][0:1, 0:P], c["b_2"][0:1, :], start=True, stop=False, skip_group_check=True)
                        pe.matmul(psO[b][h][0:P], c["identity"][0:P, 0:P], rows["x1"][0:P, b, h * half:(h + 1) * half].rearrange("p t f -> p (t f)"),
                                  start=False, stop=False, skip_group_check=True)
                    pe.wait_ge(s["hT_ready"], 2 * i + b + 1)
                    for t in range(UT):
                        last = pe.matmul(z_tile(b, t), hT[:, b, t // half, (t % half) * P:(t % half + 1) * P], c["L1_gnn_W2"][:],
                                         start=False, stop=(t % half == half - 1), skip_group_check=True)
                    last.then_inc(s["z_ready"], 1)
            turns(pe, turn)


def gather_rows(pool, s, index, ix, rows, table, last_row, c, b, done):
    pool.tensor_copy(index[:, b], ix[:, bass.ds(c * T, T)]).then_inc(s["index_ready"], 1)
    hold(pool, s, s["index_ready"], c + 1)
    for t in range(T):
        pool.indirect_dma_start(out=rows[:, b, t], out_offset=None, in_=table,
                                in_offset=bass.IndirectOffsetOnAxis(ap=index[:, b, t:t + 1], axis=0),
                                bounds_check=last_row, oob_is_err=False).then_inc(done, 16)


def attention0_scores(k):
    nc, c = k.nc, k.c
    pairs = k.pairs
    single = ["held", "index_ready", "index_d_ready", "rowsT_ready", "srcT_ready", "dstT_ready", "query_ready", "product_ready",
              "score_ready", "score_sb_ready", "low_ready", "max_ready", "start"]
    with stage(nc, "a0", single, ["gathered", "stored_rows", "stored_T"]) as s, ExitStack() as ctx:
        def sb(name, shape, dt=F32):
            return ctx.enter_context(nc.sbuf_tensor(f"a0_{name}", shape, dt))

        def bank(name):
            return [ctx.enter_context(nc.psum_tensor(f"a0_{name}{b}", [D, CH], F32)) for b in (0, 1)]
        index = sb("index", [D, 2, T], I32)
        index_d = sb("index_d", [D, 2, T], I32)
        src, dst = sb("src", [D, 2, T, D]), sb("dst", [D, 2, T, D])
        srcT, dstT = sb("srcT", [D, 2, CH]), sb("dstT", [D, 2, CH])
        product, score = sb("product", [D, 2, CH]), sb("score", [D, 2, CH])
        low, top = sb("low", [D, 2, CH]), sb("top", [D, 2, CH])
        psS, psD, psQ, psC = bank("psS"), bank("psD"), bank("psQ"), bank("psC")
        block = ctx.enter_context(nc.Block())

        @block.gpsimd
        def _(pool):
            def gather(i, b):
                n = 2 * i + b
                gather_rows(pool, s, index, k.src_ix, src, k.args["x"], k.n_nodes - 1, n, b, s["gathered"][b])
                pool.tensor_copy(index_d[:, b], k.dst_ix[:, bass.ds(n * T, T)]).then_inc(s["index_d_ready"], 1)
                hold(pool, s, s["index_d_ready"], n + 1)
                for t in range(T):
                    pool.indirect_dma_start(out=dst[:, b, t], out_offset=None, in_=k.args["x"],
                                            in_offset=bass.IndirectOffsetOnAxis(ap=index_d[:, b, t:t + 1], axis=0),
                                            bounds_check=k.n_nodes - 1, oob_is_err=False).then_inc(s["gathered"][b], 16)
            for b in (0, 1):
                gather(0, b)
            with pool.Fori(0, pairs - 1) as i:
                for b in (0, 1):
                    hold(pool, s, s["rowsT_ready"], 2 * i + b + 1)
                    hold(pool, s, s["stored_rows"][b], 32 * (i + 1))
                    gather(i + 1, b)

        @block.sync
        def _(sp):
            with sp.Fori(0, pairs) as i:
                for b in (0, 1):
                    n = 2 * i + b
                    hold(sp, s, s["gathered"][b], 32 * T * (i + 1))
                    sp.dma_start(chunk(k.s[0], n), src[:, b]).then_inc(s["stored_rows"][b], 16)
                    sp.dma_start(chunk(k.d[0], n), dst[:, b]).then_inc(s["stored_rows"][b], 16)
                for b in (0, 1):
                    n = 2 * i + b
                    hold(sp, s, s["srcT_ready"], n + 1)
                    sp.dma_start(columns(k.val_t, n), srcT[:, b]).then_inc(s["stored_T"][b], 16)
                    hold(sp, s, s["score_sb_ready"], n + 1)
                    sp.dma_start(columns(k.score_t, n), score[:, b]).then_inc(s["stored_T"][b], 16)
                    hold(sp, s, s["max_ready"], n + 1)
                    sp.dma_start(columns(k.max_t, n), top[:, b]).then_inc(s["stored_T"][b], 16)
            for b in (0, 1):
                sp.wait_ge(s["stored_rows"][b], 32 * pairs)
                sp.wait_ge(s["stored_T"][b], 48 * (pairs + 1))

        @block.tensor
        def _(pe):
            with pe.Fori(0, pairs) as i:
                for b in (0, 1):
                    pe.wait_ge(s["gathered"][b], 32 * T * (i + 1))
                    for t in range(T):
                        pe.transpose(psS[b][:, t * D:(t + 1) * D], src[:, b, t], c["identity"][:])
                        last = pe.transpose(psD[b][:, t * D:(t + 1) * D], dst[:, b, t], c["identity"][:])
                    last.then_inc(s["rowsT_ready"], 1)
                for b in (0, 1):
                    pe.wait_ge(s["dstT_ready"], 2 * i + b + 1)
                    pe.matmul(psQ[b][:], k.att0[:], dstT[:, b], start=True, stop=True).then_inc(s["query_ready"], 1)
                for b in (0, 1):
                    pe.wait_ge(s["product_ready"], 2 * i + b + 1)
                    pe.matmul(psC[b][:], c["score_block"][:], product[:, b], start=True, stop=True).then_inc(s["score_ready"], 1)

        @block.scalar
        def _(act):
            for b in (0, 1):
                act.sem_inc(s["stored_T"][b], 48)
            with act.Fori(0, pairs) as i:
                for b in (0, 1):
                    act.wait_ge(s["rowsT_ready"], 2 * i + b + 1)
                    act.activation(dstT[:, b], psD[b][:], ACT.Copy).then_inc(s["dstT_ready"], 1)
                    act.wait_ge(s["stored_T"][b], 48 * (i + 1))
                    act.activation(srcT[:, b], psS[b][:], ACT.Copy).then_inc(s["srcT_ready"], 1)
                for b in (0, 1):
                    act.wait_ge(s["score_ready"], 2 * i + b + 1)
                    act.activation(score[:, b], psC[b][:], ACT.Copy).then_inc(s["score_sb_ready"], 1)

        @block.vector
        def _(dve):
            dve.memset(top[:, 1, CH - 1:CH], 0.0).then_inc(s["start"], 1)
            dve.wait_ge(s["start"], 1)
            with dve.Fori(0, pairs) as i:
                for b in (0, 1):
                    dve.tensor_scalar(low[:, b], k.same[:, bass.ds((2 * i + b) * CH, CH)], -1.0, -LOW, ALU.add, ALU.mult).then_inc(s["low_ready"], 1)
                    dve.wait_ge(s["query_ready"], 2 * i + b + 1)
                    dve.wait_ge(s["srcT_ready"], 2 * i + b + 1)
                    dve.tensor_tensor(product[:, b], psQ[b][:], srcT[:, b], ALU.mult).then_inc(s["product_ready"], 1)
                for b in (0, 1):
                    dve.wait_ge(s["low_ready"], 2 * i + b + 1)
                    dve.wait_ge(s["stored_T"][b], 48 * (i + 1))
                    dve.wait_ge(s["score_sb_ready"], 2 * i + b + 1)
                    if b == 1:
                        dve.wait_ge(s["max_ready"], 2 * i + 1)
                    dve.tensor_tensor_scan(top[:, b], low[:, b], score[:, b], top[:, 1 - b, CH - 1:CH], ALU.add, ALU.max).then_inc(s["max_ready"], 1)
                dve.wait_ge(s["max_ready"], 2 * i + 2)


def attention0_sum(k):
    nc, c = k.nc, k.c
    pairs = k.pairs
    single = ["held", "start", "mask_ready", "lastmax_ready", "maxheld_ready", "shifted_ready", "clipped_ready", "exp_ready", "weighted_ready",
              "den_ready", "num_ready", "agg_ready", "denb_ready", "rden_ready", "biased_ready", "scaled_ready", "u_ready",
              "t_ready", "x1_ready"] + LN
    with stage(nc, "b0", single, ["loaded", "stored"]) as s, ExitStack() as ctx:
        def sb(name, shape, dt=F32):
            return ctx.enter_context(nc.sbuf_tensor(f"b0_{name}", shape, dt))

        def bank(name, n=CH):
            return [ctx.enter_context(nc.psum_tensor(f"b0_{name}{b}", [D, n], F32)) for b in (0, 1)]
        valT, score, top, x = sb("valT", [D, 2, CH]), sb("score", [D, 2, CH]), sb("top", [D, 2, CH]), sb("x", [D, 2, T, D])
        lastmax, maxheld, shifted, clipped = (sb(n, [D, 2, CH]) for n in ("lastmax", "maxheld", "shifted", "clipped"))
        expo, weighted, num, den = (sb(n, [D, 2, CH]) for n in ("expo", "weighted", "num", "den"))
        mask = sb("mask", [D, 2, CH], BF16)
        denb, rden = sb("denb", [D, 2, T]), sb("rden", [D, 2, T])
        biased, scaled, u, t_, x1 = (sb(n, [D, 2, T, D]) for n in ("biased", "scaled", "u", "t", "x1"))
        stats, mv = sb("stats", [D, 2, T, 6]), sb("mv", [D, 2, T, 2])
        var_eps, r = sb("var_eps", [D, 2, T]), sb("r", [D, 2, T])
        psA, psN = bank("psA"), bank("psN", T)
        block = ctx.enter_context(nc.Block())

        def q(i, b):
            return (2 * pairs - 1) - (2 * i + b)

        @block.sync
        def _(sp):
            def load(i, b):
                sp.dma_start(valT[:, b], columns(k.val_t, q(i, b))).then_inc(s["loaded"][b], 16)
                sp.dma_start(score[:, b], columns(k.score_t, q(i, b))).then_inc(s["loaded"][b], 16)
                sp.dma_start(top[:, b], columns(k.max_t, q(i, b))).then_inc(s["loaded"][b], 16)
                sp.dma_start(x[:, b], chunk(k.d[0], q(i, b))).then_inc(s["loaded"][b], 16)

            def body(i, more):
                for b in (0, 1):
                    if more:
                        hold(sp, s, s["t_ready"], 2 * i + b + 1)
                        load(i + 1, b)
                for b in (0, 1):
                    hold(sp, s, s["x1_ready"], 2 * i + b + 1)
                    sp.dma_start(chunk(k.d[1], q(i, b)), x1[:, b]).then_inc(s["stored"][b], 16)
            for b in (0, 1):
                load(0, b)
            with sp.Fori(0, pairs - 1) as i:
                body(i, True)
            body(pairs - 1, False)
            for b in (0, 1):
                sp.wait_ge(s["stored"][b], 16 * (pairs + 1))

        @block.scalar
        def _(act):
            def load_mask(i, b):
                act.activation(mask[:, b], k.same[:, bass.ds(q(i, b) * CH + 1, CH)], ACT.Copy).then_inc(s["mask_ready"], 1)

            def body(i, more):
                for b in (0, 1):
                    act.wait_ge(s["clipped_ready"], 2 * i + b + 1)
                    act.activation(expo[:, b], clipped[:, b], ACT.Exp).then_inc(s["exp_ready"], 1)
                for b in (0, 1):
                    if more:
                        act.wait_ge(s["num_ready"], 2 * i + b + 1)
                        load_mask(i + 1, b)
            for b in (0, 1):
                load_mask(0, b)
            with act.Fori(0, pairs - 1) as i:
                body(i, True)
            body(pairs - 1, False)

        @block.gpsimd
        def _(pool):
            with pool.Fori(0, pairs) as i:
                for b in (0, 1):
                    hold(pool, s, s["loaded"][b], 64 * (i + 1))
                    pool.tensor_tensor(flat(biased, b), flat(x, b), c["b_p"][:], ALU.add).then_inc(s["biased_ready"], 1)
                for b in (0, 1):
                    rstd(pool, s, k, D, mv[:, b], var_eps[:, b], r[:, b], 2 * i + b)

        @block.tensor
        def _(pe):
            with pe.Fori(0, pairs) as i:
                for b in (0, 1):
                    pe.wait_ge(s["den_ready"], 2 * i + b + 1)
                    for t in range(T):
                        pe.matmul(psN[b][:, t:t + 1], den[:, b, t * D:(t + 1) * D], c["first_row"][:], start=True, stop=True, skip_group_check=True)
                    pe.wait_ge(s["num_ready"], 2 * i + b + 1)
                    for t in range(T):
                        last = pe.matmul(psA[b][:, t * D:(t + 1) * D], num[:, b, t * D:(t + 1) * D], k.val0[:], start=True, stop=True, skip_group_check=True)
                    last.then_inc(s["agg_ready"], 1)

        @block.vector
        def _(dve):
            for b in (0, 1):
                dve.sem_inc(s["stored"][b], 16)
            for buf in (maxheld, num, den):
                dve.memset(buf[:, 1, 0:1], 0.0).then_inc(s["start"], 1)
            dve.wait_ge(s["start"], 3)
            with dve.Fori(0, pairs) as i:
                both = (0, 1)

                def at(b):
                    return 2 * i + b + 1

                for b in both:
                    dve.wait_ge(s["mask_ready"], at(b))
                    dve.wait_ge(s["loaded"][b], 64 * (i + 1))
                    dve.scalar_tensor_tensor(lastmax[:, b], mask[:, b], -1.0, top[:, b], ALU.add, ALU.mult).then_inc(s["lastmax_ready"], 1)
                for b in both:
                    dve.wait_ge(s["lastmax_ready"], at(b))
                    if b == 1:
                        dve.wait_ge(s["maxheld_ready"], 2 * i + 1)
                    dve.tensor_tensor_scan(maxheld[:, b, ::-1], mask[:, b, ::-1], lastmax[:, b, ::-1], maxheld[:, 1 - b, 0:1],
                                           ALU.mult, ALU.subtract).then_inc(s["maxheld_ready"], 1)
                for b in both:
                    dve.wait_ge(s["maxheld_ready"], at(b))
                    dve.tensor_tensor(shifted[:, b], score[:, b], maxheld[:, b], ALU.subtract).then_inc(s["shifted_ready"], 1)
                for b in both:
                    dve.wait_ge(s["shifted_ready"], at(b))
                    dve.tensor_scalar(clipped[:, b], shifted[:, b], -50.0, 50.0, ALU.max, ALU.min).then_inc(s["clipped_ready"], 1)
                for b in both:
                    dve.wait_ge(s["exp_ready"], at(b))
                    dve.tensor_tensor(weighted[:, b], expo[:, b], valT[:, b], ALU.mult).then_inc(s["weighted_ready"], 1)
                    if b == 1:
                        dve.wait_ge(s["den_ready"], 2 * i + 1)
                    dve.tensor_tensor_scan(den[:, b, ::-1], mask[:, b, ::-1], expo[:, b, ::-1], den[:, 1 - b, 0:1],
                                           ALU.mult, ALU.add).then_inc(s["den_ready"], 1)
                for b in both:
                    dve.wait_ge(s["weighted_ready"], at(b))
                    if b == 1:
                        dve.wait_ge(s["num_ready"], 2 * i + 1)
                    dve.tensor_tensor_scan(num[:, b, ::-1], mask[:, b, ::-1], weighted[:, b, ::-1], num[:, 1 - b, 0:1],
                                           ALU.mult, ALU.add).then_inc(s["num_ready"], 1)
                for b in both:
                    dve.wait_ge(s["agg_ready"], at(b))
                    dve.tensor_scalar(denb[:, b], psN[b][:], 1e-9, None, ALU.add).then_inc(s["denb_ready"], 1)
                    dve.wait_ge(s["denb_ready"], at(b))
                    dve.reciprocal(rden[:, b], denb[:, b]).then_inc(s["rden_ready"], 1)
                for b in both:
                    dve.wait_ge(s["rden_ready"], at(b))
                    dve.tensor_tensor(scaled[:, b], psA[b][:].rearrange("p (t f) -> p t f", t=T),
                                      rden[:, b].unsqueeze(2).to_broadcast([D, T, D]), ALU.mult).then_inc(s["scaled_ready"], 1)
                for b in both:
                    dve.wait_ge(s["scaled_ready"], at(b))
                    dve.wait_ge(s["biased_ready"], at(b))
                    dve.tensor_tensor(flat(u, b), flat(scaled, b), flat(biased, b), ALU.add).then_inc(s["u_ready"], 1)
                for b in both:
                    dve.wait_ge(s["u_ready"], at(b))
                    dve.scalar_tensor_tensor(flat(t_, b), flat(u, b), 0.0, flat(x, b), ALU.max, ALU.add).then_inc(s["t_ready"], 1)
                for b in both:
                    dve.wait_ge(s["t_ready"], at(b))
                    moments(dve, s, t_[:, b], stats[:, b], mv[:, b], 2 * i + b)
                for b in both:
                    dve.wait_ge(s["rstd_ready"], at(b))
                    dve.wait_ge(s["stored"][b], 16 * (i + 1))
                    normalise(dve, x1[:, b], t_[:, b], mv[:, b], r[:, b]).then_inc(s["x1_ready"], 1)


def edge_mlp(k):
    nc, c = k.nc, k.c
    pairs = k.pairs
    single = ["held", "start", "index_ready", "rowsT_ready", "srcT_ready", "firstrow_ready", "dstheld_ready", "message_ready",
              "relu_ready", "sum_ready", "rst_ready", "hidden_ready", "hT_ready", "z_ready", "x2_ready"] + LN
    with stage(nc, "l1", single, ["loaded_s", "loaded_d", "gathered", "stored"]) as s, ExitStack() as ctx:
        def sb(name, shape, dt=F32):
            return ctx.enter_context(nc.sbuf_tensor(f"l1_{name}", shape, dt))

        def bank(name):
            return [ctx.enter_context(nc.psum_tensor(f"l1_{name}{b}", [D, CH], F32)) for b in (0, 1)]
        index = sb("index", [D, 2, T], I32)
        src, dst, x2 = (sb(n, [D, 2, T, D]) for n in ("src", "dst", "x2"))
        srcT, firstrow, dstheld, message, neigh, rst, hT = (sb(n, [D, 2, CH]) for n in ("srcT", "firstrow", "dstheld", "message", "neigh", "rst", "hT"))
        stats, mv = sb("stats", [D, 2, T, 6]), sb("mv", [D, 2, T, 2])
        var_eps, r = sb("var_eps", [D, 2, T]), sb("r", [D, 2, T])
        psS, psD, psM, psO = bank("psS"), bank("psD"), bank("psM"), bank("psO")
        block = ctx.enter_context(nc.Block())

        @block.sync
        def _(sp):
            def load(i, b):
                sp.dma_start(src[:, b], chunk(k.s[1], 2 * i + b)).then_inc(s["loaded_s"][b], 16)
                sp.dma_start(dst[:, b], chunk(k.d[1], 2 * i + b)).then_inc(s["loaded_d"][b], 16)

            def body(i, more):
                for b in (0, 1):
                    if more:
                        hold(sp, s, s["rowsT_ready"], 2 * i + b + 1)
                        load(i + 1, b)
                for b in (0, 1):
                    hold(sp, s, s["x2_ready"], 2 * i + b + 1)
                    sp.dma_start(chunk(k.d[2], 2 * i + b), x2[:, b]).then_inc(s["stored"][b], 16)
            for b in (0, 1):
                load(0, b)
            with sp.Fori(0, pairs - 1) as i:
                body(i, True)
            body(pairs - 1, False)
            for b in (0, 1):
                sp.wait_ge(s["stored"][b], 16 * (pairs + 1))

        @block.gpsimd
        def _(pool):
            def gather(i, b):
                hold(pool, s, s["loaded_s"][b], 16 * (i + 1))
                gather_rows(pool, s, index, k.first_ix, src, k.d[1], k.slots - 1, 2 * i + b, b, s["gathered"][b])
            for b in (0, 1):
                gather(0, b)
            with pool.Fori(0, pairs - 1) as i:
                for b in (0, 1):
                    gather(i + 1, b)
                    rstd(pool, s, k, D, mv[:, b], var_eps[:, b], r[:, b], 2 * i + b)
            for b in (0, 1):
                rstd(pool, s, k, D, mv[:, b], var_eps[:, b], r[:, b], 2 * (pairs - 1) + b)

        @block.tensor
        def _(pe):
            with pe.Fori(0, pairs) as i:
                for b in (0, 1):
                    pe.wait_ge(s["gathered"][b], 16 * T * (i + 1))
                    pe.wait_ge(s["loaded_d"][b], 16 * (i + 1))
                    for t in range(T):
                        pe.transpose(psS[b][:, t * D:(t + 1) * D], src[:, b, t], c["identity"][:])
                        last = pe.transpose(psD[b][:, t * D:(t + 1) * D], dst[:, b, t], c["identity"][:])
                    last.then_inc(s["rowsT_ready"], 1)
                for b in (0, 1):
                    pe.wait_ge(s["srcT_ready"], 2 * i + b + 1)
                    pe.matmul(psM[b][:], c["L1_Wa"][:], srcT[:, b], start=True, stop=False)
                    pe.wait_ge(s["dstheld_ready"], 2 * i + b + 1)
                    pe.matmul(psM[b][:], c["L1_Wb"][:], dstheld[:, b], start=False, stop=True).then_inc(s["message_ready"], 1)
                for b in (0, 1):
                    pe.wait_ge(s["rst_ready"], 2 * i + b + 1)
                    pe.matmul(psM[b][:], c["L1_gnn_W1"][:], rst[:, b], start=True, stop=True).then_inc(s["hidden_ready"], 1)
                for b in (0, 1):
                    pe.matmul(psO[b][:], c["ones"][0:1, :], c["b_2"][0:1, :], start=True, stop=False, skip_group_check=True)
                    pe.wait_ge(s["hT_ready"], 2 * i + b + 1)
                    for t in range(T):
                        at = slice(t * D, (t + 1) * D)
                        pe.matmul(psO[b][:, at], dstheld[:, b, at], c["identity"][:], start=False, stop=False, skip_group_check=True)
                        last = pe.matmul(psO[b][:, at], hT[:, b, at], c["L1_gnn_W2"][:], start=False, stop=(t == T - 1), skip_group_check=True)
                    last.then_inc(s["z_ready"], 1)

        @block.scalar
        def _(act):
            with act.Fori(0, pairs) as i:
                for b in (0, 1):
                    act.wait_ge(s["rowsT_ready"], 2 * i + b + 1)
                    act.activation(srcT[:, b], psS[b][:], ACT.Copy).then_inc(s["srcT_ready"], 1)
                for b in (0, 1):
                    act.wait_ge(s["message_ready"], 2 * i + b + 1)
                    act.activation(message[:, b], psM[b][:], ACT.Relu, bias=c["b_edge"][:, 0:1]).then_inc(s["relu_ready"], 1)
                for b in (0, 1):
                    act.wait_ge(s["hidden_ready"], 2 * i + b + 1)
                    act.activation(hT[:, b], psM[b][:], ACT.Relu, bias=c["b_1"][:, 0:1]).then_inc(s["hT_ready"], 1)

        @block.vector
        def _(dve):
            for b in (0, 1):
                dve.sem_inc(s["stored"][b], 16)
            for buf in (dstheld, neigh):
                dve.memset(buf[:, 1, CH - 1:CH], 0.0).then_inc(s["start"], 1)
            dve.wait_ge(s["start"], 2)
            with dve.Fori(0, pairs) as i:
                both = (0, 1)

                def at(b):
                    return 2 * i + b + 1

                def same(b):
                    return k.same[:, bass.ds((2 * i + b) * CH, CH)]
                for b in both:
                    dve.wait_ge(s["rowsT_ready"], at(b))
                    dve.scalar_tensor_tensor(firstrow[:, b], same(b), -1.0, psD[b][:], ALU.add, ALU.mult).then_inc(s["firstrow_ready"], 1)
                for b in both:
                    dve.wait_ge(s["firstrow_ready"], at(b))
                    if b == 1:
                        dve.wait_ge(s["dstheld_ready"], 2 * i + 1)
                    dve.tensor_tensor_scan(dstheld[:, b], same(b), firstrow[:, b], dstheld[:, 1 - b, CH - 1:CH], ALU.mult, ALU.subtract).then_inc(s["dstheld_ready"], 1)
                for b in both:
                    dve.wait_ge(s["relu_ready"], at(b))
                    if b == 1:
                        dve.wait_ge(s["sum_ready"], 2 * i + 1)
                    dve.tensor_tensor_scan(neigh[:, b], same(b), message[:, b], neigh[:, 1 - b, CH - 1:CH], ALU.mult, ALU.add).then_inc(s["sum_ready"], 1)
                for b in both:
                    dve.wait_ge(s["sum_ready"], at(b))
                    dve.scalar_tensor_tensor(rst[:, b], dstheld[:, b], k.one_eps[:, 0:1], neigh[:, b], ALU.mult, ALU.add).then_inc(s["rst_ready"], 1)
                for b in both:
                    z = psO[b][:].rearrange("p (t f) -> p t f", t=T)
                    dve.wait_ge(s["z_ready"], at(b))
                    moments(dve, s, z, stats[:, b], mv[:, b], 2 * i + b)
                for b in both:
                    z = psO[b][:].rearrange("p (t f) -> p t f", t=T)
                    dve.wait_ge(s["rstd_ready"], at(b))
                    dve.wait_ge(s["stored"][b], 16 * (i + 1))
                    normalise(dve, x2[:, b], z, mv[:, b], r[:, b]).then_inc(s["x2_ready"], 1)
                dve.wait_ge(s["x2_ready"], at(1))


def convolution(k, tag, own, table, residual, weight, bias, out):
    nc, c = k.nc, k.c
    pairs = k.pairs
    ends = residual is not None
    single = ["held", "start", "index_ready", "weighted_ready", "rowsT_ready", "sum_ready", "product_ready", "scaled_ready", "u_ready",
              "h_ready", "t_ready", "out_ready"] + LN
    with stage(nc, tag, single, ["loaded_s", "loaded_d", "gathered", "stored"]) as s, ExitStack() as ctx:
        def sb(name, shape, dt=F32):
            return ctx.enter_context(nc.sbuf_tensor(f"{tag}_{name}", shape, dt))

        def bank(name):
            return [ctx.enter_context(nc.psum_tensor(f"{tag}_{name}{b}", [D, CH], F32)) for b in (0, 1)]
        index = sb("index", [D, 2, T], I32)
        src, dst, res, weighted, scaled, u, h, t_, x3 = (sb(n, [D, 2, T, D]) for n in ("src", "dst", "res", "weighted", "scaled", "u", "h", "t", "x3"))
        agg = sb("agg", [D, 2, CH])
        stats, mv = sb("stats", [D, 2, T, 6]), sb("mv", [D, 2, T, 2])
        var_eps, r = sb("var_eps", [D, 2, T]), sb("r", [D, 2, T])
        psS, psA = bank("psS"), bank("psA")
        final, final_ready, used = (x3, "out_ready", "t_ready") if ends else (h, "h_ready", "h_ready")
        n_d = 2 if ends else 1
        block = ctx.enter_context(nc.Block())

        @block.sync
        def _(sp):
            def load(i, b):
                sp.dma_start(src[:, b], chunk(own, 2 * i + b)).then_inc(s["loaded_s"][b], 16)
                sp.dma_start(dst[:, b], chunk(table, 2 * i + b)).then_inc(s["loaded_d"][b], 16)
                if ends:
                    sp.dma_start(res[:, b], chunk(residual, 2 * i + b)).then_inc(s["loaded_d"][b], 16)

            def body(i, more):
                for b in (0, 1):
                    if more:
                        hold(sp, s, s[used], 2 * i + b + 1)
                        load(i + 1, b)
                for b in (0, 1):
                    hold(sp, s, s[final_ready], 2 * i + b + 1)
                    sp.dma_start(chunk(out, 2 * i + b), final[:, b]).then_inc(s["stored"][b], 16)
            for b in (0, 1):
                load(0, b)
            with sp.Fori(0, pairs - 1) as i:
                body(i, True)
            body(pairs - 1, False)
            for b in (0, 1):
                sp.wait_ge(s["stored"][b], 16 * (pairs + 1))

        @block.gpsimd
        def _(pool):
            def gather(i, b):
                hold(pool, s, s["loaded_s"][b], 16 * (i + 1))
                gather_rows(pool, s, index, k.last_ix, src, table, k.slots - 1, 2 * i + b, b, s["gathered"][b])
            for b in (0, 1):
                gather(0, b)
            with pool.Fori(0, pairs - 1) as i:
                for b in (0, 1):
                    if ends:
                        rstd(pool, s, k, D, mv[:, b], var_eps[:, b], r[:, b], 2 * i + b)
                    gather(i + 1, b)
            if ends:
                for b in (0, 1):
                    rstd(pool, s, k, D, mv[:, b], var_eps[:, b], r[:, b], 2 * (pairs - 1) + b)

        @block.tensor
        def _(pe):
            with pe.Fori(0, pairs) as i:
                for b in (0, 1):
                    pe.wait_ge(s["weighted_ready"], 2 * i + b + 1)
                    for t in range(T):
                        last = pe.transpose(psS[b][:, t * D:(t + 1) * D], weighted[:, b, t], c["identity"][:])
                    last.then_inc(s["rowsT_ready"], 1)
                for b in (0, 1):
                    pe.wait_ge(s["sum_ready"], 2 * i + b + 1)
                    for t in range(T):
                        at = slice(t * D, (t + 1) * D)
                        last = pe.matmul(psA[b][:, at], agg[:, b, at], c[weight][:], start=True, stop=True, skip_group_check=True)
                    last.then_inc(s["product_ready"], 1)

        @block.vector
        def _(dve):
            for b in (0, 1):
                dve.sem_inc(s["stored"][b], 16)
            dve.memset(agg[:, 1, CH - 1:CH], 0.0).then_inc(s["start"], 1)
            dve.wait_ge(s["start"], 1)
            with dve.Fori(0, pairs) as i:
                both = (0, 1)

                def at(b):
                    return 2 * i + b + 1

                def per_slot(ap, b):
                    return ap[:, bass.ds((2 * i + b) * T, T)].unsqueeze(2).to_broadcast([D, T, D])
                for b in both:
                    dve.wait_ge(s["gathered"][b], 16 * T * (i + 1))
                    dve.tensor_tensor(weighted[:, b], src[:, b], per_slot(k.edge_scale, b), ALU.mult).then_inc(s["weighted_ready"], 1)
                for b in both:
                    dve.wait_ge(s["rowsT_ready"], at(b))
                    if b == 1:
                        dve.wait_ge(s["sum_ready"], 2 * i + 1)
                    dve.tensor_tensor_scan(agg[:, b], k.same[:, bass.ds((2 * i + b) * CH, CH)], psS[b][:], agg[:, 1 - b, CH - 1:CH],
                                           ALU.mult, ALU.add).then_inc(s["sum_ready"], 1)
                for b in both:
                    dve.wait_ge(s["product_ready"], at(b))
                    dve.tensor_tensor(scaled[:, b], psA[b][:].rearrange("p (t f) -> p t f", t=T), per_slot(k.in_norm, b), ALU.mult).then_inc(s["scaled_ready"], 1)
                for b in both:
                    dve.wait_ge(s["scaled_ready"], at(b))
                    dve.tensor_tensor(flat(u, b), flat(scaled, b), c[bias][:], ALU.add).then_inc(s["u_ready"], 1)
                for b in both:
                    dve.wait_ge(s["u_ready"], at(b))
                    dve.wait_ge(s["loaded_d"][b], 16 * n_d * (i + 1))
                    if not ends:
                        dve.wait_ge(s["stored"][b], 16 * (i + 1))
                    dve.scalar_tensor_tensor(flat(h, b), flat(u, b), 0.0, flat(dst, b), ALU.max, ALU.add).then_inc(s["h_ready"], 1)
                if ends:
                    for b in both:
                        dve.wait_ge(s["h_ready"], at(b))
                        dve.tensor_tensor(flat(t_, b), flat(h, b), flat(res, b), ALU.add).then_inc(s["t_ready"], 1)
                    for b in both:
                        dve.wait_ge(s["t_ready"], at(b))
                        moments(dve, s, t_[:, b], stats[:, b], mv[:, b], 2 * i + b)
                    for b in both:
                        dve.wait_ge(s["rstd_ready"], at(b))
                        dve.wait_ge(s["stored"][b], 16 * (i + 1))
                        normalise(dve, x3[:, b], t_[:, b], mv[:, b], r[:, b]).then_inc(s["out_ready"], 1)


def attention3_scores(k):
    nc, c = k.nc, k.c
    pairs = k.pairs
    single = ["held", "start", "mask_ready", "index_ready", "rowsT_ready", "srcT_ready", "dstT_ready", "product_ready", "value_ready",
              "lastrow_ready", "target_ready", "z_ready", "score_ready", "low_ready", "max_ready"]
    with stage(nc, "a3", single, ["loaded_s", "loaded_d", "gathered", "stored"]) as s, ExitStack() as ctx:
        def sb(name, shape, dt=F32):
            return ctx.enter_context(nc.sbuf_tensor(f"a3_{name}", shape, dt))

        def bank(name):
            return [ctx.enter_context(nc.psum_tensor(f"a3_{name}{b}", [D, CH], F32)) for b in (0, 1)]
        index = sb("index", [D, 2, T], I32)
        src, dst = sb("src", [D, 2, T, D]), sb("dst", [D, 2, T, D])
        srcT, dstT, value, lastrow, target, z, score, low, top = (
            sb(n, [D, 2, CH]) for n in ("srcT", "dstT", "value", "lastrow", "target", "z", "score", "low", "top"))
        mask = sb("mask", [D, 2, CH], BF16)
        psS, psD, psX, psF = bank("psS"), bank("psD"), bank("psX"), bank("psF")
        block = ctx.enter_context(nc.Block())

        def q(i, b):
            return (2 * pairs - 1) - (2 * i + b)

        @block.sync
        def _(sp):
            def load(i, b):
                sp.dma_start(src[:, b], chunk(k.s[3], q(i, b))).then_inc(s["loaded_s"][b], 16)
                sp.dma_start(dst[:, b], chunk(k.d[3], q(i, b))).then_inc(s["loaded_d"][b], 16)

            def body(i, more):
                for b in (0, 1):
                    if more:
                        hold(sp, s, s["rowsT_ready"], 2 * i + b + 1)
                        load(i + 1, b)
                for b in (0, 1):
                    hold(sp, s, s["value_ready"], 2 * i + b + 1)
                    sp.dma_start(columns(k.val_t, q(i, b)), value[:, b]).then_inc(s["stored"][b], 16)
                    hold(sp, s, s["max_ready"], 2 * i + b + 1)
                    sp.dma_start(columns(k.score_t, q(i, b)), score[:, b]).then_inc(s["stored"][b], 16)
                    sp.dma_start(columns(k.max_t, q(i, b)), top[:, b]).then_inc(s["stored"][b], 16)
            for b in (0, 1):
                load(0, b)
            with sp.Fori(0, pairs - 1) as i:
                body(i, True)
            body(pairs - 1, False)
            for b in (0, 1):
                sp.wait_ge(s["stored"][b], 48 * (pairs + 1))

        @block.gpsimd
        def _(pool):
            def gather(i, b):
                hold(pool, s, s["loaded_s"][b], 16 * (i + 1))
                pool.tensor_copy(index[:, b], k.last_ix[:, bass.ds(q(i, b) * T, T)]).then_inc(s["index_ready"], 1)
                hold(pool, s, s["index_ready"], 2 * i + b + 1)
                for t in range(T):
                    pool.indirect_dma_start(out=src[:, b, t], out_offset=None, in_=k.d[3],
                                            in_offset=bass.IndirectOffsetOnAxis(ap=index[:, b, t:t + 1], axis=0),
                                            bounds_check=k.slots - 1, oob_is_err=False).then_inc(s["gathered"][b], 16)
            with pool.Fori(0, pairs) as i:
                for b in (0, 1):
                    gather(i, b)

        @block.tensor
        def _(pe):
            with pe.Fori(0, pairs) as i:
                for b in (0, 1):
                    pe.wait_ge(s["gathered"][b], 16 * T * (i + 1))
                    pe.wait_ge(s["loaded_d"][b], 16 * (i + 1))
                    for t in range(T):
                        pe.transpose(psS[b][:, t * D:(t + 1) * D], src[:, b, t], c["identity"][:])
                        last = pe.transpose(psD[b][:, t * D:(t + 1) * D], dst[:, b, t], c["identity"][:])
                    last.then_inc(s["rowsT_ready"], 1)
                for b in (0, 1):
                    pe.wait_ge(s["dstT_ready"], 2 * i + b + 1)
                    pe.matmul(psD[b][:], k.att3_t[:], dstT[:, b], start=True, stop=True)
                    pe.wait_ge(s["srcT_ready"], 2 * i + b + 1)
                    pe.matmul(psF[b][:], k.att3_s[:], srcT[:, b], start=True, stop=True)
                    pe.matmul(psX[b][:], c["L3_gnn_kernel"][:], srcT[:, b], start=True, stop=True).then_inc(s["product_ready"], 1)
                pe.wait_ge(s["z_ready"], 2 * i + 2)
                pe.wait_ge(s["value_ready"], 2 * i + 2)

        @block.scalar
        def _(act):
            for b in (0, 1):
                act.sem_inc(s["stored"][b], 48)
            def load_mask(i, b):
                act.activation(mask[:, b], k.same[:, bass.ds(q(i, b) * CH + 1, CH)], ACT.Copy).then_inc(s["mask_ready"], 1)

            def body(i, more):
                for b in (0, 1):
                    act.wait_ge(s["rowsT_ready"], 2 * i + b + 1)
                    act.activation(dstT[:, b], psD[b][:], ACT.Copy).then_inc(s["dstT_ready"], 1)
                    act.activation(srcT[:, b], psS[b][:], ACT.Copy).then_inc(s["srcT_ready"], 1)
                for b in (0, 1):
                    act.wait_ge(s["product_ready"], 2 * i + b + 1)
                    act.wait_ge(s["stored"][b], 48 * (i + 1))
                    act.activation(value[:, b], psX[b][:], ACT.Copy).then_inc(s["value_ready"], 1)
                for b in (0, 1):
                    if more:
                        act.wait_ge(s["target_ready"], 2 * i + b + 1)
                        load_mask(i + 1, b)
            for b in (0, 1):
                load_mask(0, b)
            with act.Fori(0, pairs - 1) as i:
                body(i, True)
            body(pairs - 1, False)

        @block.vector
        def _(dve):
            for buf in (target, top):
                dve.memset(buf[:, 1, 0:1], 0.0).then_inc(s["start"], 1)
            dve.wait_ge(s["start"], 2)
            with dve.Fori(0, pairs) as i:
                both = (0, 1)

                def at(b):
                    return 2 * i + b + 1

                for b in both:
                    dve.wait_ge(s["mask_ready"], at(b))
                    dve.tensor_scalar(low[:, b], mask[:, b], -1.0, -LOW, ALU.add, ALU.mult).then_inc(s["low_ready"], 1)
                for b in both:
                    dve.wait_ge(s["product_ready"], at(b))
                    dve.scalar_tensor_tensor(lastrow[:, b], mask[:, b], -1.0, psD[b][:], ALU.add, ALU.mult).then_inc(s["lastrow_ready"], 1)
                for b in both:
                    dve.wait_ge(s["lastrow_ready"], at(b))
                    if b == 1:
                        dve.wait_ge(s["target_ready"], 2 * i + 1)
                    dve.tensor_tensor_scan(target[:, b, ::-1], mask[:, b, ::-1], lastrow[:, b, ::-1], target[:, 1 - b, 0:1],
                                           ALU.mult, ALU.subtract).then_inc(s["target_ready"], 1)
                for b in both:
                    dve.wait_ge(s["target_ready"], at(b))
                    dve.tensor_tensor(z[:, b], psF[b][:], target[:, b], ALU.add).then_inc(s["z_ready"], 1)
                for b in both:
                    dve.wait_ge(s["z_ready"], at(b))
                    dve.wait_ge(s["stored"][b], 48 * (i + 1))
                    dve.scalar_tensor_tensor(score[:, b], z[:, b], 0.2, z[:, b], ALU.mult, ALU.max).then_inc(s["score_ready"], 1)
                for b in both:
                    dve.wait_ge(s["score_ready"], at(b))
                    if b == 1:
                        dve.wait_ge(s["max_ready"], 2 * i + 1)
                    dve.tensor_tensor_scan(top[:, b, ::-1], low[:, b, ::-1], score[:, b, ::-1], top[:, 1 - b, 0:1],
                                           ALU.add, ALU.max).then_inc(s["max_ready"], 1)
                dve.wait_ge(s["max_ready"], at(1))


def attention3_sum(k):
    nc, c = k.nc, k.c
    pairs = k.pairs
    single = ["held", "start", "index_ready", "firstmax_ready", "maxheld_ready", "shifted_ready", "exp_ready", "weighted_ready",
              "den_ready", "num_ready", "rows_ready", "denb_ready", "rden_ready", "scaled_ready", "y_ready", "neg_ready",
              "expm_ready", "pos_ready", "t_ready", "out_ready", "out_free"] + LN
    with stage(nc, "b3", single, ["loaded", "scattered"]) as s, ExitStack() as ctx:
        def sb(name, shape, dt=F32):
            return ctx.enter_context(nc.sbuf_tensor(f"b3_{name}", shape, dt))

        def bank(name, n=CH):
            return [ctx.enter_context(nc.psum_tensor(f"b3_{name}{b}", [D, n], F32)) for b in (0, 1)]
        index = sb("index", [D, 2, T], I32)
        valT, score, top, firstmax, maxheld, shifted, expo, weighted, num, den = (
            sb(n, [D, 2, CH]) for n in ("valT", "score", "top", "firstmax", "maxheld", "shifted", "expo", "weighted", "num", "den"))
        x, scaled, y, neg, expm, pos, t_, out = (sb(n, [D, 2, T, D]) for n in ("x", "scaled", "y", "neg", "expm", "pos", "t", "out"))
        denb, rden = sb("denb", [D, 2, T * HEADS]), sb("rden", [D, 2, T * HEADS])
        stats, mv = sb("stats", [D, 2, T, 6]), sb("mv", [D, 2, T, 2])
        var_eps, r = sb("var_eps", [D, 2, T]), sb("r", [D, 2, T])
        psA, psN = bank("psA"), bank("psN", T * HEADS)
        block = ctx.enter_context(nc.Block())

        @block.sync
        def _(sp):
            def load(i, b):
                n = 2 * i + b
                sp.dma_start(valT[:, b], columns(k.val_t, n)).then_inc(s["loaded"][b], 16)
                sp.dma_start(score[:, b], columns(k.score_t, n)).then_inc(s["loaded"][b], 16)
                sp.dma_start(top[:, b], columns(k.max_t, n)).then_inc(s["loaded"][b], 16)
                sp.dma_start(x[:, b], chunk(k.d[3], n)).then_inc(s["loaded"][b], 16)
            for b in (0, 1):
                load(0, b)
            with sp.Fori(0, pairs - 1) as i:
                for b in (0, 1):
                    hold(sp, s, s["pos_ready"], 2 * i + b + 1)
                    load(i + 1, b)

        @block.scalar
        def _(act):
            with act.Fori(0, pairs) as i:
                for b in (0, 1):
                    act.wait_ge(s["shifted_ready"], 2 * i + b + 1)
                    act.activation(expo[:, b], shifted[:, b], ACT.Exp).then_inc(s["exp_ready"], 1)
                for b in (0, 1):
                    act.wait_ge(s["neg_ready"], 2 * i + b + 1)
                    act.activation(flat(expm, b), flat(neg, b), ACT.Exp).then_inc(s["expm_ready"], 1)

        @block.gpsimd
        def _(pool):
            pool.sem_inc(s["out_free"], 2)
            with pool.Fori(0, pairs) as i:
                for b in (0, 1):
                    rstd(pool, s, k, D, mv[:, b], var_eps[:, b], r[:, b], 2 * i + b)
                for b in (0, 1):
                    n = 2 * i + b
                    hold(pool, s, s["out_ready"], n + 1)
                    pool.tensor_copy(index[:, b], k.out_ix[:, bass.ds(n * T, T)]).then_inc(s["index_ready"], 1)
                    hold(pool, s, s["index_ready"], n + 1)
                    for t in range(T):
                        pool.indirect_dma_start(out=k.out, out_offset=bass.IndirectOffsetOnAxis(ap=index[:, b, t:t + 1], axis=0),
                                                in_=out[:, b, t], in_offset=None,
                                                bounds_check=k.n_nodes - 1, oob_is_err=False).then_inc(s["scattered"][b], 16)
                for b in (0, 1):
                    hold(pool, s, s["scattered"][b], 16 * T * (i + 1))
                    pool.sem_inc(s["out_free"])

        @block.tensor
        def _(pe):
            with pe.Fori(0, pairs) as i:
                for b in (0, 1):
                    pe.wait_ge(s["den_ready"], 2 * i + b + 1)
                    for t in range(T):
                        pe.matmul(psN[b][:, t * HEADS:(t + 1) * HEADS], den[:, b, t * D:(t + 1) * D], c["head_pick"][:],
                                  start=True, stop=True, skip_group_check=True)
                    pe.wait_ge(s["num_ready"], 2 * i + b + 1)
                    for t in range(T):
                        last = pe.transpose(psA[b][:, t * D:(t + 1) * D], num[:, b, t * D:(t + 1) * D], c["identity"][:])
                    last.then_inc(s["rows_ready"], 1)

        @block.vector
        def _(dve):
            for buf in (maxheld, num, den):
                dve.memset(buf[:, 1, CH - 1:CH], 0.0).then_inc(s["start"], 1)
            dve.wait_ge(s["start"], 3)
            with dve.Fori(0, pairs) as i:
                both = (0, 1)

                def at(b):
                    return 2 * i + b + 1

                def same(b):
                    return k.same[:, bass.ds((2 * i + b) * CH, CH)]
                for b in both:
                    dve.wait_ge(s["loaded"][b], 64 * (i + 1))
                    dve.scalar_tensor_tensor(firstmax[:, b], same(b), -1.0, top[:, b], ALU.add, ALU.mult).then_inc(s["firstmax_ready"], 1)
                for b in both:
                    dve.wait_ge(s["firstmax_ready"], at(b))
                    if b == 1:
                        dve.wait_ge(s["maxheld_ready"], 2 * i + 1)
                    dve.tensor_tensor_scan(maxheld[:, b], same(b), firstmax[:, b], maxheld[:, 1 - b, CH - 1:CH], ALU.mult, ALU.subtract).then_inc(s["maxheld_ready"], 1)
                for b in both:
                    dve.wait_ge(s["maxheld_ready"], at(b))
                    dve.tensor_tensor(shifted[:, b], score[:, b], maxheld[:, b], ALU.subtract).then_inc(s["shifted_ready"], 1)
                for b in both:
                    dve.wait_ge(s["exp_ready"], at(b))
                    dve.tensor_tensor(weighted[:, b], expo[:, b], valT[:, b], ALU.mult).then_inc(s["weighted_ready"], 1)
                    if b == 1:
                        dve.wait_ge(s["den_ready"], 2 * i + 1)
                    dve.tensor_tensor_scan(den[:, b], same(b), expo[:, b], den[:, 1 - b, CH - 1:CH], ALU.mult, ALU.add).then_inc(s["den_ready"], 1)
                for b in both:
                    dve.wait_ge(s["weighted_ready"], at(b))
                    if b == 1:
                        dve.wait_ge(s["num_ready"], 2 * i + 1)
                    dve.tensor_tensor_scan(num[:, b], same(b), weighted[:, b], num[:, 1 - b, CH - 1:CH], ALU.mult, ALU.add).then_inc(s["num_ready"], 1)
                for b in both:
                    dve.wait_ge(s["rows_ready"], at(b))
                    dve.tensor_scalar(denb[:, b], psN[b][:], 1e-7, None, ALU.add).then_inc(s["denb_ready"], 1)
                    dve.wait_ge(s["denb_ready"], at(b))
                    dve.reciprocal(rden[:, b], denb[:, b]).then_inc(s["rden_ready"], 1)
                for b in both:
                    dve.wait_ge(s["rden_ready"], at(b))
                    dve.tensor_tensor(flat(scaled, b).rearrange("p (g u) -> p g u", u=UNITS), psA[b][:].rearrange("p (g u) -> p g u", u=UNITS),
                                      rden[:, b].unsqueeze(2).to_broadcast([D, T * HEADS, UNITS]), ALU.mult).then_inc(s["scaled_ready"], 1)
                for b in both:
                    dve.wait_ge(s["scaled_ready"], at(b))
                    dve.tensor_tensor(flat(y, b), flat(scaled, b), c["b_3"][:], ALU.add).then_inc(s["y_ready"], 1)
                for b in both:
                    dve.wait_ge(s["y_ready"], at(b))
                    dve.tensor_scalar(flat(neg, b), flat(y, b), 0.0, None, ALU.min).then_inc(s["neg_ready"], 1)
                    dve.scalar_tensor_tensor(flat(pos, b), flat(y, b), 0.0, flat(x, b), ALU.max, ALU.add).then_inc(s["pos_ready"], 1)
                for b in both:
                    dve.wait_ge(s["pos_ready"], at(b))
                    dve.wait_ge(s["expm_ready"], at(b))
                    dve.scalar_tensor_tensor(flat(t_, b), flat(expm, b), -1.0, flat(pos, b), ALU.add, ALU.add).then_inc(s["t_ready"], 1)
                for b in both:
                    dve.wait_ge(s["t_ready"], at(b))
                    moments(dve, s, t_[:, b], stats[:, b], mv[:, b], 2 * i + b)
                for b in both:
                    dve.wait_ge(s["rstd_ready"], at(b))
                    dve.wait_ge(s["out_free"], at(b))
                    normalise(dve, out[:, b], t_[:, b], mv[:, b], r[:, b]).then_inc(s["out_ready"], 1)


def launch_arrays(inputs, n_nodes, n_edges):
    g = {n: np.ascontiguousarray(v) for n, v in inputs.items()}
    slots = padded_slots(n_edges)

    def pad(a, value):
        return np.concatenate([a, np.full(slots - n_edges, value, a.dtype)])

    def cols(a):
        return np.ascontiguousarray(a.reshape(-1, D).T)

    def rows(a):
        return np.ascontiguousarray(np.tile(a[None, :], (D, T)))

    def col(a):
        return np.ascontiguousarray(a.reshape(D, 1))
    dst_ext = np.concatenate([np.full(1, -1, np.int32), pad(g["dst"], NO_NODE), np.full(1, NO_NODE + 1, np.int32)])
    a = {
        "x": g["x"],
        "src_cols": cols(pad(g["src"], 0)), "src_hist": cols(pad(g["src"], NO_NODE)),
        "dst_gather": cols(pad(g["dst"], 0)), "dst_cols": cols(pad(g["dst"], NO_NODE)),
        "dst_next": cols(dst_ext[2:]), "dst_ext": dst_ext, "weight_cols": cols(pad(g["edge_weight"], 0)),
        "Wp_t": np.ascontiguousarray(g["L0_gnn_Wp"].T), "kernel_t": np.ascontiguousarray(g["L3_gnn_kernel"].T),
        "L1_Wa": np.ascontiguousarray(g["L1_gnn_W_edge"][:D]), "L1_Wb": np.ascontiguousarray(g["L1_gnn_W_edge"][D:]),
        "b_p": rows(g["L0_gnn_bp"]), "b_2": rows(g["L1_gnn_b2"]), "b_conv1": rows(g["L2_gnn_b1"]),
        "b_conv2": rows(g["L2_gnn_b2"]), "b_3": rows(g["L3_gnn_bias"]),
        "b_edge": col(g["L1_gnn_b_edge"]), "b_1": col(g["L1_gnn_b1"]),
        "ka1": col(g["L3_gnn_ka1"]), "ka2": col(g["L3_gnn_ka2"]),
        "eps": np.ascontiguousarray(np.broadcast_to(g["L1_gnn_eps"].reshape(1, 1), (D, 1))),
    }
    for n in ("L0_gnn_Wq", "L0_gnn_Wk", "L0_gnn_Wv", "L1_gnn_W1", "L1_gnn_W2", "L2_gnn_W1", "L2_gnn_W2", "L3_gnn_kernel"):
        a[n] = g[n]
    head = np.arange(D) // UNITS
    a["identity"] = np.eye(D, dtype=np.float32)
    a["head_block"] = (head[:, None] == head[None, :]).astype(np.float32)
    a["head_pick"] = (np.arange(D)[:, None] == UNITS * np.arange(HEADS)[None, :]).astype(np.float32)
    a["score_block"] = np.full((D, D), D ** -0.5, np.float32)
    a["first_row"] = (np.arange(D) == 0).astype(np.float32)[:, None]
    a["ones"] = np.ones((D, D), np.float32)
    a["strict_upper"] = np.triu(np.ones((D, D), np.float32), 1)
    return a


def build(nc, arrays, n_nodes, n_edges):
    args = {n: nc.dram_tensor(f"in_{n}", v.shape, mybir.dt.from_np(v.dtype), kind="ExternalInput").ap() for n, v in arrays.items()}
    out = nc.dram_tensor("out", (n_nodes, D), F32, kind="ExternalOutput").ap()
    gnn_kernel(nc, n_nodes, n_edges, args, out)


def kernel(**inputs):
    import concourse.bacc as bacc
    from concourse.bass_utils import run_bass_kernel_spmd

    n_nodes, n_edges = inputs["x"].shape[0], inputs["src"].shape[0]
    nc = bacc.Bacc("TRN2", target_bir_lowering=False, num_devices=1)
    arrays = launch_arrays({n: np.asarray(v) for n, v in inputs.items()}, n_nodes, n_edges)
    build(nc, arrays, n_nodes, n_edges)
    r = run_bass_kernel_spmd(nc, [{f"in_{n}": v for n, v in arrays.items()}], core_ids=[0])
    return r.results[0]["out"]
```

```python
from contextlib import ExitStack, contextmanager

import numpy as np

import concourse.bass as bass
from concourse import mybir

F32 = mybir.dt.float32
BF16 = mybir.dt.bfloat16
I32 = mybir.dt.int32
ALU = mybir.AluOpType
ACT = mybir.ActivationFunctionType

D = 128
T = 4
CH = T * D
UT = 8
DENSE_P = 125
HEADS = 8
UNITS = D // HEADS
TABLE_W = 1024
NO_NODE = 1 << 17
FIRST, LAST, DEGREE = 0, 1, 2
EARLY_ENDS = 64
EPS = 1e-5
LOW = -1e30


def padded_slots(n_edges):
    return -(-n_edges // (2 * CH)) * 2 * CH


@contextmanager
def stage(nc, tag, single=(), paired=(), bufs=2):
    s = {n: nc.alloc_semaphore(f"{tag}_{n}") for n in single}
    s.update({n: [nc.alloc_semaphore(f"{tag}_{n}{b}") for b in range(bufs)] for n in paired})
    yield s
    every = [x for n in single for x in [s[n]]] + [x for n in paired for x in s[n]]
    nc.clear_and_free_semaphores(every)
    nc.all_engine_barrier()


class Program:
    pass


def gnn_kernel(nc, n_nodes, n_edges, args, out):
    k = Program()
    k.nc, k.args, k.out = nc, args, out
    k.n_nodes, k.n_edges = n_nodes, n_edges
    k.slots = padded_slots(n_edges)
    k.pairs = k.slots // (2 * CH)
    k.tiles = k.slots // D
    k.table_a = -(-n_nodes // TABLE_W)

    def scratch(name, shape, dt=F32):
        return nc.dram_tensor(name, shape, dt, kind="Internal").ap()

    k.table = scratch("node_table", (k.table_a * TABLE_W, 4), I32)
    k.d = [scratch(f"d{n}", (k.slots, D)) for n in range(4)]
    k.dh = scratch("dh", (k.slots, D))
    k.s = [scratch(f"s{n}", (k.slots, D)) for n in range(4)]
    k.sh = scratch("sh", (k.slots, D))
    k.val_t = scratch("val_t", (D, k.slots))
    k.score_t = scratch("score_t", (D, k.slots))
    k.max_t = scratch("max_t", (D, k.slots))

    with ExitStack() as ctx:
        def sb(name, shape, dt=F32):
            return ctx.enter_context(nc.sbuf_tensor(name, shape, dt))

        k.same = sb("same_dst", [D, k.slots + 2], BF16)
        k.src_ix = sb("src_ix", [D, k.tiles], I32)
        k.dst_ix = sb("dst_ix", [D, k.tiles], I32)
        k.found = sb("found", [D, k.tiles, 4], I32)
        k.out_ix = sb("out_ix", [D, k.tiles], I32)
        k.edge_scale = sb("edge_scale", [D, k.tiles])
        k.in_norm = sb("in_norm", [D, k.tiles])
        k.c = {n: sb(f"c_{n}", list(args[n].shape)) for n in CONSTANTS}
        k.att0 = sb("att0", [D, D])
        k.val0 = sb("val0", [D, D])
        k.att3_t = sb("att3_t", [D, D])
        k.att3_s = sb("att3_s", [D, D])
        k.one_eps = sb("one_eps", [D, 1])
        k.conv_c = sb("conv_c", [D, CH])
        k.conv_c1 = sb("conv_c1", [D, CH])
        k.elu_c = sb("elu_c", [D, CH])
        k.neg_half = sb("neg_half", [D, T])
        k.eps_ln, k.eps_quarter = sb("eps_ln", [D, 1]), sb("eps_quarter", [D, 1])
        prepare_weights(k)
        prepare_graph(k)
        chain_pass(k, "dense", DENSE_P, k.n_nodes // DENSE_P, args["x"], k.out)
        attention0_scores(k)
        attention0_sum(k)
        chain_pass(k, "chain_s", D, k.tiles, k.s[0], None)
        edge_mlp(k)
        convolution(k, "conv1", k.s[2], k.d[2], None, "L2_gnn_W1", "b_conv1", k.dh)
        convolution(k, "conv2", k.sh, k.dh, k.d[2], "L2_gnn_W2", "b_conv2", k.d[3])
        attention3_scores(k)
        attention3_sum(k)


CONSTANTS = [
    "L0_gnn_Wq", "L0_gnn_Wk", "L0_gnn_Wv", "Wp_t", "L1_Wa", "L1_Wb", "L1_gnn_W1", "L1_gnn_W2",
    "L2_gnn_W1", "L2_gnn_W2", "L3_gnn_kernel", "kernel_t", "b_p", "b_edge", "b_2_col", "b_1", "b_2", "b_conv1",
    "b_conv2", "b_3", "ka1", "ka2", "eps", "identity", "head_block", "head_pick", "score_block",
    "first_row", "ones", "strict_upper",
]


def hold(eng, s, sem, value):
    eng.wait_ge(sem, value)
    eng.sem_inc(s["held"])


def hold_count(eng, s, sem, value):
    if not isinstance(value, int) or value > 0:
        hold(eng, s, sem, value)


def chunk(ap, c):
    return ap.rearrange("(c t p) f -> c p t f", t=T, p=D)[bass.ds(c, 1)].rearrange("a p t f -> (a p) t f")


def columns(ap, c):
    return ap[:, bass.ds(c * CH, CH)]


def flat(t, b):
    return t[:, b].rearrange("p t f -> p (t f)")


def prepare_weights(k):
    nc, c = k.nc, k.c
    with stage(nc, "w", ["loaded", "block", "product", "relu", "conv", "low", "exp", "high"]) as s, ExitStack() as ctx:
        ps = [ctx.enter_context(nc.psum_tensor(f"w_ps{n}", [D, D], F32)) for n in range(4)]
        blocks = ctx.enter_context(nc.sbuf_tensor("w_blocks", [D, 2, D], F32))
        low = ctx.enter_context(nc.sbuf_tensor("w_low", [D, CH], F32))
        relu2 = ctx.enter_context(nc.sbuf_tensor("w_relu2", [D, CH], F32))
        n_loads = 16 * len(CONSTANTS)
        block = ctx.enter_context(nc.Block())

        @block.sync
        def _(sp):
            for n in CONSTANTS:
                sp.dma_start(c[n][:], k.args[n]).then_inc(s["loaded"], 16)

        @block.tensor
        def _(pe):
            pe.wait_ge(s["loaded"], n_loads)
            pe.matmul(ps[0][:], c["L0_gnn_Wq"][:], c["L0_gnn_Wk"][:], start=True, stop=True)
            pe.matmul(ps[1][:], c["L0_gnn_Wv"][:], c["Wp_t"][:], start=True, stop=True)
            pe.wait_ge(s["block"], 2)
            pe.matmul(ps[2][:], c["kernel_t"][:], blocks[:, 0], start=True, stop=True)
            pe.matmul(ps[3][:], c["kernel_t"][:], blocks[:, 1], start=True, stop=True).then_inc(s["product"], 1)

        @block.vector
        def _(dve):
            dve.wait_ge(s["loaded"], n_loads)
            dve.tensor_scalar(blocks[:, 0], c["head_block"][:], c["ka1"][:, 0:1], None, ALU.mult).then_inc(s["block"], 1)
            dve.tensor_scalar(blocks[:, 1], c["head_block"][:], c["ka2"][:, 0:1], None, ALU.mult).then_inc(s["block"], 1)
            dve.tensor_scalar(k.one_eps[:], c["eps"][:], 1.0, None, ALU.add)
            dve.memset(k.neg_half[:], -0.5)
            dve.memset(k.eps_ln[:], EPS)
            dve.memset(k.eps_quarter[:], EPS / 4)
            dve.tensor_scalar(k.conv_c1[:], c["b_conv1"][:], 0.0, None, ALU.max).then_inc(s["relu"], 1)
            dve.tensor_scalar(relu2[:], c["b_conv2"][:], 0.0, None, ALU.max).then_inc(s["relu"], 1)
            dve.tensor_scalar(low[:], c["b_3"][:], 0.0, None, ALU.min).then_inc(s["low"], 1)
            dve.wait_ge(s["relu"], 2)
            dve.tensor_tensor(k.conv_c[:], k.conv_c1[:], relu2[:], ALU.add).then_inc(s["conv"], 1)
            dve.wait_ge(s["exp"], 1)
            dve.wait_ge(s["conv"], 1)
            dve.tensor_scalar(relu2[:], k.elu_c[:], -1.0, None, ALU.add).then_inc(s["high"], 1)
            dve.wait_ge(s["high"], 1)
            dve.scalar_tensor_tensor(k.elu_c[:], c["b_3"][:], 0.0, relu2[:], ALU.max, ALU.add)
            dve.wait_ge(s["product"], 1)
            for to, frm in ((k.att0, ps[0]), (k.val0, ps[1]), (k.att3_t, ps[2]), (k.att3_s, ps[3])):
                dve.tensor_copy(to[:], frm[:])

        @block.scalar
        def _(act):
            act.wait_ge(s["low"], 1)
            act.activation(k.elu_c[:], low[:], ACT.Exp).then_inc(s["exp"], 1)


class EndRows:
    SEMAPHORES = ["row_index", "rows_gathered", "rows_stored"]

    def __init__(self, k, s, ctx, tag, first, count):
        self.k, self.s, self.first, self.rounds = k, s, first, count // 2
        self.index = ctx.enter_context(k.nc.sbuf_tensor(f"{tag}_row_index", [D, 2, 2, T], I32))
        self.rows = ctx.enter_context(k.nc.sbuf_tensor(f"{tag}_rows", [D, 2, 2, T, D], F32))

    def gather(self, pool):
        k, s = self.k, self.s

        def one(i, b):
            c = self.first + 2 * i + b
            hold_count(pool, s, s["rows_stored"][b], 32 * i)
            for e, ix in enumerate((k.src_ix, k.dst_ix)):
                last = pool.tensor_copy(self.index[:, b, e], ix[:, bass.ds(c * T, T)])
            last.then_inc(s["row_index"][b], 1)
            hold(pool, s, s["row_index"][b], i + 1)
            for e in (0, 1):
                for t in range(T):
                    pool.indirect_dma_start(out=self.rows[:, b, e, t], out_offset=None, in_=k.args["x"],
                                            in_offset=bass.IndirectOffsetOnAxis(ap=self.index[:, b, e, t:t + 1], axis=0),
                                            bounds_check=k.n_nodes - 1, oob_is_err=False).then_inc(s["rows_gathered"][b], 16)
        for b in (0, 1):
            one(0, b)
        with pool.Fori(1, self.rounds) as i:
            for b in (0, 1):
                one(i, b)

    def store(self, sp):
        k, s = self.k, self.s
        with sp.Fori(0, self.rounds) as i:
            for b in (0, 1):
                c = self.first + 2 * i + b
                hold(sp, s, s["rows_gathered"][b], 32 * T * (i + 1))
                for e, to in enumerate((k.s[0], k.d[0])):
                    sp.dma_start(chunk(to, c), self.rows[:, b, e]).then_inc(s["rows_stored"][b], 16)
        for b in (0, 1):
            sp.wait_ge(s["rows_stored"][b], 32 * self.rounds)


def prepare_graph(k):
    nc = k.nc
    A, W = k.table_a, TABLE_W
    half = W // 2
    with stage(nc, "h", ["held", "loaded", "split", "float", "iota", "cleared", "hot", "counted", "count_in", "ranks", "offset", "offset_sb", "ended", "absent", "filled", "table"], EndRows.SEMAPHORES) as s, ExitStack() as ctx:
        def sb(name, shape, dt=F32):
            return ctx.enter_context(nc.sbuf_tensor(f"h_{name}", shape, dt))
        cols = sb("cols", [D, 2, k.tiles], I32)
        parts = sb("parts", [D, 2, 2, k.tiles], I32)
        partsf = sb("partsf", [D, 2, 2, k.tiles])
        row_no = sb("row_no", [D, W], I32)
        row_nof = sb("row_nof", [D, W], mybir.dt.int16)
        hot_a = sb("hot_a", [D, 2, 2, A], BF16)
        hot_w = sb("hot_w", [D, 2, 2, W], BF16)
        zero = sb("zero", [D, half], BF16)
        count = sb("count", [A, W])
        upto = sb("upto", [A, W])
        ones_w = sb("ones_w", [A, W])
        offset = sb("offset", [A, 1])
        absent = sb("absent", [A, W])
        table = sb("table", [A, W, 4], I32)
        ps = [[ctx.enter_context(nc.psum_tensor(f"h_ps{g}{h}", [D, half], F32)) for h in (0, 1)] for g in (0, 1)]
        ps_off = ctx.enter_context(nc.psum_tensor("h_off", [D, 1], F32))
        chunks = 2 * k.pairs
        early = 2 * (k.pairs * EARLY_ENDS // 100)
        ends = EndRows(k, s, ctx, "h", 0, early)
        block = ctx.enter_context(nc.Block())

        @block.sync
        def _(sp):
            sp.dma_start(cols[:, 0], k.args["src_hist"]).then_inc(s["loaded"], 16)
            sp.dma_start(cols[:, 1], k.args["dst_cols"]).then_inc(s["loaded"], 16)
            sp.dma_start(k.src_ix[:], k.args["src_cols"]).then_inc(s["loaded"], 16)
            sp.dma_start(k.dst_ix[:], k.args["dst_gather"]).then_inc(s["loaded"], 16)
            ends.store(sp)
            sp.wait_ge(s["filled"], 4)
            sp.dma_start(k.table.rearrange("(a w) f -> a (w f)", a=A), table[:].rearrange("a w f -> a (w f)")).then_inc(s["table"], 16)
            sp.wait_ge(s["table"], 16)
            sp.wait_ge(s["loaded"], 64)

        @block.gpsimd
        def _(pool):
            pool.iota(row_no[:], [[1, W]], base=0, channel_multiplier=0).then_inc(s["iota"], 1)
            hold(pool, s, s["loaded"], 64)
            ends.gather(pool)

        @block.vector
        def _(dve):
            dve.memset(zero[:], 0.0).then_inc(s["cleared"], 1)
            dve.memset(ones_w[:], 1.0)
            dve.wait_ge(s["iota"], 1)
            dve.tensor_copy(row_nof[:], row_no[:]).then_inc(s["iota"], 1)
            dve.wait_ge(s["loaded"], 64)
            dve.tensor_scalar(parts[:, 0], cols[:], W.bit_length() - 1, None, ALU.logical_shift_right).then_inc(s["split"], 1)
            dve.tensor_scalar(parts[:, 1], cols[:], W - 1, None, ALU.bitwise_and).then_inc(s["split"], 1)
            dve.wait_ge(s["split"], 2)
            dve.tensor_copy(partsf[:], parts[:]).then_inc(s["float"], 1)
            dve.wait_ge(s["iota"], 2)
            dve.wait_ge(s["float"], 1)
            with dve.Fori(0, k.tiles // 2) as i:
                for b in (0, 1):
                    for g in (0, 1):
                        if g == 0:
                            dve.wait_ge(s["counted"], 2 * i + b + 1)
                        a_col = partsf[:, 0, g, bass.ds(2 * i + b, 1)]
                        w_col = partsf[:, 1, g, bass.ds(2 * i + b, 1)]
                        dve.tensor_scalar(hot_a[:, b, g], row_nof[:, 0:A], a_col, None, ALU.is_equal)
                        last = dve.tensor_scalar(hot_w[:, b, g], row_nof[:], w_col, None, ALU.is_equal)
                    last.then_inc(s["hot"], 1)
            dve.wait_ge(s["counted"], k.tiles + 2)
            for h in (0, 1):
                dve.tensor_copy(count[:, h * half:(h + 1) * half], ps[1][h][0:A, :]).then_inc(s["count_in"], 1)
                dve.tensor_copy(table[:, h * half:(h + 1) * half, 2], ps[0][h][0:A, :]).then_inc(s["filled"], 1)
            dve.wait_ge(s["count_in"], 2)
            dve.tensor_tensor_scan(upto[:], ones_w[:], count[:], 0.0, ALU.mult, ALU.add).then_inc(s["ranks"], 1)
            dve.wait_ge(s["offset"], 1)
            dve.tensor_copy(offset[:], ps_off[0:A, :]).then_inc(s["offset_sb"], 1)
            dve.tensor_scalar(absent[:], count[:], 0.0, float(NO_NODE), ALU.is_equal, ALU.mult).then_inc(s["absent"], 1)
            dve.wait_ge(s["offset_sb"], 1)
            dve.tensor_scalar(ones_w[:], upto[:], offset[:, 0:1], -1.0, ALU.add, ALU.add).then_inc(s["ended"], 1)
            dve.wait_ge(s["ended"], 1)
            dve.wait_ge(s["absent"], 1)
            dve.tensor_tensor(upto[:], ones_w[:], absent[:], ALU.add).then_inc(s["ended"], 1)
            dve.wait_ge(s["ended"], 2)
            dve.tensor_copy(table[:, :, 1], upto[:]).then_inc(s["filled"], 1)
            dve.tensor_copy(table[:, :, 3], upto[:])
            dve.tensor_tensor(absent[:], upto[:], count[:], ALU.subtract).then_inc(s["ended"], 1)
            dve.wait_ge(s["ended"], 3)
            dve.tensor_scalar(table[:, :, 0], absent[:], 1.0, None, ALU.add).then_inc(s["filled"], 1)

        @block.tensor
        def _(pe):
            pe.wait_ge(s["cleared"], 1)
            for g in (0, 1):
                for h in (0, 1):
                    last = pe.matmul(ps[g][h][:], zero[:, 0:D], zero[:], start=True, stop=False, skip_group_check=True)
            last.then_inc(s["counted"], 2)
            with pe.Fori(0, k.tiles // 2) as i:
                for b in (0, 1):
                    pe.wait_ge(s["hot"], 2 * i + b + 1)
                    for g in (0, 1):
                        for h in (0, 1):
                            last = pe.matmul(ps[g][h][0:A, :], hot_a[:, b, g], hot_w[:, b, g, h * half:(h + 1) * half],
                                             start=False, stop=False, skip_group_check=True)
                    last.then_inc(s["counted"], 1)
            pe.wait_ge(s["ranks"], 1)
            pe.matmul(ps_off[0:A, :], k.c["strict_upper"][0:A, 0:A], upto[:, W - 1:W], start=True, stop=True).then_inc(s["offset"], 1)

    with stage(nc, "m", ["held", "same", "counted", "degree", "loaded_ix", "skip", "start"], ["loaded"] + EndRows.SEMAPHORES) as s, ExitStack() as ctx:
        def sb(name, shape, dt=F32):
            return ctx.enter_context(nc.sbuf_tensor(f"m_{name}", shape, dt))
        dst = sb("dst", [D, 2, CH + 1], I32)
        count = sb("count", [D, 2, CH])
        one = sb("one", [D, CH])
        nxt = sb("nxt", [D, 2, k.tiles], I32)
        skip = sb("skip", [D, k.tiles], I32)
        ps = ctx.enter_context(nc.psum_tensor("m_ps", [D, k.tiles], F32))
        dst_ext = k.args["dst_ext"]
        ends = EndRows(k, s, ctx, "m", early, chunks - early)
        block = ctx.enter_context(nc.Block())

        @block.scalar
        def _(act):
            def load(i, b):
                src = dst_ext[bass.ds((2 * i + b) * CH, CH + 1)] if not isinstance(i, int) else dst_ext[(2 * i + b) * CH:(2 * i + b + 1) * CH + 1]
                act.dma_start(dst[:, b], src.partition_broadcast(D)).then_inc(s["loaded"][b], 16)
            act.dma_start(nxt[:, 0], k.args["dst_cols"]).then_inc(s["loaded_ix"], 16)
            act.dma_start(nxt[:, 1], k.args["dst_next"]).then_inc(s["loaded_ix"], 16)
            for b in (0, 1):
                load(0, b)
            with act.Fori(0, k.pairs - 1) as i:
                for b in (0, 1):
                    act.wait_ge(s["same"], 2 * i + b + 1)
                    load(i + 1, b)

        @block.sync
        def _(sp):
            ends.store(sp)

        @block.gpsimd
        def _(pool):
            ends.gather(pool)

        @block.vector
        def _(dve):
            dve.memset(one[:], 1.0).then_inc(s["start"], 1)
            dve.memset(count[:, 1, CH - 1:CH], 0.0).then_inc(s["start"], 1)
            dve.memset(k.same[:, k.slots:], 0.0)
            dve.wait_ge(s["start"], 2)
            with dve.Fori(0, k.pairs) as i:
                for b in (0, 1):
                    c = 2 * i + b
                    dve.wait_ge(s["loaded"][b], 16 * (i + 1))
                    dve.tensor_tensor(k.same[:, bass.ds(c * CH, CH)], dst[:, b, 1:], dst[:, b, 0:CH], ALU.is_equal).then_inc(s["same"], 1)
                    dve.wait_ge(s["same"], c + 1)
                    if b == 0:
                        dve.wait_ge(s["degree"], 2 * i + 1)
                    else:
                        dve.wait_ge(s["degree"], 2 * i + 2)
                    dve.tensor_tensor_scan(count[:, b], k.same[:, bass.ds(c * CH, CH)], one[:], count[:, 1 - b, CH - 1:CH],
                                           ALU.mult, ALU.add).then_inc(s["counted"], 1)
                    dve.wait_ge(s["counted"], c + 1)
            dve.wait_ge(s["loaded_ix"], 32)
            dve.tensor_tensor(skip[:], nxt[:, 0], nxt[:, 1], ALU.is_equal).then_inc(s["skip"], 1)
            dve.wait_ge(s["skip"], 1)
            dve.scalar_tensor_tensor(k.out_ix[:], skip[:], float(NO_NODE), nxt[:, 0], ALU.mult, ALU.add)
            dve.wait_ge(s["degree"], 2 * k.pairs + 2)
            dve.tensor_copy(k.in_norm[:], ps[:])

        @block.tensor
        def _(pe):
            pe.sem_inc(s["degree"], 2)
            with pe.Fori(0, k.pairs) as i:
                for b in (0, 1):
                    c = 2 * i + b
                    pe.wait_ge(s["counted"], c + 1)
                    for t in range(T):
                        last = pe.matmul(ps[:, bass.ds(c * T + t, 1)], count[:, b, t * D:(t + 1) * D], k.c["first_row"][:],
                                         start=True, stop=True, skip_group_check=True)
                    last.then_inc(s["degree"], 1)


def moments(dve, s, z, stats, mv, n):
    for t in range(T):
        last = dve.bn_stats(stats[:, t], z[:, t])
    last.then_inc(s["stats_ready"], 1)
    hold(dve, s, s["stats_ready"], n + 1)
    for t in range(T):
        last = dve.bn_aggr(mv[:, t], stats[:, t])
    last.then_inc(s["moments_ready"], 1)


def rstd(pool, s, k, P, mv, var_eps, r, n, quarter=False):
    hold(pool, s, s["moments_ready"], n + 1)
    if quarter:
        pool.tensor_scalar(var_eps, mv[:, :, 1], EPS, 0.25, ALU.add, ALU.mult).then_inc(s["var_eps_ready"], 1)
    else:
        pool.tensor_scalar(var_eps, mv[:, :, 1], EPS, None, ALU.add).then_inc(s["var_eps_ready"], 1)
    hold(pool, s, s["var_eps_ready"], n + 1)
    pool.tensor_tensor(r, var_eps, k.neg_half[0:r.shape[0]], ALU.pow).then_inc(s["rstd_ready"], 1)


def normalise(dve, out, z, mv, r):
    for t in range(T):
        last = dve.tensor_scalar(out[:, t], z[:, t], mv[:, t, 0:1], r[:, t:t + 1], ALU.subtract, ALU.mult)
    return last


LN = ["stats_ready", "moments_ready", "var_eps_ready", "rstd_ready"]


def wait_count(eng, sem, value):
    if not isinstance(value, int) or value > 0:
        eng.wait_ge(sem, value)


BUFS = 4


class Pair:

    def __init__(self, round, parity):
        self.round, self.parity = round, parity

    def n(self, b):
        return 4 * self.round + (2 * self.parity + b)

    def at(self, b):
        return 4 * self.round + (2 * self.parity + b + 1)

    def buf(self, b):
        return 2 * self.parity + b

    def before(self):
        return Pair(self.round - 1, self.parity)


def turns(engine, pairs, turn):
    def pair(t):
        return Pair(t // 2, t % 2) if 0 <= t < pairs else None

    def peeled(t):
        turn(pair(t + 2), pair(t + 1), pair(t), pair(t - 1), pair(t - 2))
    rounds = (pairs - 4) // 2
    for t in range(5):
        peeled(t)
    with engine.Fori(2, rounds + 1) as i:
        turn(Pair(i + 1, 1), Pair(i + 1, 0), Pair(i, 1), Pair(i, 0), Pair(i - 1, 1))
        turn(Pair(i + 2, 0), Pair(i + 1, 1), Pair(i + 1, 0), Pair(i, 1), Pair(i, 0))
    for t in range(2 * rounds + 3, pairs + 2):
        peeled(t)


def shift_rows(dve, s, mv, r, shift, pair, b):
    j = pair.buf(b)
    dve.wait_ge(s["rstd_ready"], pair.at(b))
    dve.scalar_tensor_tensor(shift[:, j], mv[:, j, :, 0], -1.0, r[:, j], ALU.mult, ALU.mult).then_inc(s["shift_ready"], 1)


def uses(pair):
    return pair.round + 1


def uses_before(pair):
    return pair.round


def previous(j):
    return (j - 1) % BUFS


def carry_wait(dve, sem, pair, b):
    wait_count(dve, sem, pair.n(b))


def gather_rows(pool, s, index, ix, q, rows, table, last_row, pair, b):
    j = pair.buf(b)
    hold(pool, s, s["loaded_s"][j], 16 * uses(pair))
    pool.tensor_copy(index[:, j], ix[:, bass.ds(q * T, T)]).then_inc(s["index_ready"], 1)
    hold(pool, s, s["index_ready"], pair.at(b))
    for t in range(T):
        pool.indirect_dma_start(out=rows[:, j, t], out_offset=None, in_=table,
                                in_offset=bass.IndirectOffsetOnAxis(ap=index[:, j, t:t + 1], axis=0),
                                bounds_check=last_row, oob_is_err=False).then_inc(s["gathered"][j], 16)


def chain_pass(k, tag, P, tiles, source, final):
    nc, c = k.nc, k.c
    keep = final is None
    norms = 3 if keep else 4
    units = tiles // UT
    half = UT // 2
    W = half * P
    stored = ["stored_x1", "stored_x2", "stored_h1", "stored_x3"] if keep else ["stored_out"]
    single = ["held", "u_ready", "t_ready", "x1_ready", "x1T_ready", "rstT_ready", "hidden_ready", "hT_ready", "z_ready",
              "x2_ready", "h1_ready", "t2_ready", "x3_ready", "out_ready",
              "index_ready", "found", "kept_found"]
    per_norm = [f"{n}{m}" for m in range(norms) for n in ("stats", "joined", "squared", "variance", "root", "inverse", "scale")]
    with stage(nc, tag, single + per_norm, ["loaded"] + stored) as s, ExitStack() as ctx:
        def sb(name, shape, dt=F32):
            return ctx.enter_context(nc.sbuf_tensor(f"{tag}_{name}", shape, dt))
        names = ["x", "u", "t", "x1", "t2", "x3"] + (["x2", "h1"] if keep else ["out"])
        rows = {n: sb(n, [D, 2, UT, D]) for n in names}
        stats = sb("stats", [D, 2, norms, UT, 6])
        small = {n: sb(n, [D, 2, norms, UT]) for n in ("diff", "sum", "both", "square", "both32", "var", "sd", "r", "shift")}
        rstT, hT = sb("rstT", [D, 2, 2, W]), sb("hT", [D, 2, 2, W])
        psT = [[ctx.enter_context(nc.psum_tensor(f"{tag}_psT{b}{h}", [D, CH], F32)) for h in (0, 1)] for b in (0, 1)]
        psO = [[ctx.enter_context(nc.psum_tensor(f"{tag}_psO{b}{h}", [D, CH], F32)) for h in (0, 1)] for b in (0, 1)]

        if not keep:
            index = sb("index", [D, T], I32)
            found = sb("found", [D, T, 4], I32)
        chunks = k.slots // CH

        def view(ap, g):
            if keep:
                v = ap.rearrange("(g t p) f -> g p t f", p=P, t=UT)
            else:
                v = ap.rearrange("(g p t) f -> g p t f", p=P, t=UT)
            return v[bass.ds(g, 1)].rearrange("a p t f -> (a p) t f")

        def R(name, b):
            return rows[name][0:P, b]

        def V(name, n, b):
            return small[name][0:P, b, n]

        def per_row(ap):
            return ap[0:P, 0:D].unsqueeze(1).to_broadcast([P, UT, D])

        def z_tile(b, t):
            return psO[b][t // half][0:P, (t % half) * D:(t % half + 1) * D]

        def in_turns(engine, turn):
            pairs, odd = units // 2, units % 2
            turn(0, (0, 1), (), ())
            turn(1, (0, 1), (0, 1), ())
            turn(2, (0, 1), (0, 1), (0, 1))
            with engine.Fori(3, pairs) as i:
                turn(i, (0, 1), (0, 1), (0, 1))
            if odd:
                turn(pairs, (0,), (0, 1), (0, 1))
                turn(pairs + 1, (), (0,), (0, 1))
                turn(pairs + 2, (), (), (0,))
            else:
                turn(pairs, (), (0, 1), (0, 1))
                turn(pairs + 1, (), (), (0, 1))
        block = ctx.enter_context(nc.Block())

        @block.sync
        def _(sp):
            def load(i, b):
                sp.dma_start(R("x", b), view(source, 2 * i + b)).then_inc(s["loaded"][b], 16)

            def store(i, b, ready, name, sem, to):
                hold(sp, s, s[ready], 2 * i + b + 1)
                sp.dma_start(view(to, 2 * i + b), R(name, b)).then_inc(s[sem][b], 16)
            pairs, odd = units // 2, units % 2

            def turn(i, front, back, older, more=(0, 1)):
                for b in more:
                    hold(sp, s, s["t_ready"], 2 * i + b + 1)
                    load(i + 1, b)
                for b in older:
                    if keep:
                        store(i - 2, b, "x3_ready", "x3", "stored_x3", k.s[3])
                    else:
                        store(i - 2, b, "out_ready", "out", "stored_out", final)
                if keep:
                    for b in back:
                        store(i - 1, b, "x2_ready", "x2", "stored_x2", k.s[2])
                        store(i - 1, b, "h1_ready", "h1", "stored_h1", k.sh)
                    for b in front:
                        store(i, b, "x1_ready", "x1", "stored_x1", k.s[1])
            for b in (0, 1):
                load(0, b)
            turn(0, (0, 1), (), ())
            turn(1, (0, 1), (0, 1), ())
            with sp.Fori(2, pairs - 1) as i:
                turn(i, (0, 1), (0, 1), (0, 1))
            turn(pairs - 1, (0, 1), (0, 1), (0, 1), more=(0,) if odd else ())
            if odd:
                turn(pairs, (0,), (0, 1), (0, 1), more=())
                turn(pairs + 1, (), (0,), (0, 1), more=())
                turn(pairs + 2, (), (), (0,), more=())
            else:
                turn(pairs, (), (0, 1), (0, 1), more=())
                turn(pairs + 1, (), (), (0, 1), more=())
            for n in stored:
                sp.wait_ge(s[n][0], 16 * (pairs + odd))
                sp.wait_ge(s[n][1], 16 * pairs)

        @block.vector
        def _(dve):
            def statistics(j, b, n, tile):
                for t in range(UT):
                    last = dve.bn_stats(stats[0:P, b, n, t], tile(t))
                last.then_inc(s[f"stats{n}"], 1)

            def inverse(j, b, n, shift):
                dve.wait_ge(s[f"root{n}"], 2 * j + b + 1)
                dve.reciprocal(V("r", n, b), V("sd", n, b)).then_inc(s[f"inverse{n}"], 1)
                dve.wait_ge(s[f"inverse{n}"], 2 * j + b + 1)
                if shift:
                    dve.scalar_tensor_tensor(V("shift", n, b), V("sum", n, b), -0.5, V("r", n, b), ALU.mult, ALU.mult).then_inc(s[f"scale{n}"], 1)

            def last_inverses(j, older):
                for b in older:
                    inverse(j, b, norms - 1, True)

            def turn(i, front, back, older):
                j = i - 1
                for b in front:
                    dve.wait_ge(s["u_ready"], 2 * i + b + 1)
                    wait_count(dve, s["x1_ready"], 2 * j + b + 1)
                    dve.scalar_tensor_tensor(R("t", b), R("u", b), 0.0, R("x", b), ALU.max, ALU.add).then_inc(s["t_ready"], 1)
                    dve.wait_ge(s["t_ready"], 2 * i + b + 1)
                    statistics(i, b, 0, lambda t: rows["t"][0:P, b, t])
                    if b == 0:
                        last_inverses(i - 2, older)
                if not front:
                    last_inverses(i - 2, older)
                for b in back:
                    dve.wait_ge(s["z_ready"], 2 * j + b + 1)
                    statistics(j, b, 1, lambda t: z_tile(b, t))
                for b in (0, 1):
                    if b in front:
                        inverse(i, b, 0, True)
                    if keep and b in back:
                        inverse(j, b, 1, True)
                for b in back:
                    if keep:
                        dve.wait_ge(s["scale1"], 2 * j + b + 1)
                        wait_count(dve, s["stored_x2"][b], 16 * j)
                        wait_count(dve, s["h1_ready"], 2 * (j - 1) + b + 1)
                        for t in range(UT):
                            last = dve.tensor_scalar(rows["x2"][0:P, b, t], z_tile(b, t), V("r", 1, b)[:, t:t + 1],
                                                     V("shift", 1, b)[:, t:t + 1], ALU.mult, ALU.add)
                        last.then_inc(s["x2_ready"], 1)
                        dve.wait_ge(s["x2_ready"], 2 * j + b + 1)
                        wait_count(dve, s["x3_ready"], 2 * (j - 1) + b + 1)
                        last = dve.scalar_tensor_tensor(R("t2", b), R("x2", b), 2.0, per_row(k.conv_c), ALU.mult, ALU.add)
                    else:
                        inverse(j, b, 1, False)
                        for t in range(UT):
                            last = dve.scalar_tensor_tensor(rows["t2"][0:P, b, t], z_tile(b, t), V("r", 1, b)[:, t:t + 1],
                                                            k.conv_c[0:P, 0:D], ALU.mult, ALU.add)
                    last.then_inc(s["t2_ready"], 1)
                    dve.wait_ge(s["t2_ready"], 2 * j + b + 1)
                    statistics(j, b, 2, lambda t: rows["t2"][0:P, b, t])
                for b in back:
                    if keep:
                        continue
                    inverse(j, b, 2, False)
                    wait_count(dve, s["out_ready"], 2 * (j - 1) + b + 1)
                    for t in range(UT):
                        last = dve.scalar_tensor_tensor(rows["x3"][0:P, b, t], rows["t2"][0:P, b, t], V("r", 2, b)[:, t:t + 1],
                                                        k.elu_c[0:P, 0:D], ALU.mult, ALU.add)
                    last.then_inc(s["x3_ready"], 1)
                    dve.wait_ge(s["x3_ready"], 2 * j + b + 1)
                    statistics(j, b, 3, lambda t: rows["x3"][0:P, b, t])
            in_turns(dve, turn)

        @block.gpsimd
        def _(pool):
            def add_bias(i, b):
                hold(pool, s, s["loaded"][b], 16 * (i + 1))
                if not isinstance(i, int) or i > 0:
                    hold(pool, s, s["t_ready"], 2 * (i - 1) + b + 1)
                pool.tensor_tensor(R("u", b), R("x", b), per_row(c["b_p"]), ALU.add).then_inc(s["u_ready"], 1)

            def variance(j, b, n, need_sum):
                st = stats[0:P, b, n]
                at = 2 * j + b + 1
                hold(pool, s, s[f"stats{n}"], at)
                if need_sum:
                    pool.tensor_tensor(V("sum", n, b), st[:, :, 1], st[:, :, 4], ALU.add)
                pool.tensor_tensor(V("diff", n, b), st[:, :, 1], st[:, :, 4], ALU.subtract)
                pool.tensor_tensor(V("both", n, b), st[:, :, 2], st[:, :, 5], ALU.add).then_inc(s[f"joined{n}"], 1)
                hold(pool, s, s[f"joined{n}"], at)
                pool.tensor_tensor(V("square", n, b), V("diff", n, b), V("diff", n, b), ALU.mult)
                pool.tensor_scalar(V("both32", n, b), V("both", n, b), 1.0 / 32, None, ALU.mult).then_inc(s[f"squared{n}"], 1)
                hold(pool, s, s[f"squared{n}"], at)
                pool.tensor_tensor(V("var", n, b), V("square", n, b), V("both32", n, b), ALU.add).then_inc(s[f"variance{n}"], 1)

            def start_gathers(i):
                hold_count(pool, s, s["found"], 16 * T * i)
                pool.tensor_copy(index[:], k.src_ix[:, bass.ds(i * T, T)]).then_inc(s["index_ready"], 1)
                hold(pool, s, s["index_ready"], i + 1)

            def find_tile(i, t):
                pool.indirect_dma_start(out=found[:, t], out_offset=None, in_=k.table,
                                        in_offset=bass.IndirectOffsetOnAxis(ap=index[:, t:t + 1], axis=0),
                                        bounds_check=k.table_a * TABLE_W - 1, oob_is_err=False).then_inc(s["found"], 16)

            def keep_found(i):
                hold(pool, s, s["found"], 16 * T * (i + 1))
                pool.tensor_copy(k.found[:, bass.ds(i * T, T)], found[:]).then_inc(s["kept_found"], 1)

            def turn(i, front, back, more=(0, 1)):
                j = i - 1
                gathers = []
                if not keep and (not isinstance(i, int) or i < chunks):
                    gathers = [lambda t=t: find_tile(i, t) for t in range(T)]

                def gather(n):
                    for _ in range(min(n, len(gathers))):
                        gathers.pop(0)()
                any_gathers = bool(gathers)
                for b in front:
                    variance(i, b, 0, True)
                for b in back:
                    variance(j, b, 1, keep)
                if any_gathers:
                    start_gathers(i)
                for b in (0, 1):
                    if b in more:
                        add_bias(i + 1, b)
                    if b in back:
                        if keep:
                            hold(pool, s, s["x2_ready"], 2 * j + b + 1)
                            if not isinstance(j, int) or j > 0:
                                hold(pool, s, s["stored_h1"][b], 16 * j)
                            pool.tensor_tensor(R("h1", b), R("x2", b), per_row(k.conv_c1), ALU.add).then_inc(s["h1_ready"], 1)
                        variance(j, b, 2, keep)
                gather(3)
                for b in back:
                    if not keep:
                        variance(j, b, 3, True)
                    gather(3)
                gather(3 * T)
                if any_gathers:
                    keep_found(i)
            pairs, odd = units // 2, units % 2
            for b in (0, 1):
                add_bias(0, b)
            turn(0, (0, 1), ())
            turn(1, (0, 1), (0, 1))
            with pool.Fori(2, pairs - 1) as i:
                turn(i, (0, 1), (0, 1))
            turn(pairs - 1, (0, 1), (0, 1), more=(0,) if odd else ())
            if odd:
                turn(pairs, (0,), (0, 1), more=())
                turn(pairs + 1, (), (0,), more=())
            else:
                turn(pairs, (), (0, 1), more=())

        @block.scalar
        def _(act):
            def root(j, b, n):
                act.wait_ge(s[f"variance{n}"], 2 * j + b + 1)
                halved = n == 1 and not keep
                act.activation(V("sd", n, b), V("var", n, b), ACT.Sqrt, bias=(k.eps_quarter if halved else k.eps_ln)[0:P, 0:1],
                               scale=1.0 / 16 if halved else 0.25).then_inc(s[f"root{n}"], 1)

            def apply(j, b, n, name, tile, ready):
                act.wait_ge(s[f"scale{n}"], 2 * j + b + 1)
                for t in range(UT):
                    last = act.activation(rows[name][0:P, b, t], tile(t), ACT.Identity, bias=V("shift", n, b)[:, t:t + 1],
                                          scale=V("r", n, b)[:, t:t + 1])
                last.then_inc(s[ready], 1)

            def apply_x3(j, b):
                if keep:
                    wait_count(act, s["stored_x3"][b], 16 * j)
                    apply(j, b, 2, "x3", lambda t: rows["t2"][0:P, b, t], "x3_ready")

            def turn(i, front, back, older):
                j = i - 1
                if not keep:
                    for b in older:
                        wait_count(act, s["stored_out"][b], 16 * (i - 2))
                        apply(i - 2, b, 3, "out", lambda t: rows["x3"][0:P, b, t], "out_ready")
                for b in front:
                    root(i, b, 0)
                for b in back:
                    root(j, b, 1)
                for b in (0, 1):
                    if b in front:
                        wait_count(act, s["z_ready"], 2 * j + b + 1)
                        if keep:
                            wait_count(act, s["stored_x1"][b], 16 * i)
                        apply(i, b, 0, "x1", lambda t: rows["t"][0:P, b, t], "x1_ready")
                for b in (0, 1):
                    if b in front:
                        act.wait_ge(s["x1T_ready"], 2 * i + b + 1)
                        for h in (0, 1):
                            last = act.activation(rstT[:, b, h], psT[b][h][:, 0:W], ACT.Copy, scale=k.one_eps[:, 0:1])
                        last.then_inc(s["rstT_ready"], 1)
                    if b in back and not keep:
                        root(j, b, 2)
                if 0 in older:
                    apply_x3(i - 2, 0)
                for b in (0, 1):
                    if b in front:
                        act.wait_ge(s["hidden_ready"], 2 * i + b + 1)
                        for h in (0, 1):
                            last = act.activation(hT[:, b, h], psT[b][h][:, 0:W], ACT.Relu, bias=c["b_1"][:, 0:1])
                        last.then_inc(s["hT_ready"], 1)
                    if b in back and not keep:
                        root(j, b, 3)
                if 1 in older:
                    apply_x3(i - 2, 1)
                if keep:
                    for b in back:
                        root(j, b, 2)
            in_turns(act, turn)

        @block.tensor
        def _(pe):
            def turn(i, front, back, older):
                j = i - 1
                for b in front:
                    pe.wait_ge(s["x1_ready"], 2 * i + b + 1)
                    for t in range(UT):
                        last = pe.transpose(psT[b][t // half][:, (t % half) * P:(t % half + 1) * P], rows["x1"][0:P, b, t], c["identity"][0:P, 0:P])
                    last.then_inc(s["x1T_ready"], 1)
                for b in front:
                    pe.wait_ge(s["rstT_ready"], 2 * i + b + 1)
                    for h in (0, 1):
                        last = pe.matmul(psT[b][h][:, 0:W], c["L1_gnn_W1"][:], rstT[:, b, h], start=True, stop=True)
                    last.then_inc(s["hidden_ready"], 1)
                for b in front:
                    wait_count(pe, s["x2_ready" if keep else "t2_ready"], 2 * j + b + 1)
                    for h in (0, 1):
                        pe.matmul(psO[b][h][0:P], c["ones"][0:1, 0:P], c["b_2"][0:1, :], start=True, stop=False, skip_group_check=True)
                        pe.matmul(psO[b][h][0:P], c["identity"][0:P, 0:P], rows["x1"][0:P, b, h * half:(h + 1) * half].rearrange("p t f -> p (t f)"),
                                  start=False, stop=False, skip_group_check=True)
                    pe.wait_ge(s["hT_ready"], 2 * i + b + 1)
                    for t in range(UT):
                        last = pe.matmul(z_tile(b, t), hT[:, b, t // half, (t % half) * P:(t % half + 1) * P], c["L1_gnn_W2"][:],
                                         start=False, stop=(t % half == half - 1), skip_group_check=True)
                    last.then_inc(s["z_ready"], 1)
            in_turns(pe, turn)


def attention0_scores(k):
    nc, c = k.nc, k.c
    pairs = k.pairs
    single = ["held", "bounded", "power", "weight", "rowsT_ready", "srcT_ready", "dstT_ready", "query_ready", "product_ready",
              "score_ready", "score_sb_ready", "low_ready", "max_ready", "start"]
    with stage(nc, "a0", single, ["loaded", "stored_T"]) as s, ExitStack() as ctx:
        def sb(name, shape, dt=F32):
            return ctx.enter_context(nc.sbuf_tensor(f"a0_{name}", shape, dt))

        def bank(name):
            return [ctx.enter_context(nc.psum_tensor(f"a0_{name}{b}", [D, CH], F32)) for b in (0, 1)]
        bounded, power, neg_half = (sb(n, [D, 2, k.tiles]) for n in ("bounded", "power", "neg_half"))
        weight = sb("weight", [D, k.tiles])
        src, dst = sb("src", [D, 2, T, D]), sb("dst", [D, 2, T, D])
        srcT, dstT = sb("srcT", [D, 2, CH]), sb("dstT", [D, 2, CH])
        product, score = sb("product", [D, 2, CH]), sb("score", [D, 2, CH])
        low, top = sb("low", [D, 2, CH]), sb("top", [D, 2, CH])
        psS, psD, psQ, psC = bank("psS"), bank("psD"), bank("psQ"), bank("psC")
        block = ctx.enter_context(nc.Block())

        @block.gpsimd
        def _(pool):
            pool.wait_ge(s["bounded"], 1)
            pool.tensor_tensor(power[:], bounded[:], neg_half[:], ALU.pow).then_inc(s["power"], 1)

        @block.sync
        def _(sp):
            def load(i, b):
                sp.dma_start(src[:, b], chunk(k.s[0], 2 * i + b)).then_inc(s["loaded"][b], 16)
                sp.dma_start(dst[:, b], chunk(k.d[0], 2 * i + b)).then_inc(s["loaded"][b], 16)

            def body(i, more):
                for b in (0, 1):
                    if more:
                        hold(sp, s, s["rowsT_ready"], 2 * i + b + 1)
                        load(i + 1, b)
                for b in (0, 1):
                    n = 2 * i + b
                    hold(sp, s, s["srcT_ready"], n + 1)
                    sp.dma_start(columns(k.val_t, n), srcT[:, b]).then_inc(s["stored_T"][b], 16)
                    hold(sp, s, s["score_sb_ready"], n + 1)
                    sp.dma_start(columns(k.score_t, n), score[:, b]).then_inc(s["stored_T"][b], 16)
                    hold(sp, s, s["max_ready"], n + 1)
                    sp.dma_start(columns(k.max_t, n), top[:, b]).then_inc(s["stored_T"][b], 16)
            for b in (0, 1):
                load(0, b)
            sp.dma_start(weight[:], k.args["weight_cols"]).then_inc(s["weight"], 16)
            with sp.Fori(0, pairs - 1) as i:
                body(i, True)
            body(pairs - 1, False)
            for b in (0, 1):
                sp.wait_ge(s["stored_T"][b], 48 * (pairs + 1))

        @block.tensor
        def _(pe):
            with pe.Fori(0, pairs) as i:
                for b in (0, 1):
                    pe.wait_ge(s["loaded"][b], 32 * (i + 1))
                    for t in range(T):
                        pe.transpose(psS[b][:, t * D:(t + 1) * D], src[:, b, t], c["identity"][:])
                        last = pe.transpose(psD[b][:, t * D:(t + 1) * D], dst[:, b, t], c["identity"][:])
                    last.then_inc(s["rowsT_ready"], 1)
                for b in (0, 1):
                    pe.wait_ge(s["dstT_ready"], 2 * i + b + 1)
                    pe.matmul(psQ[b][:], k.att0[:], dstT[:, b], start=True, stop=True).then_inc(s["query_ready"], 1)
                for b in (0, 1):
                    pe.wait_ge(s["product_ready"], 2 * i + b + 1)
                    pe.matmul(psC[b][:], c["score_block"][:], product[:, b], start=True, stop=True).then_inc(s["score_ready"], 1)

        @block.scalar
        def _(act):
            for b in (0, 1):
                act.sem_inc(s["stored_T"][b], 48)
            with act.Fori(0, pairs) as i:
                for b in (0, 1):
                    act.wait_ge(s["rowsT_ready"], 2 * i + b + 1)
                    act.activation(dstT[:, b], psD[b][:], ACT.Copy).then_inc(s["dstT_ready"], 1)
                    act.wait_ge(s["stored_T"][b], 48 * (i + 1))
                    act.activation(srcT[:, b], psS[b][:], ACT.Copy).then_inc(s["srcT_ready"], 1)
                for b in (0, 1):
                    act.wait_ge(s["score_ready"], 2 * i + b + 1)
                    act.activation(score[:, b], psC[b][:], ACT.Copy).then_inc(s["score_sb_ready"], 1)

        @block.vector
        def _(dve):
            dve.memset(neg_half[:], -0.5)
            dve.tensor_scalar(bounded[:, 1], k.in_norm[:], 1.0, None, ALU.max)
            dve.tensor_scalar(bounded[:, 0], k.found[:, :, DEGREE], 1.0, None, ALU.max).then_inc(s["bounded"], 1)
            dve.memset(top[:, 1, CH - 1:CH], 0.0).then_inc(s["start"], 1)
            dve.wait_ge(s["start"], 1)
            with dve.Fori(0, pairs) as i:
                for b in (0, 1):
                    dve.tensor_scalar(low[:, b], k.same[:, bass.ds((2 * i + b) * CH, CH)], -1.0, -LOW, ALU.add, ALU.mult).then_inc(s["low_ready"], 1)
                    dve.wait_ge(s["query_ready"], 2 * i + b + 1)
                    dve.wait_ge(s["srcT_ready"], 2 * i + b + 1)
                    dve.tensor_tensor(product[:, b], psQ[b][:], srcT[:, b], ALU.mult).then_inc(s["product_ready"], 1)
                for b in (0, 1):
                    dve.wait_ge(s["low_ready"], 2 * i + b + 1)
                    dve.wait_ge(s["stored_T"][b], 48 * (i + 1))
                    dve.wait_ge(s["score_sb_ready"], 2 * i + b + 1)
                    if b == 1:
                        dve.wait_ge(s["max_ready"], 2 * i + 1)
                    dve.tensor_tensor_scan(top[:, b], low[:, b], score[:, b], top[:, 1 - b, CH - 1:CH], ALU.add, ALU.max).then_inc(s["max_ready"], 1)
                dve.wait_ge(s["max_ready"], 2 * i + 2)
            dve.wait_ge(s["power"], 1)
            dve.wait_ge(s["weight"], 16)
            dve.tensor_copy(k.in_norm[:], power[:, 1])
            dve.tensor_tensor(k.edge_scale[:], weight[:], power[:, 0], ALU.mult)


def attention0_sum(k):
    nc, c = k.nc, k.c
    pairs = k.pairs
    single = ["held", "start", "mask_ready", "lastmax_ready", "maxheld_ready", "shifted_ready", "clipped_ready", "exp_ready", "weighted_ready",
              "den_ready", "num_ready", "agg_ready", "denb_ready", "rden_ready", "biased_ready", "scaled_ready", "u_ready",
              "t_ready", "shift_ready", "x1_ready"] + LN
    with stage(nc, "b0", single, ["loaded", "loaded_x", "stored"], BUFS) as s, ExitStack() as ctx:
        def sb(name, shape, dt=F32):
            return ctx.enter_context(nc.sbuf_tensor(f"b0_{name}", shape, dt))

        def bank(name, n=CH):
            return [ctx.enter_context(nc.psum_tensor(f"b0_{name}{b}", [D, n], F32)) for b in range(BUFS)]
        valT, score, top, lastmax, maxheld, shifted, expo, weighted, num, den = (
            sb(n, [D, BUFS, CH]) for n in ("valT", "score", "top", "lastmax_clipped", "maxheld", "shifted_u", "expo_scaled", "weighted_t", "num", "den"))
        clipped, u, scaled, t_ = lastmax, shifted, expo, weighted
        x, biased, x1 = (sb(n, [D, BUFS, T, D]) for n in ("x", "biased", "x1"))
        mask = sb("mask", [D, BUFS, CH], BF16)
        denb, rden = sb("denb", [D, BUFS, T]), sb("rden", [D, BUFS, T])
        stats, mv = sb("stats", [D, BUFS, T, 6]), sb("mv", [D, BUFS, T, 2])
        var_eps, r, shift = (sb(n, [D, BUFS, T]) for n in ("var_eps", "r", "shift"))
        psA, psN = bank("psA"), bank("psN", T)
        block = ctx.enter_context(nc.Block())

        def tile(buf, j, t):
            return buf[:, j, t * D:(t + 1) * D]

        def q(pair, b):
            return (2 * pairs - 1) - pair.n(b)

        @block.sync
        def _(sp):
            def load(pair, b):
                j = pair.buf(b)
                sp.dma_start(valT[:, j], columns(k.val_t, q(pair, b))).then_inc(s["loaded"][j], 16)
                sp.dma_start(score[:, j], columns(k.score_t, q(pair, b))).then_inc(s["loaded"][j], 16)
                sp.dma_start(top[:, j], columns(k.max_t, q(pair, b))).then_inc(s["loaded"][j], 16)

            def turn(loading, gathering, front, back, older):
                for b in (0, 1):
                    if front:
                        hold_count(sp, s, s["t_ready"], front.before().at(b))
                        sp.dma_start(x[:, front.buf(b)], chunk(k.d[0], q(front, b))).then_inc(s["loaded_x"][front.buf(b)], 16)
                for b in (0, 1):
                    if older:
                        hold(sp, s, s["x1_ready"], older.at(b))
                        sp.dma_start(chunk(k.d[1], q(older, b)), x1[:, older.buf(b)]).then_inc(s["stored"][older.buf(b)], 16)
                for b in (0, 1):
                    if loading:
                        hold(sp, s, s["weighted_ready"], front.at(b))
                        load(loading, b)
            for parity in (0, 1):
                for b in (0, 1):
                    load(Pair(0, parity), b)
            turns(sp, pairs, turn)
            for j in range(BUFS):
                sp.wait_ge(s["stored"][j], 16 * ((2 * pairs - 1 - j) // BUFS + 1))

        @block.scalar
        def _(act):
            def load_mask(pair, b):
                act.activation(mask[:, pair.buf(b)], k.same[:, bass.ds(q(pair, b) * CH + 1, CH)], ACT.Copy).then_inc(s["mask_ready"], 1)

            def turn(loading, gathering, front, back, older):
                for b in (0, 1):
                    if older:
                        j = older.buf(b)
                        act.wait_ge(s["shift_ready"], older.at(b))
                        wait_count(act, s["stored"][j], 16 * uses_before(older))
                        for t in range(T):
                            last = act.activation(x1[:, j, t], tile(t_, j, t), ACT.Identity, bias=shift[:, j, t:t + 1], scale=r[:, j, t:t + 1])
                        last.then_inc(s["x1_ready"], 1)
                for b in (0, 1):
                    if front:
                        j = front.buf(b)
                        act.wait_ge(s["clipped_ready"], front.at(b))
                        act.activation(expo[:, j], clipped[:, j], ACT.Exp).then_inc(s["exp_ready"], 1)
                for b in (0, 1):
                    if back:
                        j = back.buf(b)
                        act.wait_ge(s["rden_ready"], back.at(b))
                        for t in range(T):
                            last = act.activation(tile(scaled, j, t), psA[j][:, t * D:(t + 1) * D], ACT.Copy, scale=rden[:, j, t:t + 1])
                        last.then_inc(s["scaled_ready"], 1)
                for b in (0, 1):
                    if gathering:
                        wait_count(act, s["num_ready"], gathering.before().at(b))
                        load_mask(gathering, b)
            for b in (0, 1):
                load_mask(Pair(0, 0), b)
            turns(act, pairs, turn)

        @block.gpsimd
        def _(pool):
            def turn(loading, gathering, front, back, older):
                for b in (0, 1):
                    if front:
                        j = front.buf(b)
                        hold(pool, s, s["exp_ready"], front.at(b))
                        hold_count(pool, s, s["x1_ready"], front.before().at(b))
                        pool.tensor_tensor(weighted[:, j], expo[:, j], valT[:, j], ALU.mult).then_inc(s["weighted_ready"], 1)
                for b in (0, 1):
                    if back:
                        j = back.buf(b)
                        rstd(pool, s, k, D, mv[:, j], var_eps[:, j], r[:, j], back.n(b))
                for b in (0, 1):
                    if front:
                        j = front.buf(b)
                        hold(pool, s, s["loaded_x"][j], 16 * uses(front))
                        hold_count(pool, s, s["u_ready"], front.before().at(b))
                        pool.tensor_tensor(flat(biased, j), flat(x, j), c["b_p"][:], ALU.add).then_inc(s["biased_ready"], 1)
            turns(pool, pairs, turn)

        @block.tensor
        def _(pe):
            def turn(loading, gathering, front, back, older):
                for b in (0, 1):
                    if back:
                        j = back.buf(b)
                        wait_count(pe, s["u_ready"], back.before().at(b))
                        pe.wait_ge(s["den_ready"], back.at(b))
                        for t in range(T):
                            pe.matmul(psN[j][:, t:t + 1], tile(den, j, t), c["first_row"][:], start=True, stop=True, skip_group_check=True)
                for b in (0, 1):
                    if back:
                        j = back.buf(b)
                        pe.wait_ge(s["num_ready"], back.at(b))
                        for t in range(T):
                            last = pe.matmul(psA[j][:, t * D:(t + 1) * D], tile(num, j, t), k.val0[:], start=True, stop=True, skip_group_check=True)
                        last.then_inc(s["agg_ready"], 1)
            turns(pe, pairs, turn)

        @block.vector
        def _(dve):
            for buf in (maxheld, num, den):
                dve.memset(buf[:, BUFS - 1, 0:1], 0.0).then_inc(s["start"], 1)
            dve.wait_ge(s["start"], 3)

            def scan(buf, j, data, sem, pair, b, op):
                carry_wait(dve, s[sem], pair, b)
                dve.tensor_tensor_scan(buf[:, j, ::-1], mask[:, j, ::-1], data[:, j, ::-1], buf[:, previous(j), 0:1], ALU.mult, op).then_inc(s[sem], 1)

            def turn(loading, gathering, front, back, older):
                both = (0, 1)
                if front:
                    for b in both:
                        j = front.buf(b)
                        dve.wait_ge(s["mask_ready"], front.at(b))
                        dve.wait_ge(s["loaded"][j], 48 * uses(front))
                        dve.scalar_tensor_tensor(lastmax[:, j], mask[:, j], -1.0, top[:, j], ALU.add, ALU.mult).then_inc(s["lastmax_ready"], 1)
                if older:
                    for b in both:
                        shift_rows(dve, s, mv, r, shift, older, b)
                if front:
                    for b in both:
                        dve.wait_ge(s["lastmax_ready"], front.at(b))
                        scan(maxheld, front.buf(b), lastmax, "maxheld_ready", front, b, ALU.subtract)
                    for b in both:
                        j = front.buf(b)
                        dve.wait_ge(s["maxheld_ready"], front.at(b))
                        dve.tensor_tensor(shifted[:, j], score[:, j], maxheld[:, j], ALU.subtract).then_inc(s["shifted_ready"], 1)
                if front:
                    for b in both:
                        j = front.buf(b)
                        dve.wait_ge(s["shifted_ready"], front.at(b))
                        dve.tensor_scalar(clipped[:, j], shifted[:, j], -50.0, 50.0, ALU.max, ALU.min).then_inc(s["clipped_ready"], 1)
                if back:
                    for b in both:
                        j = back.buf(b)
                        dve.wait_ge(s["agg_ready"], back.at(b))
                        dve.tensor_scalar(denb[:, j], psN[j][:], 1e-9, None, ALU.add).then_inc(s["denb_ready"], 1)
                    for b in both:
                        j = back.buf(b)
                        dve.wait_ge(s["denb_ready"], back.at(b))
                        dve.reciprocal(rden[:, j], denb[:, j]).then_inc(s["rden_ready"], 1)
                if front:
                    for b in both:
                        dve.wait_ge(s["exp_ready"], front.at(b))
                        scan(den, front.buf(b), expo, "den_ready", front, b, ALU.add)
                if back:
                    for b in both:
                        j = back.buf(b)
                        dve.wait_ge(s["scaled_ready"], back.at(b))
                        dve.wait_ge(s["biased_ready"], back.at(b))
                        dve.tensor_tensor(u[:, j], scaled[:, j], flat(biased, j), ALU.add).then_inc(s["u_ready"], 1)
                    for b in both:
                        j = back.buf(b)
                        dve.wait_ge(s["u_ready"], back.at(b))
                        dve.scalar_tensor_tensor(t_[:, j], u[:, j], 0.0, flat(x, j), ALU.max, ALU.add).then_inc(s["t_ready"], 1)
                    for b in both:
                        j = back.buf(b)
                        dve.wait_ge(s["t_ready"], back.at(b))
                        moments(dve, s, t_[:, j].rearrange("p (t f) -> p t f", t=T), stats[:, j], mv[:, j], back.n(b))
                if front:
                    for b in both:
                        dve.wait_ge(s["weighted_ready"], front.at(b))
                        scan(num, front.buf(b), weighted, "num_ready", front, b, ALU.add)
            turns(dve, pairs, turn)


def edge_mlp(k):
    nc, c = k.nc, k.c
    pairs = k.pairs
    single = ["held", "start", "index_ready", "rowsT_ready", "srcT_ready", "firstrow_ready", "dstheld_ready", "biased_ready",
              "message_ready", "relu_ready", "sum_ready", "rst_ready", "hidden_ready", "hT_ready", "z_ready", "x2_ready"] + LN
    with stage(nc, "l1", single, ["loaded_s", "loaded_d", "gathered", "stored"], BUFS) as s, ExitStack() as ctx:
        def sb(name, shape, dt=F32):
            return ctx.enter_context(nc.sbuf_tensor(f"l1_{name}", shape, dt))

        def bank(name):
            return [ctx.enter_context(nc.psum_tensor(f"l1_{name}{b}", [D, CH], F32)) for b in range(BUFS)]
        index = sb("index", [D, BUFS, T], I32)
        src, dst, x2 = (sb(n, [D, BUFS, T, D]) for n in ("src", "dst", "x2"))
        srcT, firstrow, dstheld, biased, message, neigh, rst, hT = (
            sb(n, [D, BUFS, CH]) for n in ("srcT", "firstrow", "dstheld", "biased", "message", "neigh", "rst", "hT"))
        stats, mv = sb("stats", [D, BUFS, T, 6]), sb("mv", [D, BUFS, T, 2])
        var_eps, r = sb("var_eps", [D, BUFS, T]), sb("r", [D, BUFS, T])
        psM = bank("psM")
        psO = bank("psO")
        block = ctx.enter_context(nc.Block())

        @block.sync
        def _(sp):
            def load(pair, b):
                j = pair.buf(b)
                sp.dma_start(src[:, j], chunk(k.s[1], pair.n(b))).then_inc(s["loaded_s"][j], 16)
                sp.dma_start(dst[:, j], chunk(k.d[1], pair.n(b))).then_inc(s["loaded_d"][j], 16)

            def turn(loading, gathering, front, back, older):
                for b in (0, 1):
                    if loading:
                        hold(sp, s, s["rowsT_ready"], front.at(b))
                        load(loading, b)
                for b in (0, 1):
                    if back:
                        hold(sp, s, s["x2_ready"], back.at(b))
                        sp.dma_start(chunk(k.d[2], back.n(b)), x2[:, back.buf(b)]).then_inc(s["stored"][back.buf(b)], 16)
            for parity in (0, 1):
                for b in (0, 1):
                    load(Pair(0, parity), b)
            turns(sp, pairs, turn)
            for j in range(BUFS):
                sp.wait_ge(s["stored"][j], 16 * ((2 * pairs - 1 - j) // BUFS + 1))

        @block.gpsimd
        def _(pool):
            def gather(pair, b):
                gather_rows(pool, s, index, k.found[:, :, FIRST], pair.n(b), src, k.d[1], k.slots - 1, pair, b)

            def turn(loading, gathering, front, back, older):
                for b in (0, 1):
                    if gathering:
                        gather(gathering, b)
                for b in (0, 1):
                    if back:
                        j = back.buf(b)
                        rstd(pool, s, k, D, mv[:, j], var_eps[:, j], r[:, j], back.n(b))
            for b in (0, 1):
                gather(Pair(0, 0), b)
            turns(pool, pairs, turn)

        @block.tensor
        def _(pe):
            def turn(loading, gathering, front, back, older):
                if front:
                    for b in (0, 1):
                        j = front.buf(b)
                        wait_count(pe, s["x2_ready"], front.before().at(b))
                        pe.wait_ge(s["gathered"][j], 16 * T * uses(front))
                        pe.wait_ge(s["loaded_d"][j], 16 * uses(front))
                        for t in range(T):
                            pe.transpose(psO[j][:, t * D:(t + 1) * D], dst[:, j, t], c["identity"][:])
                            last = pe.transpose(psM[j][:, t * D:(t + 1) * D], src[:, j, t], c["identity"][:])
                        last.then_inc(s["rowsT_ready"], 1)
                if back:
                    for b in (0, 1):
                        j = back.buf(b)
                        pe.wait_ge(s["rst_ready"], back.at(b))
                        pe.matmul(psM[j][:], c["L1_gnn_W1"][:], rst[:, j], start=True, stop=True).then_inc(s["hidden_ready"], 1)
                    for b in (0, 1):
                        j = back.buf(b)
                        pe.wait_ge(s["biased_ready"], back.at(b))
                        for t in range(T):
                            at = slice(t * D, (t + 1) * D)
                            pe.matmul(psO[j][:, at], biased[:, j, at], c["identity"][:], start=(t == 0), stop=False, skip_group_check=True)
                        pe.wait_ge(s["hT_ready"], back.at(b))
                        for t in range(T):
                            at = slice(t * D, (t + 1) * D)
                            last = pe.matmul(psO[j][:, at], hT[:, j, at], c["L1_gnn_W2"][:], start=False, stop=(t == T - 1), skip_group_check=True)
                        last.then_inc(s["z_ready"], 1)
                if front:
                    for b in (0, 1):
                        j = front.buf(b)
                        pe.wait_ge(s["srcT_ready"], front.at(b))
                        pe.matmul(psM[j][:], c["L1_Wa"][:], srcT[:, j], start=True, stop=False)
                        pe.wait_ge(s["dstheld_ready"], front.at(b))
                        pe.matmul(psM[j][:], c["L1_Wb"][:], dstheld[:, j], start=False, stop=True).then_inc(s["message_ready"], 1)
            turns(pe, pairs, turn)

        @block.scalar
        def _(act):
            def turn(loading, gathering, front, back, older):
                if front:
                    for b in (0, 1):
                        j = front.buf(b)
                        act.wait_ge(s["rowsT_ready"], front.at(b))
                        act.activation(srcT[:, j], psM[j][:], ACT.Copy).then_inc(s["srcT_ready"], 1)
                if back:
                    for b in (0, 1):
                        j = back.buf(b)
                        act.wait_ge(s["hidden_ready"], back.at(b))
                        act.activation(hT[:, j], psM[j][:], ACT.Relu, bias=c["b_1"][:, 0:1]).then_inc(s["hT_ready"], 1)
                if front:
                    for b in (0, 1):
                        j = front.buf(b)
                        act.wait_ge(s["dstheld_ready"], front.at(b))
                        act.activation(biased[:, j], dstheld[:, j], ACT.Identity, bias=c["b_2_col"][:, 0:1]).then_inc(s["biased_ready"], 1)
                    for b in (0, 1):
                        j = front.buf(b)
                        act.wait_ge(s["message_ready"], front.at(b))
                        act.activation(message[:, j], psM[j][:], ACT.Relu, bias=c["b_edge"][:, 0:1]).then_inc(s["relu_ready"], 1)
            turns(act, pairs, turn)

        @block.vector
        def _(dve):
            for buf in (dstheld, neigh):
                dve.memset(buf[:, BUFS - 1, CH - 1:CH], 0.0).then_inc(s["start"], 1)
            dve.wait_ge(s["start"], 2)

            def same(pair, b):
                return k.same[:, bass.ds(pair.n(b) * CH, CH)]

            def z(j):
                return psO[j][:].rearrange("p (t f) -> p t f", t=T)

            def turn(loading, gathering, front, back, older):
                if front:
                    for b in (0, 1):
                        j = front.buf(b)
                        dve.wait_ge(s["rowsT_ready"], front.at(b))
                        dve.scalar_tensor_tensor(firstrow[:, j], same(front, b), -1.0, psO[j][:], ALU.add, ALU.mult).then_inc(s["firstrow_ready"], 1)
                    for b in (0, 1):
                        j = front.buf(b)
                        dve.wait_ge(s["firstrow_ready"], front.at(b))
                        carry_wait(dve, s["dstheld_ready"], front, b)
                        dve.tensor_tensor_scan(dstheld[:, j], same(front, b), firstrow[:, j], dstheld[:, previous(j), CH - 1:CH],
                                               ALU.mult, ALU.subtract).then_inc(s["dstheld_ready"], 1)
                if back:
                    for b in (0, 1):
                        j = back.buf(b)
                        dve.wait_ge(s["z_ready"], back.at(b))
                        moments(dve, s, z(j), stats[:, j], mv[:, j], back.n(b))
                for b in (0, 1):
                    if back:
                        j = back.buf(b)
                        dve.wait_ge(s["rstd_ready"], back.at(b))
                        wait_count(dve, s["stored"][j], 16 * uses_before(back))
                        normalise(dve, x2[:, j], z(j), mv[:, j], r[:, j]).then_inc(s["x2_ready"], 1)
                    if front:
                        j = front.buf(b)
                        dve.wait_ge(s["relu_ready"], front.at(b))
                        carry_wait(dve, s["sum_ready"], front, b)
                        dve.tensor_tensor_scan(neigh[:, j], same(front, b), message[:, j], neigh[:, previous(j), CH - 1:CH],
                                               ALU.mult, ALU.add).then_inc(s["sum_ready"], 1)
                    if front:
                        j = front.buf(b)
                        dve.wait_ge(s["sum_ready"], front.at(b))
                        dve.scalar_tensor_tensor(rst[:, j], dstheld[:, j], k.one_eps[:, 0:1], neigh[:, j], ALU.mult, ALU.add).then_inc(s["rst_ready"], 1)
            turns(dve, pairs, turn)


def convolution(k, tag, own, table, residual, weight, bias, out):
    nc, c = k.nc, k.c
    pairs = k.pairs
    ends = residual is not None
    single = ["held", "start", "index_ready", "weighted_ready", "rowsT_ready", "sum_ready", "product_ready", "scaled_ready", "u_ready",
              "h_ready", "t_ready", "shift_ready", "out_ready"] + LN
    with stage(nc, tag, single, ["loaded_s", "loaded_d", "gathered", "stored"], BUFS) as s, ExitStack() as ctx:
        def sb(name, shape, dt=F32):
            return ctx.enter_context(nc.sbuf_tensor(f"{tag}_{name}", shape, dt))

        def bank(name):
            return [ctx.enter_context(nc.psum_tensor(f"{tag}_{name}{b}", [D, CH], F32)) for b in range(BUFS)]
        index = sb("index", [D, BUFS, T], I32)
        src, dst, res, weighted, scaled, u, h, t_, x3 = (
            sb(n, [D, BUFS, T, D]) for n in ("src", "dst", "res", "weighted", "scaled", "u", "h", "t", "x3"))
        agg = sb("agg", [D, BUFS, CH])
        stats, mv = sb("stats", [D, BUFS, T, 6]), sb("mv", [D, BUFS, T, 2])
        var_eps, r, shift = (sb(n, [D, BUFS, T]) for n in ("var_eps", "r", "shift"))
        psS, psA = bank("psS"), bank("psA")
        final, final_ready, used = (x3, "out_ready", "t_ready") if ends else (h, "h_ready", "h_ready")
        n_d = 2 if ends else 1
        block = ctx.enter_context(nc.Block())

        @block.sync
        def _(sp):
            def load_src(pair, b):
                j = pair.buf(b)
                sp.dma_start(src[:, j], chunk(own, pair.n(b))).then_inc(s["loaded_s"][j], 16)

            def load_dst(pair, b):
                j = pair.buf(b)
                sp.dma_start(dst[:, j], chunk(table, pair.n(b))).then_inc(s["loaded_d"][j], 16)
                if ends:
                    sp.dma_start(res[:, j], chunk(residual, pair.n(b))).then_inc(s["loaded_d"][j], 16)

            def turn(loading, gathering, front, back, older):
                for b in (0, 1):
                    if loading:
                        hold(sp, s, s["weighted_ready"], front.at(b))
                        load_src(loading, b)
                for b in (0, 1):
                    if gathering:
                        hold_count(sp, s, s[used], gathering.before().at(b))
                        load_dst(gathering, b)
                done = older if ends else back
                for b in (0, 1):
                    if done:
                        hold(sp, s, s[final_ready], done.at(b))
                        sp.dma_start(chunk(out, done.n(b)), final[:, done.buf(b)]).then_inc(s["stored"][done.buf(b)], 16)
            for b in (0, 1):
                load_src(Pair(0, 0), b)
            for b in (0, 1):
                load_src(Pair(0, 1), b)
                load_dst(Pair(0, 0), b)
            turns(sp, pairs, turn)
            for j in range(BUFS):
                sp.wait_ge(s["stored"][j], 16 * ((2 * pairs - 1 - j) // BUFS + 1))

        @block.gpsimd
        def _(pool):
            def gather(pair, b):
                gather_rows(pool, s, index, k.found[:, :, LAST], pair.n(b), src, table, k.slots - 1, pair, b)

            def turn(loading, gathering, front, back, older):
                for b in (0, 1):
                    if gathering:
                        gather(gathering, b)
                for b in (0, 1):
                    if back and ends:
                        j = back.buf(b)
                        rstd(pool, s, k, D, mv[:, j], var_eps[:, j], r[:, j], back.n(b))
            for b in (0, 1):
                gather(Pair(0, 0), b)
            turns(pool, pairs, turn)

        @block.scalar
        def _(act):
            def turn(loading, gathering, front, back, older):
                if front:
                    for b in (0, 1):
                        j = front.buf(b)
                        act.wait_ge(s["gathered"][j], 16 * T * uses(front))
                        for t in range(T):
                            last = act.activation(weighted[:, j, t], src[:, j, t], ACT.Copy, scale=k.edge_scale[:, bass.ds(front.n(b) * T + t, 1)])
                        last.then_inc(s["weighted_ready"], 1)
                if back:
                    for b in (0, 1):
                        j = back.buf(b)
                        act.wait_ge(s["product_ready"], back.at(b))
                        for t in range(T):
                            last = act.activation(scaled[:, j, t], psA[j][:, t * D:(t + 1) * D], ACT.Copy, scale=k.in_norm[:, bass.ds(back.n(b) * T + t, 1)])
                        last.then_inc(s["scaled_ready"], 1)
                if older and ends:
                    for b in (0, 1):
                        j = older.buf(b)
                        act.wait_ge(s["shift_ready"], older.at(b))
                        wait_count(act, s["stored"][j], 16 * uses_before(older))
                        for t in range(T):
                            last = act.activation(x3[:, j, t], t_[:, j, t], ACT.Identity, bias=shift[:, j, t:t + 1], scale=r[:, j, t:t + 1])
                        last.then_inc(s["out_ready"], 1)
            turns(act, pairs, turn)

        @block.tensor
        def _(pe):
            def turn(loading, gathering, front, back, older):
                if back:
                    for b in (0, 1):
                        j = back.buf(b)
                        pe.wait_ge(s["sum_ready"], back.at(b))
                        for t in range(T):
                            at = slice(t * D, (t + 1) * D)
                            last = pe.matmul(psA[j][:, at], agg[:, j, at], c[weight][:], start=True, stop=True, skip_group_check=True)
                        last.then_inc(s["product_ready"], 1)
                if front:
                    for b in (0, 1):
                        j = front.buf(b)
                        pe.wait_ge(s["weighted_ready"], front.at(b))
                        for t in range(T):
                            last = pe.transpose(psS[j][:, t * D:(t + 1) * D], weighted[:, j, t], c["identity"][:])
                        last.then_inc(s["rowsT_ready"], 1)
            turns(pe, pairs, turn)

        @block.vector
        def _(dve):
            dve.memset(agg[:, BUFS - 1, CH - 1:CH], 0.0).then_inc(s["start"], 1)
            dve.wait_ge(s["start"], 1)

            def turn(loading, gathering, front, back, older):
                for b in (0, 1):
                    if older and ends:
                        shift_rows(dve, s, mv, r, shift, older, b)
                for b in (0, 1):
                    if back:
                        j = back.buf(b)
                        dve.wait_ge(s["scaled_ready"], back.at(b))
                        dve.tensor_tensor(flat(u, j), flat(scaled, j), c[bias][:], ALU.add).then_inc(s["u_ready"], 1)
                if back:
                    for b in (0, 1):
                        j = back.buf(b)
                        dve.wait_ge(s["u_ready"], back.at(b))
                        dve.wait_ge(s["loaded_d"][j], 16 * n_d * uses(back))
                        if not ends:
                            wait_count(dve, s["stored"][j], 16 * uses_before(back))
                        dve.scalar_tensor_tensor(flat(h, j), flat(u, j), 0.0, flat(dst, j), ALU.max, ALU.add).then_inc(s["h_ready"], 1)
                if back and ends:
                    for b in (0, 1):
                        j = back.buf(b)
                        dve.wait_ge(s["h_ready"], back.at(b))
                        wait_count(dve, s["out_ready"], back.before().at(b))
                        dve.tensor_tensor(flat(t_, j), flat(h, j), flat(res, j), ALU.add).then_inc(s["t_ready"], 1)
                    for b in (0, 1):
                        j = back.buf(b)
                        dve.wait_ge(s["t_ready"], back.at(b))
                        moments(dve, s, t_[:, j], stats[:, j], mv[:, j], back.n(b))
                for b in (0, 1):
                    if front:
                        j = front.buf(b)
                        dve.wait_ge(s["rowsT_ready"], front.at(b))
                        carry_wait(dve, s["sum_ready"], front, b)
                        dve.tensor_tensor_scan(agg[:, j], k.same[:, bass.ds(front.n(b) * CH, CH)], psS[j][:], agg[:, previous(j), CH - 1:CH],
                                               ALU.mult, ALU.add).then_inc(s["sum_ready"], 1)
            turns(dve, pairs, turn)


def attention3_scores(k):
    nc, c = k.nc, k.c
    pairs = k.pairs
    single = ["held", "start", "mask_ready", "index_ready", "rowsT_ready", "srcT_ready", "dstT_ready", "target_product", "source_product",
              "value_product", "value_ready", "lastrow_ready", "target_ready", "z_ready", "score_ready", "low_ready", "max_ready"]
    with stage(nc, "a3", single, ["loaded_s", "loaded_d", "gathered", "stored_value", "stored"], BUFS) as s, ExitStack() as ctx:
        def sb(name, shape, dt=F32):
            return ctx.enter_context(nc.sbuf_tensor(f"a3_{name}", shape, dt))

        def bank(name):
            return [ctx.enter_context(nc.psum_tensor(f"a3_{name}{b}", [D, CH], F32)) for b in range(BUFS)]
        index = sb("index", [D, BUFS, T], I32)
        src, dst = sb("src", [D, BUFS, T, D]), sb("dst", [D, BUFS, T, D])
        srcT, dstT, value, lastrow, target, z, score, low, top = (
            sb(n, [D, BUFS, CH]) for n in ("srcT", "dstT", "value", "lastrow", "target", "z", "score", "low", "top"))
        mask = sb("mask", [D, BUFS, CH], BF16)
        psX = bank("psX")
        psF = bank("psF")
        block = ctx.enter_context(nc.Block())

        def q(pair, b):
            return (2 * pairs - 1) - pair.n(b)

        @block.sync
        def _(sp):
            def load(pair, b):
                j = pair.buf(b)
                sp.dma_start(src[:, j], chunk(k.s[3], q(pair, b))).then_inc(s["loaded_s"][j], 16)
                sp.dma_start(dst[:, j], chunk(k.d[3], q(pair, b))).then_inc(s["loaded_d"][j], 16)

            def turn(loading, gathering, front, back, older):
                for b in (0, 1):
                    if loading:
                        hold(sp, s, s["rowsT_ready"], front.at(b))
                        load(loading, b)
                for b in (0, 1):
                    if back:
                        j = back.buf(b)
                        hold(sp, s, s["value_ready"], back.at(b))
                        sp.dma_start(columns(k.val_t, q(back, b)), value[:, j]).then_inc(s["stored_value"][j], 16)
                        hold(sp, s, s["max_ready"], back.at(b))
                        sp.dma_start(columns(k.score_t, q(back, b)), score[:, j]).then_inc(s["stored"][j], 16)
                        sp.dma_start(columns(k.max_t, q(back, b)), top[:, j]).then_inc(s["stored"][j], 16)
            for parity in (0, 1):
                for b in (0, 1):
                    load(Pair(0, parity), b)
            turns(sp, pairs, turn)
            for j in range(BUFS):
                sp.wait_ge(s["stored_value"][j], 16 * ((2 * pairs - 1 - j) // BUFS + 1))
                sp.wait_ge(s["stored"][j], 32 * ((2 * pairs - 1 - j) // BUFS + 1))

        @block.gpsimd
        def _(pool):
            def gather(pair, b):
                gather_rows(pool, s, index, k.found[:, :, LAST], q(pair, b), src, k.d[3], k.slots - 1, pair, b)

            def turn(loading, gathering, front, back, older):
                for b in (0, 1):
                    if gathering:
                        gather(gathering, b)
            for b in (0, 1):
                gather(Pair(0, 0), b)
            turns(pool, pairs, turn)

        @block.tensor
        def _(pe):
            def turn(loading, gathering, front, back, older):
                if front:
                    for b in (0, 1):
                        j = front.buf(b)
                        wait_count(pe, s["z_ready"], front.before().at(b))
                        wait_count(pe, s["value_ready"], front.before().at(b))
                        pe.wait_ge(s["gathered"][j], 16 * T * uses(front))
                        pe.wait_ge(s["loaded_d"][j], 16 * uses(front))
                        for t in range(T):
                            pe.transpose(psF[j][:, t * D:(t + 1) * D], dst[:, j, t], c["identity"][:])
                            last = pe.transpose(psX[j][:, t * D:(t + 1) * D], src[:, j, t], c["identity"][:])
                        last.then_inc(s["rowsT_ready"], 1)
                if back:
                    for b in (0, 1):
                        j = back.buf(b)
                        pe.wait_ge(s["lastrow_ready"], back.at(b))
                        pe.matmul(psF[j][:], k.att3_s[:], srcT[:, j], start=True, stop=True).then_inc(s["source_product"], 1)
                if front:
                    for b in (0, 1):
                        j = front.buf(b)
                        pe.wait_ge(s["dstT_ready"], front.at(b))
                        pe.matmul(psF[j][:], k.att3_t[:], dstT[:, j], start=True, stop=True).then_inc(s["target_product"], 1)
                    for b in (0, 1):
                        j = front.buf(b)
                        pe.wait_ge(s["srcT_ready"], front.at(b))
                        pe.matmul(psX[j][:], c["L3_gnn_kernel"][:], srcT[:, j], start=True, stop=True).then_inc(s["value_product"], 1)
            turns(pe, pairs, turn)

        @block.scalar
        def _(act):
            def load_mask(pair, b):
                act.activation(mask[:, pair.buf(b)], k.same[:, bass.ds(q(pair, b) * CH + 1, CH)], ACT.Copy).then_inc(s["mask_ready"], 1)

            def turn(loading, gathering, front, back, older):
                for b in (0, 1):
                    if front:
                        j = front.buf(b)
                        act.wait_ge(s["rowsT_ready"], front.at(b))
                        act.activation(dstT[:, j], psF[j][:], ACT.Copy).then_inc(s["dstT_ready"], 1)
                        wait_count(act, s["z_ready"], front.before().at(b))
                        act.activation(srcT[:, j], psX[j][:], ACT.Copy).then_inc(s["srcT_ready"], 1)
                for b in (0, 1):
                    if front:
                        j = front.buf(b)
                        act.wait_ge(s["value_product"], front.at(b))
                        wait_count(act, s["stored_value"][j], 16 * uses_before(front))
                        act.activation(value[:, j], psX[j][:], ACT.Copy).then_inc(s["value_ready"], 1)
                for b in (0, 1):
                    if gathering:
                        wait_count(act, s["target_ready"], gathering.before().at(b))
                        load_mask(gathering, b)
            for b in (0, 1):
                load_mask(Pair(0, 0), b)
            turns(act, pairs, turn)

        @block.vector
        def _(dve):
            for buf in (target, top):
                dve.memset(buf[:, BUFS - 1, 0:1], 0.0).then_inc(s["start"], 1)
            dve.wait_ge(s["start"], 2)

            def turn(loading, gathering, front, back, older):
                both = (0, 1)
                if back:
                    for b in both:
                        j = back.buf(b)
                        dve.wait_ge(s["mask_ready"], back.at(b))
                        dve.tensor_scalar(low[:, j], mask[:, j], -1.0, -LOW, ALU.add, ALU.mult).then_inc(s["low_ready"], 1)
                    for b in both:
                        j = back.buf(b)
                        dve.wait_ge(s["lastrow_ready"], back.at(b))
                        carry_wait(dve, s["target_ready"], back, b)
                        dve.tensor_tensor_scan(target[:, j, ::-1], mask[:, j, ::-1], lastrow[:, j, ::-1], target[:, previous(j), 0:1],
                                               ALU.mult, ALU.subtract).then_inc(s["target_ready"], 1)
                    for b in both:
                        j = back.buf(b)
                        dve.wait_ge(s["target_ready"], back.at(b))
                        dve.wait_ge(s["source_product"], back.at(b))
                        dve.tensor_tensor(z[:, j], psF[j][:], target[:, j], ALU.add).then_inc(s["z_ready"], 1)
                    for b in both:
                        j = back.buf(b)
                        dve.wait_ge(s["z_ready"], back.at(b))
                        wait_count(dve, s["stored"][j], 32 * uses_before(back))
                        dve.scalar_tensor_tensor(score[:, j], z[:, j], 0.2, z[:, j], ALU.mult, ALU.max).then_inc(s["score_ready"], 1)
                    for b in both:
                        j = back.buf(b)
                        dve.wait_ge(s["score_ready"], back.at(b))
                        dve.wait_ge(s["low_ready"], back.at(b))
                        carry_wait(dve, s["max_ready"], back, b)
                        dve.tensor_tensor_scan(top[:, j, ::-1], low[:, j, ::-1], score[:, j, ::-1], top[:, previous(j), 0:1],
                                               ALU.add, ALU.max).then_inc(s["max_ready"], 1)
                if front:
                    for b in both:
                        j = front.buf(b)
                        dve.wait_ge(s["mask_ready"], front.at(b))
                        dve.wait_ge(s["target_product"], front.at(b))
                        dve.scalar_tensor_tensor(lastrow[:, j], mask[:, j], -1.0, psF[j][:], ALU.add, ALU.mult).then_inc(s["lastrow_ready"], 1)
            turns(dve, pairs, turn)


def attention3_sum(k):
    nc, c = k.nc, k.c
    pairs = k.pairs
    single = ["held", "start", "index_ready", "firstmax_ready", "maxheld_ready", "shifted_ready", "exp_ready", "weighted_ready",
              "den_ready", "num_ready", "agg_ready", "denb_ready", "rden_ready", "scaled_ready", "y_ready", "neg_ready",
              "expm_ready", "pos_ready", "t_ready", "shift_ready", "out_ready"] + LN
    with stage(nc, "b3", single, ["loaded", "loaded_x", "scattered"], BUFS) as s, ExitStack() as ctx:
        def sb(name, shape, dt=F32):
            return ctx.enter_context(nc.sbuf_tensor(f"b3_{name}", shape, dt))

        def bank(name, n=CH):
            return [ctx.enter_context(nc.psum_tensor(f"b3_{name}{b}", [D, n], F32)) for b in range(BUFS)]
        index = sb("index", [D, BUFS, T], I32)
        valT, score, top, firstmax, maxheld, shifted, expo, weighted, num, den = (
            sb(n, [D, BUFS, CH]) for n in ("valT", "score", "top", "firstmax_scaled", "maxheld", "shifted_y", "expo_neg", "weighted_expm", "num", "den"))
        scaled, y, neg, expm = firstmax, shifted, expo, weighted
        x, t_, out = (sb(n, [D, BUFS, T, D]) for n in ("x", "t", "out"))
        denb, rden = sb("denb", [D, BUFS, T * HEADS]), sb("rden", [D, BUFS, T * HEADS])
        stats, mv = sb("stats", [D, BUFS, T, 6]), sb("mv", [D, BUFS, T, 2])
        var_eps, r, shift = (sb(n, [D, BUFS, T]) for n in ("var_eps", "r", "shift"))
        psA, psN = bank("psA"), bank("psN", T * HEADS)
        block = ctx.enter_context(nc.Block())

        def tile(buf, j, t):
            return buf[:, j, t * D:(t + 1) * D]

        @block.sync
        def _(sp):
            def load(pair, b):
                j, n = pair.buf(b), pair.n(b)
                sp.dma_start(valT[:, j], columns(k.val_t, n)).then_inc(s["loaded"][j], 16)
                sp.dma_start(score[:, j], columns(k.score_t, n)).then_inc(s["loaded"][j], 16)
                sp.dma_start(top[:, j], columns(k.max_t, n)).then_inc(s["loaded"][j], 16)

            def turn(loading, gathering, front, back, older):
                for b in (0, 1):
                    if front:
                        hold_count(sp, s, s["pos_ready"], front.before().at(b))
                        sp.dma_start(x[:, front.buf(b)], chunk(k.d[3], front.n(b))).then_inc(s["loaded_x"][front.buf(b)], 16)
                for b in (0, 1):
                    if loading:
                        hold(sp, s, s["weighted_ready"], front.at(b))
                        load(loading, b)
            for parity in (0, 1):
                for b in (0, 1):
                    load(Pair(0, parity), b)
            turns(sp, pairs, turn)

        @block.scalar
        def _(act):
            def turn(loading, gathering, front, back, older):
                for b in (0, 1):
                    if front:
                        j = front.buf(b)
                        act.wait_ge(s["shifted_ready"], front.at(b))
                        wait_count(act, s["expm_ready"], front.before().at(b))
                        act.activation(expo[:, j], shifted[:, j], ACT.Exp).then_inc(s["exp_ready"], 1)
                for b in (0, 1):
                    if older:
                        j = older.buf(b)
                        act.wait_ge(s["shift_ready"], older.at(b))
                        wait_count(act, s["scattered"][j], 16 * T * uses_before(older))
                        for t in range(T):
                            last = act.activation(out[:, j, t], t_[:, j, t], ACT.Identity, bias=shift[:, j, t:t + 1], scale=r[:, j, t:t + 1])
                        last.then_inc(s["out_ready"], 1)
                for b in (0, 1):
                    if back:
                        j = back.buf(b)
                        act.wait_ge(s["y_ready"], back.at(b))
                        act.activation(neg[:, j], y[:, j], ACT.Relu, scale=-1.0).then_inc(s["neg_ready"], 1)
                for b in (0, 1):
                    if back:
                        j = back.buf(b)
                        act.wait_ge(s["neg_ready"], back.at(b))
                        act.activation(expm[:, j], neg[:, j], ACT.Exp, scale=-1.0).then_inc(s["expm_ready"], 1)
            turns(act, pairs, turn)

        @block.gpsimd
        def _(pool):
            def scatter(pair, b):
                j = pair.buf(b)
                hold(pool, s, s["out_ready"], pair.at(b))
                pool.tensor_copy(index[:, j], k.out_ix[:, bass.ds(pair.n(b) * T, T)]).then_inc(s["index_ready"], 1)
                hold(pool, s, s["index_ready"], pair.at(b))
                for t in range(T):
                    pool.indirect_dma_start(out=k.out, out_offset=bass.IndirectOffsetOnAxis(ap=index[:, j, t:t + 1], axis=0),
                                            in_=out[:, j, t], in_offset=None,
                                            bounds_check=k.n_nodes - 1, oob_is_err=False).then_inc(s["scattered"][j], 16)

            def turn(loading, gathering, front, back, older):
                for b in (0, 1):
                    if back:
                        j = back.buf(b)
                        hold(pool, s, s["scaled_ready"], back.at(b))
                        pool.tensor_tensor(y[:, j], scaled[:, j], c["b_3"][:], ALU.add).then_inc(s["y_ready"], 1)
                for b in (0, 1):
                    if older:
                        scatter(older, b)
                for b in (0, 1):
                    if back:
                        j = back.buf(b)
                        rstd(pool, s, k, D, mv[:, j], var_eps[:, j], r[:, j], back.n(b))
            turns(pool, pairs, turn)
            for j in range(BUFS):
                pool.wait_ge(s["scattered"][j], 16 * T * ((2 * pairs - 1 - j) // BUFS + 1))

        @block.tensor
        def _(pe):
            def turn(loading, gathering, front, back, older):
                for b in (0, 1):
                    if back:
                        j = back.buf(b)
                        wait_count(pe, s["scaled_ready"], back.before().at(b))
                        pe.wait_ge(s["den_ready"], back.at(b))
                        for t in range(T):
                            pe.matmul(psN[j][:, t * HEADS:(t + 1) * HEADS], tile(den, j, t), c["head_pick"][:],
                                      start=True, stop=True, skip_group_check=True)
                for b in (0, 1):
                    if back:
                        j = back.buf(b)
                        pe.wait_ge(s["num_ready"], back.at(b))
                        for t in range(T):
                            last = pe.transpose(psA[j][:, t * D:(t + 1) * D], tile(num, j, t), c["identity"][:])
                        last.then_inc(s["agg_ready"], 1)
            turns(pe, pairs, turn)

        @block.vector
        def _(dve):
            for buf in (maxheld, num, den):
                dve.memset(buf[:, BUFS - 1, CH - 1:CH], 0.0).then_inc(s["start"], 1)
            dve.wait_ge(s["start"], 3)

            def same(pair, b):
                return k.same[:, bass.ds(pair.n(b) * CH, CH)]

            def scan(buf, j, data, sem, pair, b, op):
                carry_wait(dve, s[sem], pair, b)
                dve.tensor_tensor_scan(buf[:, j], same(pair, b), data[:, j], buf[:, previous(j), CH - 1:CH], ALU.mult, op).then_inc(s[sem], 1)

            def turn(loading, gathering, front, back, older):
                both = (0, 1)
                if front:
                    for b in both:
                        j = front.buf(b)
                        dve.wait_ge(s["loaded"][j], 48 * uses(front))
                        wait_count(dve, s["y_ready"], front.before().at(b))
                        dve.scalar_tensor_tensor(firstmax[:, j], same(front, b), -1.0, top[:, j], ALU.add, ALU.mult).then_inc(s["firstmax_ready"], 1)
                if front:
                    for b in both:
                        dve.wait_ge(s["firstmax_ready"], front.at(b))
                        scan(maxheld, front.buf(b), firstmax, "maxheld_ready", front, b, ALU.subtract)
                if front:
                    for b in both:
                        j = front.buf(b)
                        dve.wait_ge(s["maxheld_ready"], front.at(b))
                        wait_count(dve, s["neg_ready"], front.before().at(b))
                        dve.tensor_tensor(shifted[:, j], score[:, j], maxheld[:, j], ALU.subtract).then_inc(s["shifted_ready"], 1)
                if older:
                    for b in both:
                        shift_rows(dve, s, mv, r, shift, older, b)
                if back:
                    for b in both:
                        j = back.buf(b)
                        dve.wait_ge(s["agg_ready"], back.at(b))
                        dve.tensor_scalar(denb[:, j], psN[j][:], 1e-7, None, ALU.add).then_inc(s["denb_ready"], 1)
                    for b in both:
                        j = back.buf(b)
                        dve.wait_ge(s["denb_ready"], back.at(b))
                        dve.reciprocal(rden[:, j], denb[:, j]).then_inc(s["rden_ready"], 1)
                    for b in both:
                        j = back.buf(b)
                        dve.wait_ge(s["rden_ready"], back.at(b))
                        dve.tensor_tensor(scaled[:, j].rearrange("p (g u) -> p g u", u=UNITS), psA[j][:].rearrange("p (g u) -> p g u", u=UNITS),
                                          rden[:, j].unsqueeze(2).to_broadcast([D, T * HEADS, UNITS]), ALU.mult).then_inc(s["scaled_ready"], 1)
                if front:
                    for b in both:
                        j = front.buf(b)
                        dve.wait_ge(s["exp_ready"], front.at(b))
                        dve.tensor_tensor(weighted[:, j], expo[:, j], valT[:, j], ALU.mult).then_inc(s["weighted_ready"], 1)
                if front:
                    for b in both:
                        dve.wait_ge(s["exp_ready"], front.at(b))
                        scan(den, front.buf(b), expo, "den_ready", front, b, ALU.add)
                    for b in both:
                        dve.wait_ge(s["weighted_ready"], front.at(b))
                        scan(num, front.buf(b), weighted, "num_ready", front, b, ALU.add)
                if back:
                    for b in both:
                        j = back.buf(b)
                        dve.wait_ge(s["y_ready"], back.at(b))
                        dve.wait_ge(s["loaded_x"][j], 16 * uses(back))
                        wait_count(dve, s["out_ready"], back.before().at(b))
                        dve.scalar_tensor_tensor(flat(t_, j), y[:, j], 0.0, flat(x, j), ALU.max, ALU.add).then_inc(s["pos_ready"], 1)
                if back:
                    for b in both:
                        j = back.buf(b)
                        dve.wait_ge(s["pos_ready"], back.at(b))
                        dve.wait_ge(s["expm_ready"], back.at(b))
                        dve.scalar_tensor_tensor(flat(t_, j), expm[:, j], -1.0, flat(t_, j), ALU.add, ALU.add).then_inc(s["t_ready"], 1)
                    for b in both:
                        j = back.buf(b)
                        dve.wait_ge(s["t_ready"], back.at(b))
                        moments(dve, s, t_[:, j], stats[:, j], mv[:, j], back.n(b))
            turns(dve, pairs, turn)


def launch_arrays(inputs, n_nodes, n_edges):
    g = {n: np.ascontiguousarray(v) for n, v in inputs.items()}
    slots = padded_slots(n_edges)

    def pad(a, value):
        return np.concatenate([a, np.full(slots - n_edges, value, a.dtype)])

    def cols(a):
        return np.ascontiguousarray(a.reshape(-1, D).T)

    def rows(a):
        return np.ascontiguousarray(np.tile(a[None, :], (D, T)))

    def col(a):
        return np.ascontiguousarray(a.reshape(D, 1))
    dst_ext = np.concatenate([np.full(1, -1, np.int32), pad(g["dst"], NO_NODE), np.full(1, NO_NODE + 1, np.int32)])
    a = {
        "x": g["x"],
        "src_cols": cols(pad(g["src"], 0)), "src_hist": cols(pad(g["src"], NO_NODE)),
        "dst_gather": cols(pad(g["dst"], 0)), "dst_cols": cols(pad(g["dst"], NO_NODE)),
        "dst_next": cols(dst_ext[2:]), "dst_ext": dst_ext, "weight_cols": cols(pad(g["edge_weight"], 0)),
        "Wp_t": np.ascontiguousarray(g["L0_gnn_Wp"].T), "kernel_t": np.ascontiguousarray(g["L3_gnn_kernel"].T),
        "L1_Wa": np.ascontiguousarray(g["L1_gnn_W_edge"][:D]), "L1_Wb": np.ascontiguousarray(g["L1_gnn_W_edge"][D:]),
        "b_p": rows(g["L0_gnn_bp"]), "b_2": rows(g["L1_gnn_b2"]), "b_conv1": rows(g["L2_gnn_b1"]),
        "b_conv2": rows(g["L2_gnn_b2"]), "b_3": rows(g["L3_gnn_bias"]),
        "b_edge": col(g["L1_gnn_b_edge"]), "b_2_col": col(g["L1_gnn_b2"]), "b_1": col(g["L1_gnn_b1"]),
        "ka1": col(g["L3_gnn_ka1"]), "ka2": col(g["L3_gnn_ka2"]),
        "eps": np.ascontiguousarray(np.broadcast_to(g["L1_gnn_eps"].reshape(1, 1), (D, 1))),
    }
    for n in ("L0_gnn_Wq", "L0_gnn_Wk", "L0_gnn_Wv", "L1_gnn_W1", "L1_gnn_W2", "L2_gnn_W1", "L2_gnn_W2", "L3_gnn_kernel"):
        a[n] = g[n]
    head = np.arange(D) // UNITS
    a["identity"] = np.eye(D, dtype=np.float32)
    a["head_block"] = (head[:, None] == head[None, :]).astype(np.float32)
    a["head_pick"] = (np.arange(D)[:, None] == UNITS * np.arange(HEADS)[None, :]).astype(np.float32)
    a["score_block"] = np.full((D, D), D ** -0.5, np.float32)
    a["first_row"] = (np.arange(D) == 0).astype(np.float32)[:, None]
    a["ones"] = np.ones((D, D), np.float32)
    a["strict_upper"] = np.triu(np.ones((D, D), np.float32), 1)
    return a


def build(nc, arrays, n_nodes, n_edges):
    args = {n: nc.dram_tensor(f"in_{n}", v.shape, mybir.dt.from_np(v.dtype), kind="ExternalInput").ap() for n, v in arrays.items()}
    out = nc.dram_tensor("out", (n_nodes, D), F32, kind="ExternalOutput").ap()
    gnn_kernel(nc, n_nodes, n_edges, args, out)


def kernel(**inputs):
    import concourse.bacc as bacc
    from concourse.bass_utils import run_bass_kernel_spmd

    n_nodes, n_edges = inputs["x"].shape[0], inputs["src"].shape[0]
    nc = bacc.Bacc("TRN2", target_bir_lowering=False, num_devices=1)
    arrays = launch_arrays({n: np.asarray(v) for n, v in inputs.items()}, n_nodes, n_edges)
    build(nc, arrays, n_nodes, n_edges)
    r = run_bass_kernel_spmd(nc, [{f"in_{n}": v for n, v in arrays.items()}], core_ids=[0])
    return r.results[0]["out"]
```
